# Optimizing a Trainium2 kernel written in Bass

```python
import numpy as np
import jax
import jax.numpy as jnp

def _softmax(x, axis=-1):
    return jax.nn.softmax(x, axis=axis)

def _gelu(x):
    return jax.nn.gelu(x, approximate=True)

def _silu(x):
    return jax.nn.silu(x)

def _sigmoid(x):
    return jax.nn.sigmoid(x)

def _layernorm(x, axis=-1, eps=1e-05):
    m = jnp.mean(x, axis=axis, keepdims=True)
    v = jnp.var(x, axis=axis, keepdims=True)
    return (x - m) / jnp.sqrt(v + eps)

def _scatter_add(tgt, idx, src, axis=0):
    return tgt.at[idx].add(src)

def _segment_sum(src, seg, n):
    return jax.ops.segment_sum(src, seg, n)
kernel_name = 'mk_seq_postln_d2_jaxref_r8_50f977'

def setup_inputs(seed: int=0):
    np.random.seed(seed)
    _w = jnp.asarray

    def _L0_attn_setup():
        import jax, jax.numpy as jnp
        import numpy as np
        NHEAD = 8
        ATTN_EPS = 1e-06
        LN_EPS = 1e-05

        def _layernorm(y, g, b):
            mu = jnp.mean(y, axis=-1, keepdims=True)
            var = jnp.var(y, axis=-1, keepdims=True)
            return (y - mu) * jax.lax.rsqrt(var + LN_EPS) * g + b
        key = jax.random.key(seed)
        ks = jax.random.split(key, 6)
        B, L, D = (2, 1024, 128)
        s = 1.0 / np.sqrt(D)
        return {'x': jax.random.normal(ks[0], (B, L, D), jnp.float32), 'Wq': jax.random.normal(ks[1], (D, D), jnp.float32) * s, 'Wm': jax.random.normal(ks[2], (D, D), jnp.float32) * s, 'W1': jax.random.normal(ks[3], (D, 2 * D), jnp.float32) * s, 'W2': jax.random.normal(ks[4], (2 * D, D), jnp.float32) * (1.0 / np.sqrt(2 * D)), 'g1': jnp.ones((D,), jnp.float32), 'b1': jnp.zeros((D,), jnp.float32), 'g2': jnp.ones((D,), jnp.float32), 'b2': jnp.zeros((D,), jnp.float32)}
    _L0_attn_in = _L0_attn_setup()

    def _L0_ffn_setup():
        import jax, jax.numpy as jnp
        import numpy as np
        B, S, D = (1, 256, 128)
        E, K, F = (64, 8, 96)
        SF = 96
        C = 64
        ROUTED_SCALE = 1.0

        def _moe_forward(x, router_w, w_gate, w_up, w_down, ws_gate_up, ws_down):
            T = x.shape[0]
            logits = x.astype(jnp.float32) @ router_w.T
            probs = jax.nn.softmax(logits, axis=-1)
            topk_w, topk_ids = jax.lax.top_k(probs, K)
            topk_w = topk_w / jnp.sum(topk_w, axis=-1, keepdims=True)
            topk_w = topk_w.astype(x.dtype)
            N = T * K
            flat_e = topk_ids.reshape(-1)
            flat_w = topk_w.reshape(-1)
            tok = jnp.arange(N) // K
            onehot = flat_e[:, None] == jnp.arange(E)[None, :]
            pos = jnp.cumsum(onehot, axis=0)[jnp.arange(N), flat_e] - 1
            valid = pos < C
            idx = jnp.where(valid, flat_e * C + pos, E * C)
            x_buf = jnp.zeros((E * C + 1, x.shape[1]), x.dtype).at[idx].set(x[tok])
            xb = x_buf[:E * C].reshape(E, C, -1)
            g = jnp.einsum('ecd,edf->ecf', xb, w_gate)
            u = jnp.einsum('ecd,edf->ecf', xb, w_up)
            h = jax.nn.silu(g) * u
            y = jnp.einsum('ecf,efd->ecd', h, w_down).reshape(E * C, -1)
            safe = jnp.where(valid, idx, 0)
            contrib = y[safe] * (flat_w * valid.astype(flat_w.dtype))[:, None]
            routed = jax.ops.segment_sum(contrib, tok, num_segments=T)
            routed = routed * ROUTED_SCALE
            gu = x @ ws_gate_up
            sg, su = (gu[:, :SF], gu[:, SF:])
            shared = jax.nn.silu(sg) * su @ ws_down
            return routed + shared
        key = jax.random.key(seed)
        ks = jax.random.split(key, 7)
        w = 0.02
        return {'hidden_states': jax.random.normal(ks[0], (B, S, D), jnp.float32), 'router_w': jax.random.normal(ks[1], (E, D), jnp.float32) * w, 'w_gate': jax.random.normal(ks[2], (E, D, F), jnp.float32) * w, 'w_up': jax.random.normal(ks[3], (E, D, F), jnp.float32) * w, 'w_down': jax.random.normal(ks[4], (E, F, D), jnp.float32) * w, 'ws_gate_up': jax.random.normal(ks[5], (D, 2 * SF), jnp.float32) * w, 'ws_down': jax.random.normal(ks[6], (SF, D), jnp.float32) * w}
    _L0_ffn_in = _L0_ffn_setup()

    def _L1_attn_setup():
        import jax, jax.numpy as jnp
        import numpy as np
        DIM = 128
        G = 32
        QK = 128
        HID = 256
        NUM_BUCKETS = 32
        MAX_DIST = 128
        BIAS_SCALE = QK ** 0.5
        LN_EPS = 1e-05

        def t5_rel_bias(rel_table):
            pos = jnp.arange(G)
            rel = pos[None, :] - pos[:, None]
            n = jnp.maximum(-rel, 0)
            max_exact = NUM_BUCKETS // 2
            is_small = n < max_exact
            ln_ratio = np.log(MAX_DIST / max_exact)
            val_large = max_exact + (jnp.log(jnp.maximum(n, 1).astype(jnp.float32) / max_exact) / ln_ratio * (NUM_BUCKETS - max_exact)).astype(jnp.int32)
            val_large = jnp.minimum(val_large, NUM_BUCKETS - 1)
            bucket = jnp.where(is_small, n, val_large)
            return rel_table[bucket] * BIAS_SCALE
        key = jax.random.key(seed)
        ks = jax.random.split(key, 10)
        s = 0.02
        return {'x': jax.random.normal(ks[0], (4, 512, DIM), dtype=jnp.float32), 'ln_w': jnp.ones((DIM,), jnp.float32), 'ln_b': jnp.zeros((DIM,), jnp.float32), 'Wh': jax.random.normal(ks[1], (DIM, 2 * HID), jnp.float32) * s, 'bh': jnp.zeros((2 * HID,), jnp.float32), 'Wqk': jax.random.normal(ks[2], (DIM, QK), jnp.float32) * s, 'bqk': jnp.zeros((QK,), jnp.float32), 'qk_w': jax.random.normal(ks[3], (4, QK), jnp.float32) * s + 1.0, 'qk_b': jnp.zeros((4, QK), jnp.float32), 'rel_table': jax.random.normal(ks[4], (NUM_BUCKETS,), jnp.float32) * s, 'Wout': jax.random.normal(ks[5], (HID, DIM), jnp.float32) * s, 'bout': jnp.zeros((DIM,), jnp.float32)}
    _L1_attn_in = _L1_attn_setup()

    def _L1_ffn_setup():
        import jax, jax.numpy as jnp
        import numpy as np
        TOP_K = 2
        EPS = 1e-09
        key = jax.random.key(seed)
        ks = jax.random.split(key, 6)
        B, T, D, H, E = (4, 256, 128, 256, 8)
        x = jax.random.normal(ks[0], (B, T, D), dtype=jnp.float32)
        Wg = jax.random.normal(ks[1], (E, D), dtype=jnp.float32) * 0.02
        W1 = jax.random.normal(ks[2], (E, 2 * H, D), dtype=jnp.float32) * 0.02
        b1 = jax.random.normal(ks[3], (E, 2 * H), dtype=jnp.float32) * 0.02
        Wo = jax.random.normal(ks[4], (D, H), dtype=jnp.float32) * 0.02
        bo = jax.random.normal(ks[5], (D,), dtype=jnp.float32) * 0.02
        return {'x': x, 'Wg': Wg, 'W1': W1, 'b1': b1, 'Wo': Wo, 'bo': bo}
    _L1_ffn_in = _L1_ffn_setup()
    _d = {'L0_attn_x': _L0_attn_in['x'], 'L0_attn_Wq': _L0_attn_in['Wq'], 'L0_attn_Wm': _L0_attn_in['Wm'], 'L0_attn_W1': _L0_attn_in['W1'], 'L0_attn_W2': _L0_attn_in['W2'], 'L0_attn_g1': _L0_attn_in['g1'], 'L0_attn_b1': _L0_attn_in['b1'], 'L0_attn_g2': _L0_attn_in['g2'], 'L0_attn_b2': _L0_attn_in['b2'], 'L0_ffn_router_w': _L0_ffn_in['router_w'], 'L0_ffn_w_gate': _L0_ffn_in['w_gate'], 'L0_ffn_w_up': _L0_ffn_in['w_up'], 'L0_ffn_w_down': _L0_ffn_in['w_down'], 'L0_ffn_ws_gate_up': _L0_ffn_in['ws_gate_up'], 'L0_ffn_ws_down': _L0_ffn_in['ws_down'], 'L1_attn_ln_w': _L1_attn_in['ln_w'], 'L1_attn_ln_b': _L1_attn_in['ln_b'], 'L1_attn_Wh': _L1_attn_in['Wh'], 'L1_attn_bh': _L1_attn_in['bh'], 'L1_attn_Wqk': _L1_attn_in['Wqk'], 'L1_attn_bqk': _L1_attn_in['bqk'], 'L1_attn_qk_w': _L1_attn_in['qk_w'], 'L1_attn_qk_b': _L1_attn_in['qk_b'], 'L1_attn_rel_table': _L1_attn_in['rel_table'], 'L1_attn_Wout': _L1_attn_in['Wout'], 'L1_attn_bout': _L1_attn_in['bout'], 'L1_ffn_Wg': _L1_ffn_in['Wg'], 'L1_ffn_W1': _L1_ffn_in['W1'], 'L1_ffn_b1': _L1_ffn_in['b1'], 'L1_ffn_Wo': _L1_ffn_in['Wo'], 'L1_ffn_bo': _L1_ffn_in['bo']}
    _x0 = _d['L0_attn_x']
    _d['L0_attn_x'] = jax.random.normal(jax.random.fold_in(jax.random.key(seed), 1), (8, 512, 128), dtype=_x0.dtype)
    del _x0
    return _d

def reference(L0_attn_x, L0_attn_Wq, L0_attn_Wm, L0_attn_W1, L0_attn_W2, L0_attn_g1, L0_attn_b1, L0_attn_g2, L0_attn_b2, L0_ffn_router_w, L0_ffn_w_gate, L0_ffn_w_up, L0_ffn_w_down, L0_ffn_ws_gate_up, L0_ffn_ws_down, L1_attn_ln_w, L1_attn_ln_b, L1_attn_Wh, L1_attn_bh, L1_attn_Wqk, L1_attn_bqk, L1_attn_qk_w, L1_attn_qk_b, L1_attn_rel_table, L1_attn_Wout, L1_attn_bout, L1_ffn_Wg, L1_ffn_W1, L1_ffn_b1, L1_ffn_Wo, L1_ffn_bo):

    def _L0_attn_ref(x, Wq, Wm, W1, W2, g1, b1, g2, b2):
        import jax, jax.numpy as jnp
        import numpy as np
        NHEAD = 8
        ATTN_EPS = 1e-06
        LN_EPS = 1e-05

        def _layernorm(y, g, b):
            mu = jnp.mean(y, axis=-1, keepdims=True)
            var = jnp.var(y, axis=-1, keepdims=True)
            return (y - mu) * jax.lax.rsqrt(var + LN_EPS) * g + b
        B, L, D = x.shape
        H = NHEAD
        d = D // H
        q = (x @ Wq).reshape(B, L, H, d)
        feat = jax.nn.elu(q) + 1.0
        Q = feat
        K = feat
        V = q / L
        KV = jnp.einsum('nshd,nshv->nhdv', K, V)
        Ksum = K.sum(axis=1)
        Z = 1.0 / (jnp.einsum('nlhd,nhd->nlh', Q, Ksum) + ATTN_EPS)
        msg = jnp.einsum('nlhd,nhdv,nlh->nlhv', Q, KV, Z) * L
        msg = msg.reshape(B, L, D) @ Wm
        x = x + _layernorm(msg, g1, b1)
        mlp = jax.nn.relu(msg @ W1) @ W2
        x = x + _layernorm(mlp, g2, b2)
        return x

    def _L0_ffn_ref(hidden_states, router_w, w_gate, w_up, w_down, ws_gate_up, ws_down):
        import jax, jax.numpy as jnp
        import numpy as np
        B, S, D = (1, 256, 128)
        E, K, F = (64, 8, 96)
        SF = 96
        C = 64
        ROUTED_SCALE = 1.0

        def _moe_forward(x, router_w, w_gate, w_up, w_down, ws_gate_up, ws_down):
            T = x.shape[0]
            logits = x.astype(jnp.float32) @ router_w.T
            probs = jax.nn.softmax(logits, axis=-1)
            topk_w, topk_ids = jax.lax.top_k(probs, K)
            topk_w = topk_w / jnp.sum(topk_w, axis=-1, keepdims=True)
            topk_w = topk_w.astype(x.dtype)
            N = T * K
            flat_e = topk_ids.reshape(-1)
            flat_w = topk_w.reshape(-1)
            tok = jnp.arange(N) // K
            onehot = flat_e[:, None] == jnp.arange(E)[None, :]
            pos = jnp.cumsum(onehot, axis=0)[jnp.arange(N), flat_e] - 1
            valid = pos < C
            idx = jnp.where(valid, flat_e * C + pos, E * C)
            x_buf = jnp.zeros((E * C + 1, x.shape[1]), x.dtype).at[idx].set(x[tok])
            xb = x_buf[:E * C].reshape(E, C, -1)
            g = jnp.einsum('ecd,edf->ecf', xb, w_gate)
            u = jnp.einsum('ecd,edf->ecf', xb, w_up)
            h = jax.nn.silu(g) * u
            y = jnp.einsum('ecf,efd->ecd', h, w_down).reshape(E * C, -1)
            safe = jnp.where(valid, idx, 0)
            contrib = y[safe] * (flat_w * valid.astype(flat_w.dtype))[:, None]
            routed = jax.ops.segment_sum(contrib, tok, num_segments=T)
            routed = routed * ROUTED_SCALE
            gu = x @ ws_gate_up
            sg, su = (gu[:, :SF], gu[:, SF:])
            shared = jax.nn.silu(sg) * su @ ws_down
            return routed + shared
        b, s, d = hidden_states.shape
        x = hidden_states.reshape(-1, d)
        out = _moe_forward(x, router_w, w_gate, w_up, w_down, ws_gate_up, ws_down)
        return out.reshape(b, s, d)

    def _L1_attn_ref(x, ln_w, ln_b, Wh, bh, Wqk, bqk, qk_w, qk_b, rel_table, Wout, bout):
        import jax, jax.numpy as jnp
        import numpy as np
        DIM = 128
        G = 32
        QK = 128
        HID = 256
        NUM_BUCKETS = 32
        MAX_DIST = 128
        BIAS_SCALE = QK ** 0.5
        LN_EPS = 1e-05

        def t5_rel_bias(rel_table):
            pos = jnp.arange(G)
            rel = pos[None, :] - pos[:, None]
            n = jnp.maximum(-rel, 0)
            max_exact = NUM_BUCKETS // 2
            is_small = n < max_exact
            ln_ratio = np.log(MAX_DIST / max_exact)
            val_large = max_exact + (jnp.log(jnp.maximum(n, 1).astype(jnp.float32) / max_exact) / ln_ratio * (NUM_BUCKETS - max_exact)).astype(jnp.int32)
            val_large = jnp.minimum(val_large, NUM_BUCKETS - 1)
            bucket = jnp.where(is_small, n, val_large)
            return rel_table[bucket] * BIAS_SCALE
        b, n, _ = x.shape
        g = G
        ng = n // g
        mu = jnp.mean(x, -1, keepdims=True)
        var = jnp.var(x, -1, keepdims=True)
        normed = (x - mu) * jax.lax.rsqrt(var + LN_EPS) * ln_w + ln_b
        hv = jax.nn.silu(normed @ Wh + bh)
        v, gate = jnp.split(hv, 2, axis=-1)
        qk = jax.nn.silu(normed @ Wqk + bqk)
        qk4 = qk[..., None, :] * qk_w + qk_b
        quad_q, lin_q, quad_k, lin_k = [qk4[..., h, :] for h in range(4)]
        grp = lambda t: t.reshape(b, ng, g, t.shape[-1])
        quad_q, quad_k, lin_q, lin_k, vg = map(grp, (quad_q, quad_k, lin_q, lin_k, v))
        sim = jnp.einsum('bgid,bgjd->bgij', quad_q, quad_k) / g
        sim = sim + t5_rel_bias(rel_table)
        attn = jnp.square(jax.nn.relu(sim))
        causal_mask = jnp.triu(jnp.ones((g, g), bool), 1)
        attn = jnp.where(causal_mask, 0.0, attn)
        quad_out = jnp.einsum('bgij,bgje->bgie', attn, vg)
        lin_kv = jnp.einsum('bgnd,bgne->bgde', lin_k, vg) / g
        lin_kv = jnp.cumsum(lin_kv, axis=1)
        lin_kv = jnp.pad(lin_kv, ((0, 0), (1, 0), (0, 0), (0, 0)))[:, :-1]
        lin_out = jnp.einsum('bgde,bgnd->bgne', lin_kv, lin_q)
        out = gate * (quad_out + lin_out).reshape(b, n, HID)
        return out @ Wout + bout + x

    def _L1_ffn_ref(x, Wg, W1, b1, Wo, bo):
        import jax, jax.numpy as jnp
        import numpy as np
        TOP_K = 2
        EPS = 1e-09
        E = Wg.shape[0]
        gate_logits = jnp.einsum('btd,ed->bte', x, Wg)
        gate_scores = jax.nn.softmax(gate_logits, axis=-1)
        topk_val, topk_idx = jax.lax.top_k(gate_scores, TOP_K)
        topk_val = topk_val / (topk_val.sum(axis=-1, keepdims=True) + EPS)
        comb = (jax.nn.one_hot(topk_idx, E, dtype=x.dtype) * topk_val[..., None]).sum(axis=-2)
        out = jnp.zeros_like(x)
        for e in range(E):
            h = jnp.einsum('btd,hd->bth', x, W1[e]) + b1[e]
            a, b = jnp.split(h, 2, axis=-1)
            g = a * jax.nn.sigmoid(b)
            eo = jnp.einsum('bth,dh->btd', g, Wo) + bo
            out = out + eo * comb[..., e:e + 1]
        return out
    x = L0_attn_x
    x = _layernorm(x + _L0_attn_ref(x, L0_attn_Wq, L0_attn_Wm, L0_attn_W1, L0_attn_W2, L0_attn_g1, L0_attn_b1, L0_attn_g2, L0_attn_b2), axis=-1)
    x = _layernorm(x + _L0_ffn_ref(x, L0_ffn_router_w, L0_ffn_w_gate, L0_ffn_w_up, L0_ffn_w_down, L0_ffn_ws_gate_up, L0_ffn_ws_down), axis=-1)
    x = _layernorm(x + _L1_attn_ref(x, L1_attn_ln_w, L1_attn_ln_b, L1_attn_Wh, L1_attn_bh, L1_attn_Wqk, L1_attn_bqk, L1_attn_qk_w, L1_attn_qk_b, L1_attn_rel_table, L1_attn_Wout, L1_attn_bout), axis=-1)
    x = _layernorm(x + _L1_ffn_ref(x, L1_ffn_Wg, L1_ffn_W1, L1_ffn_b1, L1_ffn_Wo, L1_ffn_bo), axis=-1)
    return x

_drawn_inputs = setup_inputs


def setup_inputs(seed=0):
    import zlib

    import numpy as np

    out = dict(_drawn_inputs(seed))
    spreads = {'L0_attn_g1': (1.0, 0.2),
     'L0_attn_b1': (0.0, 0.1),
     'L0_attn_g2': (1.0, 0.2),
     'L0_attn_b2': (0.0, 0.1),
     'L1_attn_ln_w': (1.0, 0.6),
     'L1_attn_ln_b': (0.0, 0.8),
     'L1_attn_bh': (0.0, 0.8),
     'L1_attn_bqk': (0.0, 0.8),
     'L1_attn_qk_b': (0.0, 2.0),
     'L1_attn_bout': (0.0, 0.8)}
    factors = {'L0_ffn_router_w': 8.0,
     'L0_ffn_w_gate': 8.0,
     'L0_ffn_w_up': 8.0,
     'L0_ffn_w_down': 8.0,
     'L0_ffn_ws_gate_up': 8.0,
     'L0_ffn_ws_down': 8.0,
     'L1_attn_Wh': 4.489,
     'L1_attn_Wqk': 8.0,
     'L1_attn_qk_w': 64.0,
     'L1_attn_rel_table': 64.0,
     'L1_attn_Wout': 4.43,
     'L1_ffn_b1': 23.864}
    for name, (base, spread) in spreads.items():
        noise = np.random.default_rng([zlib.crc32(name.encode()), seed]).standard_normal(out[name].shape)
        drawn = base * np.exp(spread * noise) if base else spread * noise
        out[name] = jnp.asarray(drawn.astype(out[name].dtype))
    for name, factor in factors.items():
        out[name] = (out[name] * factor).astype(out[name].dtype)
    return out
```

```python
import numpy as np
import concourse.bass as bass
from concourse import mybir
from contextlib import ExitStack

F32 = mybir.dt.float32
F32R = mybir.dt.float32r
I32 = mybir.dt.int32
U32 = mybir.dt.uint32
ALU = mybir.AluOpType
ACT = mybir.ActivationFunctionType
AX = mybir.AxisListType

P = 128
B, L, D = 8, 512, 128
T = B * L
NT = L // P
PAIRS = B // 2
EPS = 1e-5
H0, DH = 8, 16
ATTN_EPS = 1e-6
E0, K0N, F0, CAP = 64, 8, 96, 64
EP = E0 // 2
EP_EARLY = 12
ROW = D + E0
NKEY = T * K0N
NEG = -3.0e38
G, HID, QK = 32, 256, 128
BIAS_SCALE = float(QK) ** 0.5
NBUCKET, MAXDIST = 32, 128
E1, H1 = 8, 256
MASKED = -1e30
NROWS = 5 + 4 + 4 + E1 + 4 * E1
GATE_STEPS = 18


def bcast_last(ap, n):
    shape = list(ap.shape) + [n]
    return ap.unsqueeze(len(shape) - 1).broadcast_to(shape)


def bcast_mid(ap, n):
    return ap.unsqueeze(1).broadcast_to([ap.shape[0], n, ap.shape[1]])


def bucket_runs():
    exact = NBUCKET // 2
    runs = []
    for n in range(G):
        if n < exact:
            b = n
        else:
            b = exact + int(np.float32(np.log(np.float32(n) / np.float32(exact))) / np.float32(np.log(MAXDIST / exact))
                            * np.float32(NBUCKET - exact))
            b = min(b, NBUCKET - 1)
        if runs and runs[-1][2] == b:
            runs[-1] = (runs[-1][0], runs[-1][1] + 1, b)
        else:
            runs.append((n, 1, b))
    return runs


class StageC:

    def __init__(self, nc, sb, sem, region):
        self.nc = nc
        keep = {}
        def k(name, shape, dt=F32):
            keep[name] = sb("c_" + name, shape, dt)
        k("rows", [NROWS, D]); k("cols", [P, NROWS]); k("whqk", [P, 2 * HID + QK])
        k("wh_hi", [P, 2 * HID + QK], F32R); k("wh_lo", [P, 2 * HID + QK], F32R)
        k("vb", [1, HID]); k("vb_hi", [1, HID], F32R); k("vb_lo", [1, HID], F32R); k("bh_row", [1, HID]); k("one11", [1, 1])
        k("ones_f", [1, P]); k("ones", [1, P], F32R); k("bcols", [P, 3]); k("quadw", [P, 2]); k("quadb", [P, 2])
        k("biasT", [P, P]); k("ltmask", [P, P]); k("rel", [1, 64]); k("ext", [1, 64])
        k("wout", [P, 2, D]); k("wo", [P, H1]); k("woT", [P, 2, D])
        k("bout", [1, NT, D]); k("bout_hi", [1, NT * D], F32R); k("bout_lo", [1, NT * D], F32R)
        k("bo16", [16, D]); k("bo_hi", [16, D], F32R); k("bo_lo", [16, D], F32R)
        k("wg_hi", [P, E1], F32R); k("wg_lo", [P, E1], F32R)
        k("sel_f", [16, E1, P]); k("sel", [16, E1, P], F32R); k("iota8", [P, E1])
        k("mhalf", [P, NT]); k("eps", [P, NT])
        self.k = keep
        self.region = region
        self.sem = sem
        self.setup_loaded = sem("c_setup_loaded")
        self.setup_skew = sem("c_setup_skew")
        self.setup_pool = sem("c_setup_pool")
        self.act_setup = sem("c_setup_act")
        self.setup_cols = sem("c_setup_cols")
        self.n_loads = 19

    def buffers(self, sb):
        b = {}
        def k(name, shape, dt=F32):
            b[name] = sb("c_" + name, shape, dt)
        k("c", [P, NT, K0N * D]); k("y", [P, NT * D])
        k("w1_hi", [P, E1, 2 * H1], F32R); k("w1_lo", [P, E1, 2 * H1], F32R)
        for u in range(2):
            k(f"x2{u}", [P, NT * D]); k(f"z{u}", [P, NT * D]); k(f"x3{u}", [P, NT * D])
            k(f"x3h{u}", [P, L], F32R); k(f"x3l{u}", [P, L], F32R); k(f"combT{u}", [16, L], F32R)
            k(f"outb{u}", [P, NT * D]); k(f"sgt{u}", [P, L]); k(f"sg{u}", [P, L]); k(f"g{u}", [P, 2, L])
        k("zh", [P, L], F32R); k("zl", [P, L], F32R); k("v", [P, NT, HID]); k("gateT", [P, 2, L]); k("qkT", [P, L])
        for n in ("qq", "lq", "qk", "lk"):
            k(n, [P, L])
        k("t", [P, NT, P]); k("ml", [P, NT, P]); k("off1", [P, 512]); k("off2", [P, 256]); k("goT", [P, 2, L])
        k("y3", [P, NT * D]); k("acc", [P, 2, L]); k("y4", [P, NT * D])
        for n in ("r", "a", "f"):
            k(f"st_{n}", [P, 6 * NT]); k(f"mv_{n}", [P, 2 * NT]); k(f"rs_{n}", [P, NT])
        k("rq", [P, NT]); k("rz", [P, NT])
        for n in ("lgs", "top", "dif", "s1", "s2", "m0", "m1"):
            k(n, [P, NT * E1])
        k("idx", [P, NT * 8], U32); k("idxf", [P, NT * 8]); k("zsum", [P, NT]); k("p01", [P, NT, 2]); k("den", [P, NT])
        k("ch", [P, NT * 16]); k("chr", [P, NT * E1], F32R)
        self.b = b
        self.contrib_loaded, self.out_stored = self.sem("contrib_loaded"), [self.sem(f"out_stored{u}") for u in range(2)]
        self.w1_loaded = [self.sem(f"w1_loaded{q}") for q in range(2)]
        self.s = {n: self.sem("c_" + n) for n in """w1_mm w1_hi w1_lo sum_step y st_r mv_r rz_step r12 z zT_mm zh zl
            v_mm gate_mm qk_mm sig5 prod5 quads diag_mm t1 t2 atd off_mm off2 av_mm go w_mm y3 st_a mv_a rs_step rf_step rs_a x3
            x3T_mm x3h x3l lg_mm gate_step sig_d combT_mm combT cb_mm b_mm a_mm sig g gc acc out_mm y4 st_f mv_f rs_f outb""".split()}

    def setup_sync(self, sp):
        k, i = self.k, self.inputs
        r = k["rows"]
        loads = [(r[0:1, :], i["ln_w"].unsqueeze(0)), (r[1:2, :], i["ln_b"].unsqueeze(0)),
                 (r[2:4, :], i["bh"][HID:2 * HID].rearrange("(h p) -> h p", p=P)), (r[4:5, :], i["bqk"].unsqueeze(0)),
                 (r[5:9, :], i["qk_w"]), (r[9:13, :], i["qk_b"]), (r[13:21, :], i["Wg"]),
                 (r[21:53, :], i["b1e"].rearrange("e (c p) -> (e c) p", p=P)), 
                 (k["whqk"][:, 0:2 * HID], i["Wh"]), (k["whqk"][:, 2 * HID:], i["Wqk"]),
                 (k["bh_row"][:, :], i["bh"][0:HID].unsqueeze(0)), (k["rel"][:, 0:NBUCKET], i["rel_table"].unsqueeze(0)),
                 (k["wout"][:, :, :], i["Wout"].rearrange("(h p) d -> p h d", p=P)), (k["wo"][:, :], i["Wo"]),
                 (k["bo16"][:, :], i["bo"].partition_broadcast(16))]
        loads += [(k["bout"][:, j, :], i["bout"].unsqueeze(0)) for j in range(NT)]
        assert len(loads) == self.n_loads
        for dst, src in loads:
            sp.dma_start(dst, src).then_inc(self.setup_loaded, 16)

    def setup_sync_skew(self, sp):
        k, G2 = self.k, 2 * G - 1
        sp.wait_ge(self.setup_pool, self.pool_ext)
        for j in range(G):
            sp.dma_start(self.skew[j:j + 1, :], k["ext"][0:1, 0:G2]).then_inc(self.setup_skew, 16)
        sp.wait_ge(self.setup_skew, 16 * G)
        src = bass.AP(tensor=self.skew.tensor, offset=G - 1, ap=[[G2 - 1, G], [1, G]])
        for q in range(P // G):
            sp.dma_start(k["biasT"][q * G:(q + 1) * G, q * G:(q + 1) * G], src).then_inc(self.setup_skew, 16)

    def setup_pool_early(self, pool):
        g, k = self.nc.gpsimd, self.k
        c = [0]

        def chain(ins):
            c[0] += 1
            ins.then_inc(self.setup_pool, 1)
            pool.wait_ge(self.setup_pool, c[0])
        pool.wait_ge(self.setup_loaded, 16 * self.n_loads)
        chain(g.memset(k["ext"][:, :], 0.0))
        for n0, cnt, b in bucket_runs():
            for n in range(n0, n0 + cnt):
                ins = g.tensor_scalar(k["ext"][:, G - 1 + n:G + n], k["rel"][:, b:b + 1], BIAS_SCALE, None, ALU.mult)
        chain(ins)
        self.pool_ext = c[0]
        chain(g.memset(k["biasT"][:, :], MASKED))
        self.pool_masked = c[0]
        chain(g.memset(k["ltmask"][:, :], 0.0))
        for q in range(P // G - 1):
            chain(g.memset(k["ltmask"][q * G:(q + 1) * G, (q + 1) * G:P], 1.0))
        g.memset(k["one11"][:, :], 1.0)
        g.memset(k["mhalf"][:, :], -0.5)
        g.memset(k["eps"][:, :], EPS)
        chain(g.memset(k["ones_f"][:, :], 1.0))
        g.tensor_copy(k["ones"][:, :], k["ones_f"][:, :])
        g.iota(k["iota8"][:, :], pattern=[[1, E1]], base=0, channel_multiplier=0, allow_small_or_imprecise_dtypes=True)
        chain(g.memset(k["sel_f"][:, :, :], 0.0))
        for o in (0, E1):
            chain(g.affine_select(out=k["sel_f"][:, :, :], in_=k["sel_f"][:, :, :], compare_op=ALU.not_equal, fill=1.0, base=-o,
                                  pattern=[[-1, E1], [0, P]], channel_multiplier=1))
        chain(g.tensor_copy(k["sel"][:, :, :], k["sel_f"][:, :, :]))
        g.tensor_copy(k["bout_hi"][:, :], k["bout"][:, :, :].rearrange("o j d -> o (j d)"))
        chain(g.tensor_copy(k["bo_hi"][:, :], k["bo16"][:, :]))
        g.tensor_tensor(k["bout_lo"][:, :], k["bout"][:, :, :].rearrange("o j d -> o (j d)"), k["bout_hi"][:, :].bitcast(F32), ALU.subtract)
        chain(g.tensor_tensor(k["bo_lo"][:, :], k["bo16"][:, :], k["bo_hi"][:, :].bitcast(F32), ALU.subtract))
        self.pool_consts = c[0]
        self.pool_chain = chain
        self.pool_c = c

    def setup_pool_late(self, pool):
        g, k, chain = self.nc.gpsimd, self.k, self.pool_chain
        pool.wait_ge(self.act_setup, 2)
        cols = k["cols"]
        chain(g.tensor_scalar(k["whqk"][:, :], k["whqk"][:, :], cols[:, 0:1], None, ALU.mult))
        chain(g.tensor_copy(k["wh_hi"][:, :], k["whqk"][:, :]))
        chain(g.tensor_tensor(k["wh_lo"][:, :], k["whqk"][:, :], k["wh_hi"][:, :].bitcast(F32), ALU.subtract))
        chain(g.tensor_tensor(k["bcols"][:, :], k["bcols"][:, :], cols[:, 2:5], ALU.add))
        g.tensor_scalar(k["quadw"][:, :], cols[:, 5:7], 1.0 / G, None, ALU.mult)
        g.tensor_scalar(k["quadb"][:, :], cols[:, 9:11], 1.0 / G, None, ALU.mult)
        chain(g.tensor_copy(k["vb_hi"][:, :], k["vb"][:, :]))
        chain(g.tensor_tensor(k["vb_lo"][:, :], k["vb"][:, :], k["vb_hi"][:, :].bitcast(F32), ALU.subtract))
        chain(g.tensor_copy(k["wg_hi"][:, :], cols[:, 13:21]))
        chain(g.tensor_tensor(k["wg_lo"][:, :], cols[:, 13:21], k["wg_hi"][:, :].bitcast(F32), ALU.subtract))
        pool.wait_ge(self.setup_skew, 16 * (G + P // G))
        chain(g.affine_select(out=k["biasT"][:, :], in_=k["biasT"][:, :], compare_op=ALU.is_ge, fill=MASKED, base=0,
                              pattern=[[1, P]], channel_multiplier=-1))
        self.pool_done = self.pool_c[0]

    def setup_pe(self, pe):
        t, k, bank = self.nc.tensor, self.k, self.bank
        pe.wait_ge(self.setup_loaded, 16 * self.n_loads)
        pe.wait_ge(self.setup_pool, self.pool_consts)
        t.transpose(bank[3][:, 0:NROWS], k["rows"][:, :], self.ident[0:NROWS, 0:NROWS])
        for h in range(2):
            ins = t.transpose(bank[3][:, 128 + h * D:128 + (h + 1) * D], k["wo"][:, h * P:(h + 1) * P], self.ident[:, :])
        ins.then_inc(self.setup_cols, 1)
        pe.wait_ge(self.act_setup, 1)
        lnb = k["cols"][:, 1:2]
        t.matmul(bank[7][0:1, 0:HID], lnb, k["whqk"][:, 0:HID], start=True, stop=False)
        t.matmul(bank[7][0:1, 0:HID], k["one11"][:, :], k["bh_row"][:, :], start=False, stop=True)
        for c in range(3):
            ins = t.matmul(bank[3][:, c:c + 1], k["whqk"][:, HID + c * P:HID + (c + 1) * P], lnb, start=True, stop=True)
        ins.then_inc(self.setup_cols, 1)

    def setup_act(self, act):
        a, k, bank = self.nc.scalar, self.k, self.bank
        act.wait_ge(self.setup_cols, 1)
        a.copy(k["cols"][:, :], bank[3][:, 0:NROWS])
        a.copy(k["woT"][:, :, :], bank[3][:, 128:128 + 2 * D].rearrange("p (h d) -> p h d", h=2)).then_inc(self.act_setup, 1)
        act.wait_ge(self.setup_cols, 2)
        a.copy(k["vb"][:, :], bank[7][0:1, 0:HID])
        a.copy(k["bcols"][:, :], bank[3][:, 0:3]).then_inc(self.act_setup, 1)

    @staticmethod
    def bodies(eng, body):
        body(eng, 0, 1, r=0)
        body(eng, 1, 0, r=1, a=0)
        with eng.Fori(0, (B - 2) // 2) as i:
            k = 2 * i
            body(eng, 0, 1, r=k + 2, a=k + 1, f=k)
            body(eng, 1, 0, r=k + 3, a=k + 2, f=k + 1)
        body(eng, 0, 1, a=B - 1, f=B - 2)
        body(eng, 1, 0, f=B - 1)

    def sync(self, sp):
        b, s = self.b, self.s
        sp.wait_ge(self.rows_scattered, 16 * EP)
        self.load_contrib(sp, 0)
        for q in range(4):
            if q >= 2:
                sp.wait_ge(s["w1_mm"], 2 * (q - 1))
            dst = b[f"g{q % 2}"][:, :, :].rearrange("p h l -> p (h l)").rearrange("p (n d) -> p n d", d=D)
            sp.dma_start(dst, self.inputs["W1e"][2 * q:2 * q + 2].rearrange("e (c p) d -> p (e c) d", p=P)).then_inc(self.w1_loaded[q % 2], 16)

        def body(sp, ur, ua, r=None, a=None, f=None):
            if r is not None and not (isinstance(r, int) and r == B - 1):
                sp.wait_ge(s["sum_step"], 3 * r + 3)
                self.load_contrib(sp, r + 1)
            if f is not None:
                sp.wait_ge(s["outb"], f + 1)
                self.store_out(sp, f, ur)

        body(sp, 0, 1, r=0)
        body(sp, 1, 0, r=1, a=0)
        with sp.Fori(0, (B - 4) // 2) as i:
            k = 2 * i
            body(sp, 0, 1, r=k + 2, a=k + 1, f=k)
            body(sp, 1, 0, r=k + 3, a=k + 2, f=k + 1)
        body(sp, 0, 1, r=B - 2, a=B - 3, f=B - 4)
        body(sp, 1, 0, r=B - 1, a=B - 2, f=B - 3)
        body(sp, 0, 1, a=B - 1, f=B - 2)
        body(sp, 1, 0, f=B - 1)
        for u in range(2):
            sp.wait_ge(self.out_stored[u], 16 * (B // 2) + 16)

    def load_contrib(self, sp, r):
        src = self.contrib_view[r] if isinstance(r, int) else self.contrib_view[bass.ds(r, 1)].rearrange("o p j d -> (o p) j d")
        sp.dma_start(self.b["c"][:, :, :], src).then_inc(self.contrib_loaded, 16)

    def store_out(self, sp, f, u):
        dst = self.out_view[f] if isinstance(f, int) else self.out_view[bass.ds(f, 1)].rearrange("o p j d -> (o p) j d")
        sp.dma_start(dst, self.b[f"outb{u}"][:, :].rearrange("p (j d) -> p j d", d=D)).then_inc(self.out_stored[u], 16)

    def pool(self, pool):
        g, b, s, k = self.nc.gpsimd, self.b, self.s, self.k

        def rstd(name, n, step, at, done):
            var = b["mv_" + name][:, :].rearrange("p (j t) -> p j t", t=2)[:, :, 1]
            pool.wait_ge(s["mv_" + name], n)
            g.tensor_tensor(b["rs_" + name][:, :], var, k["eps"][:, :], ALU.add).then_inc(s[step], 1)
            pool.wait_ge(s[step], at)
            g.tensor_tensor(b["rs_" + name][:, :], b["rs_" + name][:, :], k["mhalf"][:, :], ALU.pow).then_inc(s[done], 1)

        def add_expert(f, e):
            pool.wait_ge(s["gc"], 8 * f + (e + 1))
            if e >= 2:
                pool.wait_ge(s["acc"], 7 * f + (e - 1))
            g.tensor_tensor(b["acc"][:, :, :], b["acc"][:, :, :], b[f"g{e % 2}"][:, :, :], ALU.add).then_inc(s["acc"], 1)

        def body(pool, ur, ua, r=None, a=None, f=None):
            if f is not None:
                add_expert(f, 1)
            if r is not None:
                c = b["c"]
                pool.wait_ge(self.contrib_loaded, 16 * r + 16)
                g.tensor_tensor(c[:, :, 0:512], c[:, :, 0:512], c[:, :, 512:1024], ALU.add).then_inc(s["sum_step"], 1)
            if f is not None:
                add_expert(f, 2)
            if r is not None:
                pool.wait_ge(s["sum_step"], 3 * r + 1)
                g.tensor_tensor(c[:, :, 0:256], c[:, :, 0:256], c[:, :, 256:512], ALU.add).then_inc(s["sum_step"], 1)
                pool.wait_ge(s["sum_step"], 3 * r + 2)
                if not (isinstance(r, int) and r == 0):
                    pool.wait_ge(s["z"], r)
                yv = b["y"][:, :].rearrange("p (j d) -> p j d", d=D)
                g.tensor_tensor(yv, c[:, :, 0:128], c[:, :, 128:256], ALU.add).then_inc(s["sum_step"], 1)
                pool.wait_ge(s["sum_step"], 3 * r + 3)
                bs = self.base_all[:, r, :] if isinstance(r, int) else self.base_all[:, bass.ds(r, 1), :].rearrange("p o d -> p (o d)")
                g.tensor_tensor(b["y"][:, :], b["y"][:, :], bs, ALU.add).then_inc(s["y"], 1)
            if f is not None:
                add_expert(f, 3)
                add_expert(f, 4)
            if r is not None:
                n = r + 1
                rstd("r", n, "rz_step", 6 * r + 1, "rz_step")
                var = b["mv_r"][:, :].rearrange("p (j t) -> p j t", t=2)[:, :, 1]
                pool.wait_ge(s["rz_step"], 6 * r + 2)
                g.tensor_tensor(b["rq"][:, :], b["rs_r"][:, :], b["rs_r"][:, :], ALU.mult).then_inc(s["rz_step"], 1)
                pool.wait_ge(s["rz_step"], 6 * r + 3)
                g.tensor_tensor(b["rq"][:, :], b["rq"][:, :], var, ALU.mult).then_inc(s["rz_step"], 1)
                pool.wait_ge(s["rz_step"], 6 * r + 4)
                g.tensor_tensor(b["rq"][:, :], b["rq"][:, :], k["eps"][:, :], ALU.add).then_inc(s["rz_step"], 1)
                pool.wait_ge(s["rz_step"], 6 * r + 5)
                g.tensor_tensor(b["rq"][:, :], b["rq"][:, :], k["mhalf"][:, :], ALU.pow).then_inc(s["rz_step"], 1)
                pool.wait_ge(s["rz_step"], 6 * r + 6)
                g.tensor_tensor(b["rz"][:, :], b["rq"][:, :], b["rs_r"][:, :], ALU.mult).then_inc(s["r12"], 1)
            if f is not None:
                add_expert(f, 5)
            if a is not None:
                rstd("a", a + 1, "rs_step", a + 1, "rs_a")
            if f is not None:
                add_expert(f, 6)
                add_expert(f, 7)
                rstd("f", f + 1, "rf_step", f + 1, "rs_f")

        self.bodies(pool, body)

    def act(self, act):
        a_, b, s, k, bank = self.nc.scalar, self.b, self.s, self.k, self.bank
        cols, SIG = k["cols"], ACT.Sigmoid
        X, Y, Z = bank[5], bank[6], bank[7]

        for q in range(8):
            act.wait_ge(s["w1_mm"], q + 1)
            a_.copy(b["w1_hi"][:, q, :], bank[q % 4][:, :]).then_inc(s["w1_hi"], 1)

        def gate(a, step, src, bias=None):
            if step >= 2:
                act.wait_ge(s["prod5"], 5 * a + (step - 1))
            kw = {} if bias is None else {"bias": bias}
            a_.activation(b[f"sgt{step % 2}"][:, :], src[:, :], SIG, **kw).then_inc(s["sig5"], 1)

        def sig(f, kk):
            e, h = divmod(kk, 2)
            act.wait_ge(s["b_mm"], 16 * f + (kk + 1))
            if kk >= 2:
                act.wait_ge(s["g"], 16 * f + (kk - 1))
            col = 21 + 4 * e + 2 + h
            a_.activation(b[f"sg{kk % 2}"][:, :], bank[2 * (kk % 2)][:, :], SIG, bias=cols[:, col:col + 1]).then_inc(s["sig"], 1)

        def body(act, ur, ua, r=None, a=None, f=None):
            uf = ur
            for e in range(E1 + 1):
                if f is not None and e < E1:
                    sig(f, 2 * e)
                if a is not None:
                    if e == 0:
                        act.wait_ge(s["zT_mm"], a + 1)
                        a_.copy(b["zh"][:, :], X[:, :]).then_inc(s["zh"], 1)
                    if e == 1:
                        act.wait_ge(s["v_mm"], a + 1)
                        gate(a, 0, Y)
                        gate(a, 1, Z)
                    if e == 2:
                        act.wait_ge(s["gate_mm"], 2 * a + 1)
                        gate(a, 2, X, k["bcols"][:, 0:1])
                        act.wait_ge(s["gate_mm"], 2 * a + 2)
                        gate(a, 3, Y, k["bcols"][:, 1:2])
                    if e == 3:
                        act.wait_ge(s["qk_mm"], a + 1)
                        gate(a, 4, Z, k["bcols"][:, 2:3])
                    if e == 4:
                        act.wait_ge(s["off_mm"], 2 * a + 1)
                        a_.copy(b["off1"][:, :], Z[:, :])
                        act.wait_ge(s["off_mm"], 2 * a + 2)
                        a_.copy(b["off2"][:, :], X[:, 0:256]).then_inc(s["off2"], 1)
                    if e == 7:
                        act.wait_ge(s["x3T_mm"], a + 1)
                        a_.copy(b[f"x3h{ua}"][:, :], Y[:, :]).then_inc(s["x3h"], 1)
                    if e == 8:
                        act.wait_ge(s["gate_step"], GATE_STEPS * a + 3)
                        a_.activation(b["s1"][:, :], b["dif"][:, :], SIG)
                        a_.activation(b["s2"][:, :], b["dif"][:, :], SIG, scale=-1.0).then_inc(s["sig_d"], 1)
                        act.wait_ge(s["combT_mm"], a + 1)
                        a_.copy(b[f"combT{ua}"][:, :], X[0:16, :]).then_inc(s["combT"], 1)
                if f is not None and e < E1:
                    sig(f, 2 * e + 1)

        self.bodies(act, body)

    def dve(self, dve):
        v, b, s, k, bank = self.nc.vector, self.b, self.s, self.k, self.bank
        cols = k["cols"]
        X, Y, Z = bank[5], bank[6], bank[7]

        for q in range(8):
            dve.wait_ge(s["w1_hi"], q + 1)
            v.tensor_tensor(b["w1_lo"][:, q, :], bank[q % 4][:, :], b["w1_hi"][:, q, :].bitcast(F32), ALU.subtract).then_inc(s["w1_lo"], 1)
        v.memset(self.landing(), 0.0).then_inc(s["y4"], 1)
        for u in range(2):
            v.memset(self.landing(), 0.0).then_inc(self.out_stored[u], 16)
        dve.wait_ge(self.setup_pool, self.pool_done)

        def stats(name, src, n):
            st = b["st_" + name][:, :].rearrange("p (j t) -> p j t", t=6)
            mv = b["mv_" + name][:, :].rearrange("p (j t) -> p j t", t=2)
            for j in range(NT):
                ins = v.bn_stats(st[:, j, :], src[:, j * D:(j + 1) * D])
            ins.then_inc(s["st_" + name], 1)
            dve.wait_ge(s["st_" + name], n)
            v.memset(self.landing(), 0.0)
            for j in range(NT):
                ins = v.bn_aggr(mv[:, j, :], st[:, j, :])
            ins.then_inc(s["mv_" + name], 1)

        def norm(name, dst, src, rs, done):
            mv = b["mv_" + name][:, :].rearrange("p (j t) -> p j t", t=2)
            for j in range(NT):
                ins = v.tensor_scalar(dst[:, j * D:(j + 1) * D], src[:, j * D:(j + 1) * D], mv[:, j, 0:1], rs[:, j:j + 1], ALU.subtract, ALU.mult)
            if done is not None:
                ins.then_inc(done, 1)

        def prod(a, step, src, dst, bias=None):
            dve.wait_ge(s["sig5"], 5 * a + (step + 1))
            sg = b[f"sgt{step % 2}"][:, :]
            if bias is None:
                v.tensor_tensor(dst, src[:, :], sg, ALU.mult).then_inc(s["prod5"], 1)
            else:
                v.scalar_tensor_tensor(out=dst, in0=src[:, :], scalar=bias, in1=sg, op0=ALU.add, op1=ALU.mult).then_inc(s["prod5"], 1)

        def half(f, kk):
            e, h = divmod(kk, 2)
            dve.wait_ge(s["sig"], 16 * f + (kk + 1))
            dve.wait_ge(s["a_mm"], 16 * f + (kk + 1))
            if h == 0 and e >= 3:
                dve.wait_ge(s["acc"], 7 * f + (e - 2))
            col = 21 + 4 * e + h
            v.scalar_tensor_tensor(out=b[f"g{e % 2}"][:, h, :], in0=bank[2 * (kk % 2) + 1][:, :], scalar=cols[:, col:col + 1],
                                   in1=b[f"sg{kk % 2}"][:, :], op0=ALU.add, op1=ALU.mult).then_inc(s["g"], 1)

        def weigh(f, e):
            dve.wait_ge(s["g"], 16 * f + (2 * e + 2))
            dve.wait_ge(s["cb_mm"], 8 * f + (e + 1))
            dst = b["acc"] if e == 0 else b[f"g{e % 2}"]
            v.tensor_tensor(dst[:, :, :], b[f"g{e % 2}"][:, :, :], bcast_mid(bank[4][:, :], 2), ALU.mult).then_inc(s["gc"], 1)

        def gating(a, ua):
            done = [0]

            def link(ins):
                done[0] += 1
                ins.then_inc(s["gate_step"], 1)
                dve.wait_ge(s["gate_step"], GATE_STEPS * a + done[0])

            def t3(n):
                return b[n][:, :].rearrange("p (j e) -> p j e", e=E1)

            dve.wait_ge(s["lg_mm"], a + 1)
            link(v.tensor_copy(b["lgs"][:, :], Z[:, 0:NT * E1]))
            v.memset(self.landing(), 0.0)
            for j in range(NT):
                ins = v.max(t3("top")[:, j, :], t3("lgs")[:, j, :])
            link(ins)
            link(v.tensor_tensor(t3("dif"), t3("top"), bcast_last(t3("top")[:, :, 0], E1), ALU.subtract))
            v.memset(self.landing(), 0.0)
            for j in range(NT):
                ins = v.max_index(b["idx"][:, 8 * j:8 * j + 8], t3("top")[:, j, :], t3("lgs")[:, j, :])
            link(ins)
            link(v.tensor_copy(b["idxf"][:, :], b["idx"][:, :]))
            idxf = t3("idxf")
            iota = bcast_mid(k["iota8"][:, :], NT)
            v.tensor_tensor(t3("m0"), iota, bcast_last(idxf[:, :, 0], E1), ALU.is_equal)
            link(v.tensor_tensor(t3("m1"), iota, bcast_last(idxf[:, :, 1], E1), ALU.is_equal))
            dve.wait_ge(s["sig_d"], a + 1)
            link(v.reciprocal(b["s2"][:, :], b["s2"][:, :]))
            link(v.tensor_tensor(b["s1"][:, :], b["s1"][:, :], b["s2"][:, :], ALU.mult))
            link(v.tensor_reduce(b["zsum"][:, :], t3("s1"), AX.X, ALU.add))
            link(v.reciprocal(b["zsum"][:, :], b["zsum"][:, :]))
            link(v.tensor_tensor(b["p01"][:, :, :], t3("s1")[:, :, 0:2], bcast_last(b["zsum"][:, :], 2), ALU.mult))
            link(v.scalar_tensor_tensor(out=b["den"][:, :], in0=b["p01"][:, :, 0], scalar=1e-9, in1=b["p01"][:, :, 1], op0=ALU.add, op1=ALU.add))
            link(v.reciprocal(b["den"][:, :], b["den"][:, :]))
            link(v.tensor_tensor(b["p01"][:, :, :], b["p01"][:, :, :], bcast_last(b["den"][:, :], 2), ALU.mult))
            v.tensor_tensor(t3("m0"), t3("m0"), bcast_last(b["p01"][:, :, 0], E1), ALU.mult)
            link(v.tensor_tensor(t3("m1"), t3("m1"), bcast_last(b["p01"][:, :, 1], E1), ALU.mult))
            link(v.tensor_tensor(b["m0"][:, :], b["m0"][:, :], b["m1"][:, :], ALU.add))
            ch = b["ch"][:, :].rearrange("p (j e) -> p j e", e=16)
            link(v.tensor_copy(b["chr"][:, :], b["m0"][:, :]))
            v.tensor_copy(ch[:, :, 0:E1], t3("chr").bitcast(F32))
            link(v.tensor_tensor(ch[:, :, E1:16], t3("m0"), t3("chr").bitcast(F32), ALU.subtract))
            assert done[0] == GATE_STEPS

        def body(dve, ur, ua, r=None, a=None, f=None):
            for e in range(E1 + 1):
                if f is not None and e < E1:
                    half(f, 2 * e)
                if a is not None:
                    if e == 0:
                        dve.wait_ge(s["zh"], a + 1)
                        v.tensor_tensor(b["zl"][:, :], X[:, :], b["zh"][:, :].bitcast(F32), ALU.subtract).then_inc(s["zl"], 1)
                    if e == 1:
                        prod(a, 0, Y, b["v"][:, 0:2, :].rearrange("p j e -> p (j e)"))
                        prod(a, 1, Z, b["v"][:, 2:4, :].rearrange("p j e -> p (j e)"))
                    if e == 2:
                        prod(a, 2, X, b["gateT"][:, 0, :], k["bcols"][:, 0:1])
                        prod(a, 3, Y, b["gateT"][:, 1, :], k["bcols"][:, 1:2])
                    if e == 3:
                        prod(a, 4, Z, b["qkT"][:, :], k["bcols"][:, 2:3])
                        dve.wait_ge(s["prod5"], 5 * a + 5)
                        for n, w, o in (("qq", k["quadw"][:, 0:1], k["quadb"][:, 0:1]), ("lq", k["quadw"][:, 1:2], k["quadb"][:, 1:2]),
                                        ("qk", cols[:, 7:8], cols[:, 11:12]), ("lk", cols[:, 8:9], cols[:, 12:13])):
                            ins = v.tensor_scalar(b[n][:, :], b["qkT"][:, :], w, o, ALU.mult, ALU.add)
                        ins.then_inc(s["quads"], 1)
                    if e == 4:
                        dve.wait_ge(s["diag_mm"], a + 1)
                        t_, ml = b["t"][:, :, :], b["ml"][:, :, :]
                        v.tensor_tensor(t_, X[:, :].rearrange("p (j i) -> p j i", i=P), bcast_mid(k["biasT"][:, :], NT), ALU.add).then_inc(s["t1"], 1)
                        v.tensor_tensor(ml, Y[:, :].rearrange("p (j i) -> p j i", i=P), bcast_mid(k["ltmask"][:, :], NT), ALU.mult)
                        dve.wait_ge(s["t1"], a + 1)
                        v.scalar_tensor_tensor(out=t_, in0=t_, scalar=0.0, in1=t_, op0=ALU.max, op1=ALU.mult).then_inc(s["t2"], 1)
                        dve.wait_ge(s["t2"], a + 1)
                        v.tensor_tensor(t_, t_, ml, ALU.add).then_inc(s["atd"], 1)
                    if e == 5:
                        for h, src in ((0, Y), (1, Z)):
                            dve.wait_ge(s["av_mm"], 2 * a + (h + 1))
                            v.tensor_tensor(b["goT"][:, h, :], src[:, :], b["gateT"][:, h, :], ALU.mult).then_inc(s["go"], 1)
                    if e == 6:
                        dve.wait_ge(s["w_mm"], a + 1)
                        v.scalar_tensor_tensor(out=b["y3"][:, :], in0=b[f"x2{ua}"][:, :], scalar=2.0, in1=X[:, :], op0=ALU.mult, op1=ALU.add).then_inc(s["y3"], 1)
                        dve.wait_ge(s["y3"], a + 1)
                        v.memset(self.landing(), 0.0)
                        stats("a", b["y3"], a + 1)
                    if e == 7:
                        dve.wait_ge(s["rs_a"], a + 1)
                        norm("a", b[f"x3{ua}"], b["y3"], b["rs_a"], s["x3"])
                    if e == 8:
                        dve.wait_ge(s["x3h"], a + 1)
                        v.tensor_tensor(b[f"x3l{ua}"][:, :], Y[:, :], b[f"x3h{ua}"][:, :].bitcast(F32), ALU.subtract).then_inc(s["x3l"], 1)
                    if e == 8:
                        gating(a, ua)
                if r is not None:
                    if e == 5:
                        dve.wait_ge(s["y"], r + 1)
                        v.memset(self.landing(), 0.0)
                        stats("r", b["y"], r + 1)
                    if e == 7:
                        dve.wait_ge(s["r12"], r + 1)
                        norm("r", b[f"x2{ur}"], b["y"], b["rs_r"], None)
                        norm("r", b[f"z{ur}"], b["y"], b["rz"], s["z"])
                if f is not None and e < E1:
                    half(f, 2 * e + 1)
                    weigh(f, e)
            if f is not None:
                uf = ur
                dve.wait_ge(s["out_mm"], f + 1)
                v.tensor_tensor(b["y4"][:, :], b[f"x3{uf}"][:, :], bank[4][:, :], ALU.add).then_inc(s["y4"], 1)
                dve.wait_ge(s["y4"], f + 2)
                v.memset(self.landing(), 0.0)
                stats("f", b["y4"], f + 1)
                dve.wait_ge(s["rs_f"], f + 1)
                dve.wait_ge(self.out_stored[uf], 8 * (f - uf) + 16)
                norm("f", b[f"outb{uf}"], b["y4"], b["rs_f"], s["outb"])

        self.bodies(dve, body)

    def pe(self, pe):
        t, b, s, k, bank = self.nc.tensor, self.b, self.s, self.k, self.bank
        X, Y, Z = bank[5], bank[6], bank[7]
        ident = self.ident

        def split3(dst, w_hi, w_lo, x_hi, x_lo, start=True, stop=True):
            t.matmul(dst, w_hi, x_hi, start=start, stop=False)
            t.matmul(dst, w_hi, x_lo, start=False, stop=False)
            return t.matmul(dst, w_lo, x_hi, start=False, stop=stop)

        pe.wait_ge(self.y_sb, EP)
        for q in range(8):
            if q % 2 == 0:
                pe.wait_ge(self.w1_loaded[(q // 2) % 2], 16 * (q // 4 + 1))
            if q >= 4:
                pe.wait_ge(s["w1_lo"], q - 3)
            src = b[f"g{(q // 2) % 2}"][:, :, :].rearrange("p h l -> p (h l)")
            for c in range(4):
                o = ((q % 2) * 4 + c) * D
                ins = t.transpose(bank[q % 4][:, c * P:(c + 1) * P], src[:, o:o + D], ident[:, :])
            ins.then_inc(s["w1_mm"], 1)
        pe.wait_ge(s["w1_lo"], 8)
        pe.wait_ge(self.setup_pool, self.pool_done)

        def up(f, uf, kk):
            e, h = divmod(kk, 2)
            xh, xl = b[f"x3h{uf}"][:, :], b[f"x3l{uf}"][:, :]
            if h == 0:
                if e == 0:
                    pe.wait_ge(s["combT"], f + 1)
                    pe.wait_ge(s["y4"], f + 1)
                else:
                    pe.wait_ge(s["gc"], 8 * f + e)
                t.matmul(bank[4][:, :], k["sel"][:, e, :], b[f"combT{uf}"][:, :], start=True, stop=True).then_inc(s["cb_mm"], 1)
            for part, o, done in (("b", H1, "b_mm"), ("a", 0, "a_mm")):
                if kk >= 2:
                    pe.wait_ge(s["sig" if part == "b" else "g"], 16 * f + (kk - 1))
                w = slice(o + h * P, o + (h + 1) * P)
                split3(bank[2 * (kk % 2) + (part == "a")][:, :], b["w1_hi"][:, e, w], b["w1_lo"][:, e, w], xh, xl).then_inc(s[done], 1)

        def body(pe, ur, ua, r=None, a=None, f=None):
            uf = ur
            zh, zl = b["zh"], b["zl"]
            hi, lo = k["wh_hi"], k["wh_lo"]
            for e in range(E1 + 1):
                if f is not None and e < E1:
                    up(f, uf, 2 * e)
                if a is not None:
                    if e == 0:
                        pe.wait_ge(s["z"], a + 1)
                        for j in range(NT):
                            ins = t.transpose(X[:, j * P:(j + 1) * P], b[f"z{ua}"][:, j * D:(j + 1) * D], ident[:, :])
                        ins.then_inc(s["zT_mm"], 1)
                    if e == 1:
                        pe.wait_ge(s["zl"], a + 1)
                        for j in range(NT):
                            dst = (Y, Z)[j // 2][:, (j % 2) * HID:(j % 2 + 1) * HID]
                            tok = slice(j * P, (j + 1) * P)
                            t.matmul(dst, k["ones"][:, :], k["vb_hi"][:, :], start=True, stop=False)
                            t.matmul(dst, k["ones"][:, :], k["vb_lo"][:, :], start=False, stop=False)
                            ins = split3(dst, zh[:, tok], zl[:, tok], hi[:, 0:HID], lo[:, 0:HID], start=False)
                        ins.then_inc(s["v_mm"], 1)
                    if e == 2:
                        split3(X[:, :], hi[:, HID:HID + P], lo[:, HID:HID + P], zh[:, :], zl[:, :]).then_inc(s["gate_mm"], 1)
                        pe.wait_ge(s["prod5"], 5 * a + 1)
                        split3(Y[:, :], hi[:, HID + P:2 * HID], lo[:, HID + P:2 * HID], zh[:, :], zl[:, :]).then_inc(s["gate_mm"], 1)
                    if e == 3:
                        pe.wait_ge(s["prod5"], 5 * a + 2)
                        split3(Z[:, :], hi[:, 2 * HID:], lo[:, 2 * HID:], zh[:, :], zl[:, :]).then_inc(s["qk_mm"], 1)
                    if e == 4:
                        pe.wait_ge(s["quads"], a + 1)
                        for j in range(NT):
                            tok = slice(j * P, (j + 1) * P)
                            t.matmul(X[:, tok], b["qk"][:, tok], b["qq"][:, tok], start=True, stop=True)
                            ins = t.matmul(Y[:, tok], b["lk"][:, tok], b["lq"][:, tok], start=True, stop=True)
                        ins.then_inc(s["diag_mm"], 1)
                        t.matmul(Z[:, 0:384], b["lk"][:, 0:P], b["lq"][:, P:L], start=True, stop=True)
                        t.matmul(Z[:, 384:512], b["lk"][:, 2 * P:3 * P], b["lq"][:, 3 * P:L], start=True, stop=True).then_inc(s["off_mm"], 1)
                        pe.wait_ge(s["t1"], a + 1)
                        t.matmul(X[:, 0:256], b["lk"][:, P:2 * P], b["lq"][:, 2 * P:L], start=True, stop=True).then_inc(s["off_mm"], 1)
                    if e == 5:
                        pe.wait_ge(s["atd"], a + 1)
                        pe.wait_ge(s["off2"], a + 1)
                        for h, dst in ((0, Y), (1, Z)):
                            c = slice(h * P, (h + 1) * P)
                            t.matmul(dst[:, P:L], b["v"][:, 0, c], b["off1"][:, 0:384], start=True, stop=False, skip_group_check=True)
                            t.matmul(dst[:, 0:P], b["v"][:, 0, c], b["t"][:, 0, :], start=False, stop=False, skip_group_check=True)
                            t.matmul(dst[:, 2 * P:L], b["v"][:, 1, c], b["off2"][:, 0:256], start=False, stop=False, skip_group_check=True)
                            t.matmul(dst[:, 3 * P:L], b["v"][:, 2, c], b["off1"][:, 384:512], start=False, stop=False, skip_group_check=True)
                            for j in range(1, NT):
                                ins = t.matmul(dst[:, j * P:(j + 1) * P], b["v"][:, j, c], b["t"][:, j, :], start=False, stop=(j == NT - 1), skip_group_check=True)
                            ins.then_inc(s["av_mm"], 1)
                    if e == 6:
                        t.matmul(X[:, :], k["ones"][:, :], k["bout_hi"][:, :], start=True, stop=False, skip_group_check=True)
                        t.matmul(X[:, :], k["ones"][:, :], k["bout_lo"][:, :], start=False, stop=False, skip_group_check=True)
                        pe.wait_ge(s["go"], 2 * a + 2)
                        for j in range(NT):
                            for h in range(2):
                                ins = t.matmul(X[:, j * D:(j + 1) * D], b["goT"][:, h, j * P:(j + 1) * P], k["wout"][:, h, :],
                                               start=False, stop=(h == 1), skip_group_check=True)
                        ins.then_inc(s["w_mm"], 1)
                    if e == 7:
                        pe.wait_ge(s["x3"], a + 1)
                        for j in range(NT):
                            ins = t.transpose(Y[:, j * P:(j + 1) * P], b[f"x3{ua}"][:, j * D:(j + 1) * D], ident[:, :])
                        ins.then_inc(s["x3T_mm"], 1)
                    if e == 8:
                        pe.wait_ge(s["x3l"], a + 1)
                        xh, xl = b[f"x3h{ua}"], b[f"x3l{ua}"]
                        for j in range(NT):
                            tok = slice(j * P, (j + 1) * P)
                            ins = split3(Z[:, j * E1:(j + 1) * E1], xh[:, tok], xl[:, tok], k["wg_hi"][:, :], k["wg_lo"][:, :])
                        ins.then_inc(s["lg_mm"], 1)
                if f is not None and e < E1:
                    up(f, uf, 2 * e + 1)
            if f is not None:
                pe.wait_ge(s["gc"], 8 * f + 8)
                cb = b[f"combT{uf}"]
                for j in range(NT):
                    tok = slice(j * P, (j + 1) * P)
                    dst = bank[4][:, j * D:(j + 1) * D]
                    t.matmul(dst, cb[:, tok], k["bo_hi"][:, :], start=True, stop=False)
                    t.matmul(dst, cb[:, tok], k["bo_lo"][:, :], start=False, stop=False)
                    if j == 0:
                        pe.wait_ge(s["acc"], 7 * f + 7)
                    t.matmul(dst, b["acc"][:, 0, tok], k["woT"][:, 0, :], start=False, stop=False)
                    ins = t.matmul(dst, b["acc"][:, 1, tok], k["woT"][:, 1, :], start=False, stop=True)
                ins.then_inc(s["out_mm"], 1)
            if a is not None:
                pe.wait_ge(s["gate_step"], GATE_STEPS * (a + 1))
                for j in range(NT):
                    ins = t.transpose(X[0:16, j * P:(j + 1) * P], b["ch"][:, j * 16:(j + 1) * 16], ident[:, :])
                ins.then_inc(s["combT_mm"], 1)

        self.bodies(pe, body)


def build(nc, x_in, Wq, Wm, W1, W2, g1, b1, g2, b2, router_w, w_gate, w_up, w_down, ws_gate_up, ws_down,
          ln_w, ln_b, Wh, bh, Wqk, bqk, qk_w, qk_b, rel_table, Wout, bout, Wg, W1e, b1e, Wo, bo, out):
    ctx = ExitStack()
    with ctx:
        def scope():
            return ExitStack()

        def sb(name, shape, dt=F32, where=ctx):
            return where.enter_context(nc.sbuf_tensor(name, shape, dt))

        def sem(name):
            return ctx.enter_context(nc.semaphore(name))

        table = nc.dram_tensor("token_rows", (T + 1, ROW), F32, kind="Internal").ap()
        contrib = nc.dram_tensor("routed_rows", (NKEY, D), F32, kind="Internal").ap()

        ident = sb("ident", [P, P])
        base_all = sb("base_all", [P, B, NT * D])
        landing_all = sb("landing", [P, 96])
        cells = iter(range(96))

        def landing():
            c = next(cells)
            return landing_all[:, c:c + 1]

        C = StageC(nc, sb, sem, None)
        AB = scope()
        x1T_all = sb("x1T_all", [P, T], where=AB)
        y_all = x1T_all
        rows_all = sb("rows_all", [P, EP * ROW], where=AB)
        ZCOLS = 4096
        zeros = rows_all[:, 0:ZCOLS]
        keyT = sb("keyT", [P, T // 2], where=AB)
        cand = sb("cand", [P, CAP], where=AB)
        both = sb("both", [E0, 2 * CAP], where=AB)
        slot_key = sb("slot_key", [E0, CAP], where=AB)
        dest_f = sb("dest_f", [P, EP], where=AB)
        dest_row = sb("dest_row", [P, EP], U32, where=AB)
        tok_row = sb("tok_row", [P, EP], U32, where=AB)
        wgu_e = sb("wgu_early", [P, 2 * EP_EARLY, 2, F0], where=AB)
        wd_e = sb("wd_early", [F0, 2 * EP_EARLY, D], where=AB)
        wsgu_sb = sb("wsgu_sb", [P, 2 * F0], where=AB)
        wsd_sb = sb("wsd_sb", [F0, D], where=AB)
        xgT = [sb(f"xgT{b}", [P, P], where=AB) for b in range(2)]
        sil = [sb(f"sil{b}", [F0, P], where=AB) for b in range(2)]
        hexp = [sb(f"hexp{b}", [F0, P], where=AB) for b in range(2)]
        A = scope()
        Wq_sb = sb("Wq_sb", [P, D], where=A)
        Wm_sb = sb("Wm_sb", [P, D], where=A)
        W1_sb = sb("W1_sb", [P, 2 * D], where=A)
        W2_sb = sb("W2_sb", [P, 2, D], where=A)
        rw_sb = sb("rw_sb", [E0, D], where=A)
        rwT = sb("rwT", [P, E0], where=A)
        g1_bc = sb("g1_bc", [P, D], where=A)
        g2_bc = sb("g2_bc", [P, D], where=A)
        b12_bc = sb("b12_bc", [P, 2, D], where=A)
        headmask = sb("headmask", [P, D + H0], where=A)
        reset = sb("reset", [P, NT * E0], where=A)
        mhalf = sb("mhalf", [P, 2 * NT], where=A)
        epsc = sb("epsc", [P, 2 * NT], where=A)
        keyc = [sb(f"keyc{u}", [P, NT * E0], where=A) for u in range(2)]
        keys = sb("keys", [P, NT, 2, E0], where=A)
        S = []
        for u in range(2):
            s = {}
            for name, cols in dict(x=NT * D, xT=L, feat=NT * D, e=NT * D, featT=L, hT=2 * L, r=NT * D,
                                   lg=NT * E0, zap=NT * E0, mask=NT * E0, ex=NT * E0, incl=NT * E0,
                                   stats=12 * NT, mv=4 * NT, rstd=2 * NT, stats3=6 * NT, mv3=2 * NT, rstd3=NT,
                                   z=NT * H0, kvm=D + H0, top=NT * 8, esum=NT, q=NT * (D + 4), xw=NT * ROW).items():
                s[name] = sb(f"{name}_{u}", [P, cols], where=A)
            s["x1T"] = s["hT"][:, 0:L]
            s["msg"], s["msgT"], s["m2T"], s["a1"], s["a2"] = s["e"], s["xT"], s["featT"], s["feat"], s["e"]
            S.append(s)
        A.close()
        late = scope()
        wgu_l = sb("wgu_late", [P, 2 * (EP - EP_EARLY), 2, F0], where=late)
        wd_l = sb("wd_late", [F0, 2 * (EP - EP_EARLY), D], where=late)
        late.close()
        AB.close()
        C.buffers(sb)

        bank = [ctx.enter_context(nc.psum_tensor(f"bank{k}", [P, 512], F32)) for k in range(8)]

        names = """consts_ready weights_ready zero_tile zeros_written xT_mm xT_sb q_mm negq eq feat_sb featT_mm kv_mm featT_sb kvm_sb
        num_mm z_step msg_sb msgT_mm msgT_sb m2T_mm m2T_sb hT_mm hT1_sb mlp_mm st1 mv1 var_eps rstd1
        xr1 xr2 centred r_step st3 mv3 rstd3 x1_sb x1T_mm x1T_sb x1T_kept lg_mm lg_sb pick_step soft_step
        d_sb ex_sb w_sb incl_sb ka_sb key_sb keyT_mm keyT_sb rwT_mm rwT_sb pool_setup late_weights early_weights
        round_done slots_sb slotT_mm slot_index sg_mm su_sb sh_sb ysh_mm ysh_sb base_sb
        xgT_mm xgT_sb gu_mm sil_sb hexp_sb y_mm y_sb rows_scattered""".split()
        s_ = {n: sem(n) for n in names}
        x_loaded = [sem(f"x_loaded{u}") for u in range(2)]
        xw_stored = [sem(f"xw_stored{u}") for u in range(2)]
        gathered = [sem(f"gathered{m}") for m in range(8)]

        x_view = x_in.rearrange("b (j p) d -> b p j d", p=P)
        table_view = table[0:T, :].rearrange("(b j p) r -> b p j r", j=NT, p=P)
        zero_view = contrib.rearrange("(n p f) d -> n p (f d)", p=P, f=ZCOLS // D)
        NZ = NKEY * D // (P * ZCOLS)

        def tiles(ap, w=D):
            return ap.rearrange("p (j d) -> p j d", d=w)

        def carve(k, cols, parts=P):
            return rows_all[0:parts, k * 512:k * 512 + cols]
        x1s = [carve(5 * u, 512) for u in range(2)]
        sgs = [carve(1 + 5 * u, 512, F0) for u in range(2)]
        sus = [carve(2 + 5 * u, 512, F0) for u in range(2)]
        shs = [carve(3 + 5 * u, 512, F0) for u in range(2)]
        yss = [carve(4 + 5 * u, 512) for u in range(2)]

        def late_early(pair):
            if pair < EP_EARLY:
                return wgu_e[:, 2 * pair:2 * pair + 2], wd_e[:, 2 * pair:2 * pair + 2]
            k = 2 * (pair - EP_EARLY)
            return wgu_l[:, k:k + 2], wd_l[:, k:k + 2]

        def expert_silu(act, m):
            act.wait_ge(s_["gu_mm"], m + 1)
            if m >= 2:
                act.wait_ge(s_["hexp_sb"], m - 1)
            nc.scalar.activation(sil[m % 2][:, :], bank[2 + m % 2][0:F0, 0:P], ACT.Silu).then_inc(s_["sil_sb"], 1)

        def expert_weigh(dve, m):
            dve.wait_ge(s_["y_mm"], m + 1)
            for h in range(2):
                part = slice(h * CAP, (h + 1) * CAP)
                w = rows_all[part, m * ROW + D + 2 * m + h:m * ROW + D + 2 * m + h + 1]
                ins = nc.vector.tensor_scalar(y_all[part, m * D:(m + 1) * D], bank[4 + m % 2][part, 0:D], w, None, ALU.mult)
            ins.then_inc(s_["y_sb"], 1)

        def expert_up(pe, m):
            wgu, _ = late_early(m)
            pe.wait_ge(s_["xgT_sb"], m + 1)
            if m >= 2:
                pe.wait_ge(s_["hexp_sb"], m - 1)
            for gu in range(2):
                for h in range(2):
                    ins = nc.tensor.matmul(bank[2 + m % 2][0:F0, gu * P + h * CAP:gu * P + (h + 1) * CAP], wgu[:, h, gu, :],
                                           xgT[m % 2][:, h * CAP:(h + 1) * CAP], start=True, stop=True)
            ins.then_inc(s_["gu_mm"], 1)

        def expert_down(pe, m):
            _, wd = late_early(m)
            pe.wait_ge(s_["hexp_sb"], m + 1)
            if m >= 2:
                pe.wait_ge(s_["y_sb"], m - 1)
            for h in range(2):
                ins = nc.tensor.matmul(bank[4 + m % 2][h * CAP:(h + 1) * CAP, 0:D], hexp[m % 2][:, h * CAP:(h + 1) * CAP], wd[:, h, :],
                                       start=True, stop=True)
            ins.then_inc(s_["y_mm"], 1)

        C.bank, C.ident, C.landing, C.base_all = bank, ident, landing, base_all
        C.rows_scattered, C.y_sb = s_["rows_scattered"], s_["y_sb"]
        C.skew = nc.dram_tensor("bias_rows", (G, 2 * G - 1), F32, kind="Internal").ap()
        C.contrib_view = contrib.rearrange("(b j p k) d -> b p j (k d)", j=NT, p=P, k=K0N)
        C.out_view = out.rearrange("b (j p) d -> b p j d", p=P)
        C.inputs = dict(Wq=Wq, ln_w=ln_w, ln_b=ln_b, Wh=Wh, bh=bh, Wqk=Wqk, bqk=bqk, qk_w=qk_w, qk_b=qk_b, rel_table=rel_table,
                        Wout=Wout, bout=bout, Wg=Wg, W1e=W1e, b1e=b1e, Wo=Wo, bo=bo)

        block = ctx.enter_context(nc.Block())


        @block.gpsimd
        def _(pool):
            g = nc.gpsimd
            count = [0]

            def chain(ins):
                count[0] += 1
                ins.then_inc(s_["pool_setup"], 1)
                pool.wait_ge(s_["pool_setup"], count[0])

            chain(g.memset(ident[:, :], 0.0))
            g.affine_select(out=ident[:, :], in_=ident[:, :], compare_op=ALU.not_equal, fill=1.0, base=0,
                            pattern=[[-1, P]], channel_multiplier=1).then_inc(s_["consts_ready"], 1)
            g.memset(zeros, 0.0).then_inc(s_["zero_tile"], 1)
            chain(g.memset(headmask[:, :], 1.0))
            hm = headmask[:, 0:D].rearrange("p (h v) -> p h v", v=DH)
            hi = headmask[:, D:D + H0]
            chain(g.affine_select(out=hm, in_=hm, compare_op=ALU.is_ge, fill=0.0, base=0, pattern=[[-DH, H0], [0, DH]], channel_multiplier=1))
            chain(g.affine_select(out=hm, in_=hm, compare_op=ALU.is_ge, fill=0.0, base=DH - 1, pattern=[[DH, H0], [0, DH]], channel_multiplier=-1))
            chain(g.affine_select(out=hi, in_=hi, compare_op=ALU.is_ge, fill=0.0, base=0, pattern=[[-DH, H0]], channel_multiplier=1))
            g.affine_select(out=hi, in_=hi, compare_op=ALU.is_ge, fill=0.0, base=DH - 1, pattern=[[DH, H0]], channel_multiplier=-1).then_inc(s_["consts_ready"], 1)
            chain(g.memset(reset[:, :], 1.0))
            chain(g.memset(tiles(reset[:, :], E0)[:, :, 0:1], 0.0))
            for u in range(2):
                g.memset(tiles(S[u]["q"][:, :], D + 4)[:, :, D:D + 4], 1.0).then_inc(s_["consts_ready"], 1)
                g.iota(keyc[u][:, :], pattern=[[-K0N * P, NT], [0, E0]], base=NKEY + 1 - K0N * L * PAIRS * u, channel_multiplier=-K0N,
                       allow_small_or_imprecise_dtypes=True).then_inc(s_["consts_ready"], 1)
            g.memset(epsc[:, :], EPS)
            g.memset(mhalf[:, :], -0.5).then_inc(s_["consts_ready"], 1)
            pool.wait_ge(s_["weights_ready"], 16 * 11)
            g.tensor_tensor(b12_bc[:, 0, :], b12_bc[:, 0, :], b12_bc[:, 1, :], ALU.add).then_inc(s_["consts_ready"], 1)
            pool.wait_ge(s_["consts_ready"], 8)
            C.setup_pool_early(pool)

            with pool.Fori(0, PAIRS) as i:
                for u in range(2):
                    s, n = S[u], 2 * i + (u + 1)
                    pool.wait_ge(x_loaded[u], 16 * i + 16)
                    g.tensor_tensor(s["r"][:, :], s["x"][:, :], s["x"][:, :], ALU.add).then_inc(s_["xr1"], 1)
                    pool.wait_ge(s_["xr1"], n)
                    g.tensor_tensor(tiles(s["r"][:, :]), tiles(s["r"][:, :]), bcast_mid(b12_bc[:, 0, :], NT), ALU.add).then_inc(s_["xr2"], 1)
                for u in range(2):
                    s, n = S[u], 2 * i + (u + 1)
                    pool.wait_ge(s_["mv1"], n)
                    var = tiles(s["mv"][:, :], 2)[:, :, 1]
                    g.tensor_tensor(s["rstd"][:, :], var, epsc[:, :], ALU.add).then_inc(s_["var_eps"], 1)
                    pool.wait_ge(s_["var_eps"], 4 * i + (u + 1))
                    g.tensor_tensor(s["rstd"][:, :], s["rstd"][:, :], mhalf[:, :], ALU.pow).then_inc(s_["rstd1"], 1)
                for u in range(2):
                    s, n = S[u], 2 * i + (u + 1)
                    pool.wait_ge(s_["mv3"], n)
                    var = tiles(s["mv3"][:, :], 2)[:, :, 1]
                    g.tensor_tensor(s["rstd3"][:, :], var, epsc[:, 0:NT], ALU.add).then_inc(s_["var_eps"], 1)
                    pool.wait_ge(s_["var_eps"], 4 * i + (u + 3))
                    g.tensor_tensor(s["rstd3"][:, :], s["rstd3"][:, :], mhalf[:, 0:NT], ALU.pow).then_inc(s_["rstd3"], 1)
                for u in range(2):
                    s, n = S[u], 2 * i + (u + 1)
                    pool.wait_ge(s_["x1T_sb"], n)
                    g.tensor_copy(x1T_all[:, bass.ds(i * L + u * (T // 2), L)], S[u]["x1T"]).then_inc(s_["x1T_kept"], 1)
                    pool.wait_ge(s_["incl_sb"], n)
                    g.tensor_tensor(s["incl"][:, :], keyc[u][:, :], s["incl"][:, :], ALU.subtract).then_inc(s_["ka_sb"], 1)
                    g.tensor_scalar(keyc[u][:, :], keyc[u][:, :], float(-K0N * L), None, ALU.add)
                    pool.wait_ge(s_["ka_sb"], n)
                    pool.wait_ge(s_["keyT_mm"], i + 1)
                    g.tensor_tensor(keys[:, :, u, :], tiles(s["incl"][:, :], E0), tiles(s["mask"][:, :], E0), ALU.mult).then_inc(s_["key_sb"], 1)
                    pool.wait_ge(s_["key_sb"], n)

            with pool.Fori(0, PAIRS) as i:
                for u in range(2):
                    n = 2 * i + (u + 1)
                    pool.wait_ge(s_["su_sb"], n)
                    g.tensor_tensor(shs[u], sgs[u], sus[u], ALU.mult).then_inc(s_["sh_sb"], 1)
                for u in range(2):
                    n = 2 * i + (u + 1)
                    pool.wait_ge(s_["ysh_sb"], n)
                    pool.wait_ge(x_loaded[u], 16 * i + 16 * (PAIRS + 1))
                    g.tensor_tensor(base_all[:, bass.ds(2 * i + u, 1), :].rearrange("p o d -> p (o d)"), x1s[u], yss[u], ALU.add).then_inc(s_["base_sb"], 1)

            C.setup_pool_late(pool)
            pool.wait_ge(s_["slot_index"], 2)
            pool.wait_ge(s_["x1T_kept"], B)
            pool.wait_ge(s_["base_sb"], B + 1)
            for u in range(2):
                pool.wait_ge(xw_stored[u], 16 * PAIRS + 16)
            pool.wait_ge(s_["zeros_written"], 16 * (NZ + 1))
            for m in range(EP):
                if m >= 8:
                    pool.wait_ge(gathered[m % 8], 16 * (m // 8))
                g.indirect_dma_start(rows_all[:, m * ROW:(m + 1) * ROW], None, table,
                                     bass.IndirectOffsetOnAxis(ap=tok_row[:, m:m + 1], axis=0)).then_inc(gathered[m % 8], 16)
            for m in range(EP):
                pool.wait_ge(s_["y_sb"], m + 1)
                g.indirect_dma_start(contrib, bass.IndirectOffsetOnAxis(ap=dest_row[:, m:m + 1], axis=0),
                                     y_all[:, m * D:(m + 1) * D], None, bounds_check=NKEY - 1, oob_is_err=False).then_inc(s_["rows_scattered"], 16)
            C.pool(pool)


        @block.sync
        def _(sp):
            for u in range(2):
                sp.dma_start(tiles(S[u]["x"][:, :]), x_view[PAIRS * u]).then_inc(x_loaded[u], 16)
            smalls = [(rw_sb[:, :], router_w), (Wq_sb[:, :], Wq), (Wm_sb[:, :], Wm), (W1_sb[:, :], W1),
                      (W2_sb[:, :, :], W2.rearrange("(h p) d -> p h d", p=P)),
                      (g1_bc[:, :], g1.partition_broadcast(P)), (g2_bc[:, :], g2.partition_broadcast(P)),
                      (b12_bc[:, 0, :], b1.partition_broadcast(P)), (b12_bc[:, 1, :], b2.partition_broadcast(P)),
                      (wsgu_sb[:, :], ws_gate_up), (wsd_sb[:, :], ws_down)]
            for dst, src in smalls:
                sp.dma_start(dst, src).then_inc(s_["weights_ready"], 16)
            C.setup_sync(sp)
            sp.wait_ge(s_["zero_tile"], 1)
            sp.dma_start(table[T:T + 1, :], zeros[0:1, 0:ROW]).then_inc(s_["zeros_written"], 16)
            for k in range(NZ // 2):
                sp.dma_start(zero_view[k], zeros).then_inc(s_["zeros_written"], 16)
            with sp.Fori(0, PAIRS - 1) as i:
                for u in range(2):
                    sp.wait_ge(s_["xT_mm"], 2 * i + u + 1)
                    sp.wait_ge(s_["xr1"], 2 * i + u + 1)
                    sp.dma_start(tiles(S[u]["x"][:, :]), x_view[bass.ds(i + (PAIRS * u + 1), 1)].rearrange("o p j d -> (o p) j d")).then_inc(x_loaded[u], 16)
                for u in range(2):
                    sp.wait_ge(s_["x1_sb"], 2 * i + u + 1)
                    sp.wait_ge(s_["w_sb"], 2 * i + u + 1)
                    sp.dma_start(table_view[bass.ds(i + PAIRS * u, 1)].rearrange("o p j d -> (o p) j d"), tiles(S[u]["xw"][:, :], ROW)).then_inc(xw_stored[u], 16)
            for u in range(2):
                sp.wait_ge(s_["x1_sb"], 2 * (PAIRS - 1) + u + 1)
                sp.wait_ge(s_["w_sb"], 2 * (PAIRS - 1) + u + 1)
                sp.dma_start(table_view[PAIRS - 1 + PAIRS * u], tiles(S[u]["xw"][:, :], ROW)).then_inc(xw_stored[u], 16)
            C.setup_sync_skew(sp)
            for u in range(2):
                sp.wait_ge(xw_stored[u], 16 * PAIRS + 16)
            sp.wait_ge(s_["zeros_written"], 16 * (NZ + 1))
            with sp.Fori(0, PAIRS) as i:
                for u in range(2):
                    sp.wait_ge(s_["base_sb"], 2 * i + 1)
                    sp.dma_start(tiles(x1s[u]), table_view[bass.ds(2 * i + u, 1), :, :, 0:D].rearrange("o p j d -> (o p) j d")).then_inc(x_loaded[u], 16)
            C.sync(sp)


        @block.scalar
        def _(act):
            a = nc.scalar
            n = 2 * EP_EARLY
            act.dma_start(wgu_e[:, :, 0, :], w_gate[0:n].rearrange("e p f -> p e f")).then_inc(s_["early_weights"], 16)
            act.dma_start(wgu_e[:, :, 1, :], w_up[0:n].rearrange("e p f -> p e f")).then_inc(s_["early_weights"], 16)
            act.dma_start(wd_e[:, :, :], w_down[0:n].rearrange("e p f -> p e f")).then_inc(s_["early_weights"], 16)
            act.wait_ge(s_["zero_tile"], 1)
            for k in range(NZ // 2, NZ):
                act.dma_start(zero_view[k], zeros).then_inc(s_["zeros_written"], 16)
            act.wait_ge(s_["rwT_mm"], 1)
            a.copy(rwT[:, :], bank[2][:, 0:E0]).then_inc(s_["rwT_sb"], 1)
            act.wait_ge(s_["consts_ready"], 8)
            with act.Fori(0, PAIRS) as i:
                for u in range(2):
                    n = 2 * i + (u + 1)
                    act.wait_ge(s_["xT_mm"], n)
                    a.copy(S[u]["xT"][:, :], bank[4 * u][:, :]).then_inc(s_["xT_sb"], 1)
                for u in range(2):
                    s, n = S[u], 2 * i + (u + 1)
                    act.wait_ge(s_["q_mm"], n)
                    a.activation(s["e"][:, :], bank[4 * u + 1][:, :], ACT.Relu, scale=-1.0).then_inc(s_["negq"], 1)
                    a.copy(tiles(s["q"][:, :], D + 4)[:, :, 0:D], tiles(bank[4 * u + 1][:, :]))
                    act.wait_ge(s_["negq"], n)
                    a.activation(s["e"][:, :], s["e"][:, :], ACT.Exp, scale=-1.0).then_inc(s_["eq"], 1)
                for u in range(2):
                    s, n = S[u], 2 * i + (u + 1)
                    act.wait_ge(s_["featT_mm"], n)
                    a.copy(s["featT"][:, :], bank[4 * u][:, :]).then_inc(s_["featT_sb"], 1)
                for u in range(2):
                    s, n = S[u], 2 * i + (u + 1)
                    act.wait_ge(s_["msgT_mm"], n)
                    a.copy(s["msgT"][:, :], bank[4 * u][:, :]).then_inc(s_["msgT_sb"], 1)
                for u in range(2):
                    s, n = S[u], 2 * i + (u + 1)
                    act.wait_ge(s_["m2T_mm"], n)
                    a.copy(s["m2T"][:, :], bank[4 * u + 2][:, :]).then_inc(s_["m2T_sb"], 1)
                for u in range(2):
                    s, n = S[u], 2 * i + (u + 1)
                    act.wait_ge(s_["hT_mm"], n)
                    a.activation(s["hT"][:, 0:L], bank[4 * u][:, :], ACT.Relu)
                    a.activation(s["hT"][:, L:2 * L], bank[4 * u + 3][:, :], ACT.Relu).then_inc(s_["hT1_sb"], 1)
                for u in range(2):
                    n = 2 * i + (u + 1)
                    act.wait_ge(s_["x1T_mm"], n)
                    a.copy(S[u]["x1T"], bank[4 * u][:, :]).then_inc(s_["x1T_sb"], 1)
                for u in range(2):
                    s, n = S[u], 2 * i + (u + 1)
                    act.wait_ge(s_["lg_mm"], n)
                    a.copy(s["lg"][:, :], bank[4 * u + 1][:, 0:NT * E0]).then_inc(s_["lg_sb"], 1)
                for u in range(2):
                    s, n = S[u], 2 * i + (u + 1)
                    act.wait_ge(s_["d_sb"], n)
                    a.activation(s["ex"][:, :], s["ex"][:, :], ACT.Exp).then_inc(s_["ex_sb"], 1)
                act.wait_ge(s_["keyT_mm"], i + 2)
                a.copy(keyT[:, bass.ds(i * L, L)], bank[3][:, :]).then_inc(s_["keyT_sb"], 1)

            for u in range(2):
                act.wait_ge(xw_stored[u], 16 * PAIRS + 16)
            act.wait_ge(s_["key_sb"], B)
            KL = EP - EP_EARLY
            for k in range(0, 2 * KL, KL // 2):
                e0 = 2 * EP_EARLY + k
                n = KL // 2
                act.dma_start(wgu_l[:, k:k + n, 0, :], w_gate[e0:e0 + n].rearrange("e p f -> p e f")).then_inc(s_["late_weights"], 16)
                act.dma_start(wgu_l[:, k:k + n, 1, :], w_up[e0:e0 + n].rearrange("e p f -> p e f")).then_inc(s_["late_weights"], 16)
                act.dma_start(wd_l[:, k:k + n, :], w_down[e0:e0 + n].rearrange("e p f -> p e f")).then_inc(s_["late_weights"], 16)

            act.wait_ge(s_["zeros_written"], 16 * (NZ + 1))
            with act.Fori(0, PAIRS) as i:
                for u in range(2):
                    n = 2 * i + (u + 1)
                    act.wait_ge(s_["sg_mm"], n)
                    a.activation(sgs[u], bank[4 * u][0:F0, :], ACT.Silu)
                    a.copy(sus[u], bank[4 * u + 1][0:F0, :]).then_inc(s_["su_sb"], 1)
                for u in range(2):
                    n = 2 * i + (u + 1)
                    act.wait_ge(s_["ysh_mm"], n)
                    a.copy(yss[u], bank[4 * u + 2][:, :]).then_inc(s_["ysh_sb"], 1)

            C.setup_act(act)
            for m in range(EP):
                act.wait_ge(s_["xgT_mm"], m + 1)
                a.copy(xgT[m % 2][:, :], bank[m % 2][:, 0:P]).then_inc(s_["xgT_sb"], 1)
                if m >= 1:
                    expert_silu(act, m - 1)
            expert_silu(act, EP - 1)
            C.act(act)


        @block.vector
        def _(dve):
            v = nc.vector
            v.memset(landing(), 0.0).then_inc(s_["keyT_mm"], 1)
            v.memset(landing(), 0.0).then_inc(s_["keyT_sb"], 1)
            v.memset(landing(), 0.0).then_inc(s_["base_sb"], 1)
            for u in range(2):
                v.memset(landing(), 0.0).then_inc(xw_stored[u], 16)
            dve.wait_ge(s_["consts_ready"], 8)
            with dve.Fori(0, PAIRS) as i:
                for u in range(2):
                    s, n = S[u], 2 * i + (u + 1)
                    dve.wait_ge(s_["eq"], n)
                    v.scalar_tensor_tensor(out=s["feat"][:, :], in0=bank[4 * u + 1][:, :], scalar=0.0, in1=s["e"][:, :],
                                           op0=ALU.max, op1=ALU.add).then_inc(s_["feat_sb"], 1)
                for u in range(2):
                    s, n = S[u], 2 * i + (u + 1)
                    dve.wait_ge(s_["kv_mm"], n)
                    v.tensor_tensor(s["kvm"][:, 0:D], bank[4 * u + 2][:, 0:D], headmask[:, 0:D], ALU.mult)
                    v.tensor_scalar(s["kvm"][:, D:D + H0], headmask[:, D:D + H0], bank[4 * u + 2][:, D:D + 1], None, ALU.mult).then_inc(s_["kvm_sb"], 1)
                for u in range(2):
                    s, n = S[u], 2 * i + (u + 1)
                    dve.wait_ge(s_["num_mm"], n)
                    v.tensor_scalar(s["z"][:, :], bank[4 * u + 2][:, 256:256 + NT * H0], ATTN_EPS, None, ALU.add).then_inc(s_["z_step"], 1)
                    dve.wait_ge(s_["z_step"], 2 * n - 1)
                    v.reciprocal(s["z"][:, :], s["z"][:, :]).then_inc(s_["z_step"], 1)
                    dve.wait_ge(s_["z_step"], 2 * n)
                    v.tensor_tensor(s["msg"][:, :].rearrange("p (a c) -> p a c", c=DH), bank[4 * u + 1][:, :].rearrange("p (a c) -> p a c", c=DH),
                                    bcast_last(s["z"][:, :], DH), ALU.mult).then_inc(s_["msg_sb"], 1)
                for u in range(2):
                    s, n = S[u], 2 * i + (u + 1)
                    dve.wait_ge(s_["mlp_mm"], n)
                    st = tiles(s["stats"][:, :], 6)
                    mv = tiles(s["mv"][:, :], 2)
                    for k in range(2):
                        for j in range(NT):
                            ins = v.bn_stats(st[:, NT * k + j, :], bank[4 * u + 1 + k][:, j * D:(j + 1) * D])
                    ins.then_inc(s_["st1"], 1)
                    dve.wait_ge(s_["st1"], n)
                    v.memset(landing(), 0.0)
                    for k in range(2 * NT):
                        ins = v.bn_aggr(mv[:, k, :], st[:, k, :])
                    ins.then_inc(s_["mv1"], 1)
                for u in range(2):
                    s, n = S[u], 2 * i + (u + 1)
                    mv = tiles(s["mv"][:, :], 2)
                    dve.wait_ge(s_["mv1"], n)
                    for k, dst, gain in ((0, "a1", g1_bc), (1, "a2", g2_bc)):
                        for j in range(NT):
                            ins = v.scalar_tensor_tensor(out=s[dst][:, j * D:(j + 1) * D], in0=bank[4 * u + 1 + k][:, j * D:(j + 1) * D],
                                                         scalar=mv[:, NT * k + j, 0:1], in1=gain[:, :], op0=ALU.subtract, op1=ALU.mult)
                    ins.then_inc(s_["centred"], 1)
                for u in range(2):
                    s, n = S[u], 2 * i + (u + 1)
                    dve.wait_ge(s_["centred"], n)
                    dve.wait_ge(s_["rstd1"], n)
                    dve.wait_ge(s_["xr2"], n)
                    for k, src in enumerate(("a1", "a2")):
                        for j in range(NT):
                            c = slice(j * D, (j + 1) * D)
                            ins = v.scalar_tensor_tensor(out=s["r"][:, c], in0=s[src][:, c], scalar=s["rstd"][:, NT * k + j:NT * k + j + 1],
                                                         in1=s["r"][:, c], op0=ALU.mult, op1=ALU.add)
                        ins.then_inc(s_["r_step"], 1)
                        dve.wait_ge(s_["r_step"], 2 * n - 1 + k)
                    v.memset(landing(), 0.0)
                    st, mv = tiles(s["stats3"][:, :], 6), tiles(s["mv3"][:, :], 2)
                    for j in range(NT):
                        ins = v.bn_stats(st[:, j, :], s["r"][:, j * D:(j + 1) * D])
                    ins.then_inc(s_["st3"], 1)
                    dve.wait_ge(s_["st3"], n)
                    v.memset(landing(), 0.0)
                    for j in range(NT):
                        ins = v.bn_aggr(mv[:, j, :], st[:, j, :])
                    ins.then_inc(s_["mv3"], 1)
                for u in range(2):
                    s, n = S[u], 2 * i + (u + 1)
                    mv, xw = tiles(s["mv3"][:, :], 2), tiles(s["xw"][:, :], ROW)
                    dve.wait_ge(s_["rstd3"], n)
                    dve.wait_ge(xw_stored[u], 16 * i + 16)
                    for j in range(NT):
                        ins = v.tensor_scalar(xw[:, j, 0:D], s["r"][:, j * D:(j + 1) * D], mv[:, j, 0:1], s["rstd3"][:, j:j + 1], ALU.subtract, ALU.mult)
                    ins.then_inc(s_["x1_sb"], 1)
                for u in range(2):
                    s, n = S[u], 2 * i + (u + 1)
                    dve.wait_ge(s_["lg_sb"], n)
                    v.memset(landing(), 0.0)
                    lg, top = tiles(s["lg"][:, :], E0), tiles(s["top"][:, :], 8)
                    for j in range(NT):
                        ins = v.max(top[:, j, :], lg[:, j, :])
                    ins.then_inc(s_["pick_step"], 1)
                    dve.wait_ge(s_["pick_step"], 3 * n - 2)
                    v.tensor_tensor(tiles(s["ex"][:, :], E0), lg, bcast_last(top[:, :, 0], E0), ALU.subtract).then_inc(s_["d_sb"], 1)
                    for j in range(NT):
                        ins = v.match_replace(tiles(s["zap"][:, :], E0)[:, j, :], top[:, j, :], lg[:, j, :], NEG)
                    ins.then_inc(s_["pick_step"], 1)
                    dve.wait_ge(s_["pick_step"], 3 * n - 1)
                    v.tensor_tensor(s["mask"][:, :], s["zap"][:, :], s["lg"][:, :], ALU.not_equal).then_inc(s_["pick_step"], 1)
                    dve.wait_ge(s_["pick_step"], 3 * n)
                    v.tensor_tensor_scan(s["incl"][:, :], reset[:, :], s["mask"][:, :], 0.0, ALU.mult, ALU.add).then_inc(s_["incl_sb"], 1)
                for u in range(2):
                    s, n = S[u], 2 * i + (u + 1)
                    xw = tiles(s["xw"][:, :], ROW)
                    dve.wait_ge(s_["ex_sb"], n)
                    v.tensor_tensor(s["ex"][:, :], s["ex"][:, :], s["mask"][:, :], ALU.mult).then_inc(s_["soft_step"], 1)
                    dve.wait_ge(s_["soft_step"], 3 * n - 2)
                    v.tensor_reduce(s["esum"][:, :], tiles(s["ex"][:, :], E0), AX.X, ALU.add).then_inc(s_["soft_step"], 1)
                    dve.wait_ge(s_["soft_step"], 3 * n - 1)
                    v.reciprocal(s["esum"][:, :], s["esum"][:, :]).then_inc(s_["soft_step"], 1)
                    dve.wait_ge(s_["soft_step"], 3 * n)
                    v.tensor_tensor(xw[:, :, D:ROW], tiles(s["ex"][:, :], E0), bcast_last(s["esum"][:, :], E0), ALU.mult).then_inc(s_["w_sb"], 1)

            rounds = [0]

            def step(ins):
                rounds[0] += 1
                ins.then_inc(s_["round_done"], 1)
                dve.wait_ge(s_["round_done"], rounds[0])

            dve.wait_ge(s_["keyT_sb"], PAIRS + 1)
            for r in range(CAP // 8):
                step(v.max(cand[:, 8 * r:8 * r + 8], keyT[:, :]))
                if r < CAP // 8 - 1:
                    step(v.match_replace(keyT[:, :], cand[:, 8 * r:8 * r + 8], keyT[:, :], 0.0))
            v.tensor_copy(both[:, 0:CAP], cand[0:E0, :])
            step(v.tensor_copy(both[:, CAP:2 * CAP], cand[E0:2 * E0, :]))
            for r in range(CAP // 8):
                step(v.max(slot_key[:, 8 * r:8 * r + 8], both[:, :]))
                if r < CAP // 8 - 1:
                    step(v.match_replace(both[:, :], slot_key[:, 8 * r:8 * r + 8], both[:, :], 0.0))
            v.tensor_scalar(slot_key[:, :], slot_key[:, :], -1.0, float(NKEY), ALU.mult, ALU.add).then_inc(s_["slots_sb"], 1)
            dve.wait_ge(s_["slotT_mm"], 1)
            pairs = bank[6][0:CAP, 0:E0].rearrange("c (m two) -> c m two", two=2)
            v.tensor_copy(dest_row[0:CAP, :], pairs[:, :, 0])
            v.tensor_copy(dest_row[CAP:2 * CAP, :], pairs[:, :, 1]).then_inc(s_["slot_index"], 1)
            dve.wait_ge(s_["slot_index"], 1)
            v.tensor_scalar(tok_row[:, :], dest_row[:, :], 3, None, ALU.logical_shift_right).then_inc(s_["slot_index"], 1)

            for m in range(EP):
                dve.wait_ge(s_["sil_sb"], m + 1)
                if m >= 2:
                    dve.wait_ge(s_["y_mm"], m - 1)
                v.tensor_tensor(hexp[m % 2][:, :], sil[m % 2][:, :], bank[2 + m % 2][0:F0, P:2 * P], ALU.mult).then_inc(s_["hexp_sb"], 1)
                if m >= 1:
                    expert_weigh(dve, m - 1)
            expert_weigh(dve, EP - 1)
            C.dve(dve)


        @block.tensor
        def _(pe):
            t = nc.tensor

            def transposes(dst, src, w=D):
                for j in range(NT):
                    ins = t.transpose(dst[:, j * P:(j + 1) * P], src[:, j * w:j * w + P], ident[:, :])
                return ins

            pe.wait_ge(s_["consts_ready"], 8)
            pe.wait_ge(s_["weights_ready"], 16 * 11)
            t.transpose(bank[2][:, 0:E0], rw_sb[:, :], ident[0:E0, 0:E0]).then_inc(s_["rwT_mm"], 1)
            pe.wait_ge(s_["rwT_sb"], 1)
            with pe.Fori(0, PAIRS) as i:
                for u in range(2):
                    pe.wait_ge(x_loaded[u], 16 * i + 16)
                    transposes(bank[4 * u], S[u]["x"]).then_inc(s_["xT_mm"], 1)
                for u in range(2):
                    s, n = S[u], 2 * i + (u + 1)
                    pe.wait_ge(s_["xT_sb"], n)
                    for j in range(NT):
                        ins = t.matmul(bank[4 * u + 1][:, j * D:(j + 1) * D], s["xT"][:, j * P:(j + 1) * P], Wq_sb[:, :], start=True, stop=True)
                    ins.then_inc(s_["q_mm"], 1)
                for u in range(2):
                    s, n = S[u], 2 * i + (u + 1)
                    pe.wait_ge(s_["feat_sb"], n)
                    transposes(bank[4 * u], s["feat"]).then_inc(s_["featT_mm"], 1)
                    for j in range(NT):
                        ins = t.matmul(bank[4 * u + 2][:, 0:D + 1], s["feat"][:, j * D:(j + 1) * D], s["q"][:, j * (D + 4):j * (D + 4) + D + 1],
                                       start=(j == 0), stop=(j == NT - 1))
                    ins.then_inc(s_["kv_mm"], 1)
                for u in range(2):
                    s, n = S[u], 2 * i + (u + 1)
                    pe.wait_ge(s_["featT_sb"], n)
                    pe.wait_ge(s_["kvm_sb"], n)
                    for j in range(NT):
                        ft = s["featT"][:, j * P:(j + 1) * P]
                        t.matmul(bank[4 * u + 1][:, j * D:(j + 1) * D], ft, s["kvm"][:, 0:D], start=True, stop=True)
                        ins = t.matmul(bank[4 * u + 2][:, 256 + j * H0:256 + (j + 1) * H0], ft, s["kvm"][:, D:D + H0], start=True, stop=True)
                    ins.then_inc(s_["num_mm"], 1)
                for u in range(2):
                    s, n = S[u], 2 * i + (u + 1)
                    pe.wait_ge(s_["msg_sb"], n)
                    transposes(bank[4 * u], s["msg"]).then_inc(s_["msgT_mm"], 1)
                for u in range(2):
                    s, n = S[u], 2 * i + (u + 1)
                    pe.wait_ge(s_["msgT_sb"], n)
                    t.matmul(bank[4 * u + 2][:, :], Wm_sb[:, :], s["msgT"][:, :], start=True, stop=True).then_inc(s_["m2T_mm"], 1)
                    for j in range(NT):
                        t.matmul(bank[4 * u + 1][:, j * D:(j + 1) * D], s["msgT"][:, j * P:(j + 1) * P], Wm_sb[:, :], start=True, stop=True)
                pe.wait_ge(s_["keyT_sb"], i + 1)
                for u in range(2):
                    s, n = S[u], 2 * i + (u + 1)
                    pe.wait_ge(s_["m2T_sb"], n)
                    t.matmul(bank[4 * u][:, :], W1_sb[:, 0:D], s["m2T"][:, :], start=True, stop=True)
                    t.matmul(bank[4 * u + 3][:, :], W1_sb[:, D:2 * D], s["m2T"][:, :], start=True, stop=True).then_inc(s_["hT_mm"], 1)
                for u in range(2):
                    s, n = S[u], 2 * i + (u + 1)
                    pe.wait_ge(s_["hT1_sb"], n)
                    for j in range(NT):
                        for h in range(2):
                            ins = t.matmul(bank[4 * u + 2][:, j * D:(j + 1) * D], s["hT"][:, h * L + j * P:h * L + (j + 1) * P], W2_sb[:, h, :],
                                           start=(h == 0), stop=(h == 1))
                    ins.then_inc(s_["mlp_mm"], 1)
                for u in range(2):
                    s, n = S[u], 2 * i + (u + 1)
                    pe.wait_ge(s_["x1_sb"], n)
                    transposes(bank[4 * u], s["xw"], ROW).then_inc(s_["x1T_mm"], 1)
                for u in range(2):
                    n = 2 * i + (u + 1)
                    pe.wait_ge(s_["x1T_sb"], n)
                    for j in range(NT):
                        ins = t.matmul(bank[4 * u + 1][:, j * E0:(j + 1) * E0], S[u]["x1T"][:, j * P:(j + 1) * P], rwT[:, :], start=True, stop=True)
                    ins.then_inc(s_["lg_mm"], 1)
                pe.wait_ge(s_["key_sb"], 2 * i + 2)
                for j in range(NT):
                    ins = t.transpose(bank[3][:, j * P:(j + 1) * P], keys[:, j, :, :].rearrange("p u e -> p (u e)"), ident[:, :])
                ins.then_inc(s_["keyT_mm"], 1)

            with pe.Fori(0, PAIRS) as i:
                for u in range(2):
                    n = 2 * i + (u + 1)
                    xs = x1T_all[:, bass.ds(i * 2 * L + u * L, L)]
                    t.matmul(bank[4 * u][0:F0, :], wsgu_sb[:, 0:F0], xs, start=True, stop=True)
                    t.matmul(bank[4 * u + 1][0:F0, :], wsgu_sb[:, F0:2 * F0], xs, start=True, stop=True).then_inc(s_["sg_mm"], 1)
                for u in range(2):
                    n = 2 * i + (u + 1)
                    pe.wait_ge(s_["sh_sb"], n)
                    for j in range(NT):
                        ins = t.matmul(bank[4 * u + 2][:, j * D:(j + 1) * D], shs[u][:, j * P:(j + 1) * P], wsd_sb[:, :], start=True, stop=True)
                    ins.then_inc(s_["ysh_mm"], 1)

            C.setup_pe(pe)
            pe.wait_ge(s_["slots_sb"], 1)
            pe.wait_ge(s_["ysh_sb"], B)
            t.transpose(bank[6][0:CAP, 0:E0], slot_key[:, :], ident[0:E0, 0:E0]).then_inc(s_["slotT_mm"], 1)
            pe.wait_ge(s_["early_weights"], 16 * 3)
            for m in range(EP + 2):
                if m == EP_EARLY:
                    pe.wait_ge(s_["late_weights"], 16 * 12)
                if m < EP:
                    pe.wait_ge(gathered[m % 8], 16 * (m // 8 + 1))
                    t.transpose(bank[m % 2][:, 0:P], rows_all[:, m * ROW:m * ROW + D], ident[:, :]).then_inc(s_["xgT_mm"], 1)
                if 1 <= m <= EP:
                    expert_up(pe, m - 1)
                if m >= 2:
                    expert_down(pe, m - 2)
            C.pe(pe)


_INS = ["L0_attn_x", "L0_attn_Wq", "L0_attn_Wm", "L0_attn_W1", "L0_attn_W2", "L0_attn_g1", "L0_attn_b1", "L0_attn_g2",
        "L0_attn_b2", "L0_ffn_router_w", "L0_ffn_w_gate", "L0_ffn_w_up", "L0_ffn_w_down", "L0_ffn_ws_gate_up",
        "L0_ffn_ws_down", "L1_attn_ln_w", "L1_attn_ln_b", "L1_attn_Wh", "L1_attn_bh", "L1_attn_Wqk", "L1_attn_bqk",
        "L1_attn_qk_w", "L1_attn_qk_b", "L1_attn_rel_table", "L1_attn_Wout", "L1_attn_bout", "L1_ffn_Wg", "L1_ffn_W1",
        "L1_ffn_b1", "L1_ffn_Wo", "L1_ffn_bo"]


def kernel(**inputs):
    import concourse.bacc as bacc
    from concourse.bass_utils import run_bass_kernel_spmd as run

    nc = bacc.Bacc("TRN2", target_bir_lowering=False, num_devices=1)
    arrays, args = {}, []
    for name in _INS:
        a = np.ascontiguousarray(inputs[name])
        arrays[f"in_{name}"] = a
        args.append(nc.dram_tensor(f"in_{name}", a.shape, mybir.dt.from_np(a.dtype), kind="ExternalInput").ap())
    out = nc.dram_tensor("out_0", (B, L, D), F32, kind="ExternalOutput").ap()
    build(nc, *args, out)
    r = run(nc, [arrays], core_ids=[0])
    return r.results[0]["out_0"]
```

```python
import numpy as np
import concourse.bass as bass
from concourse import mybir
from contextlib import ExitStack

F32 = mybir.dt.float32
F32R = mybir.dt.float32r
I32 = mybir.dt.int32
U32 = mybir.dt.uint32
ALU = mybir.AluOpType
ACT = mybir.ActivationFunctionType
AX = mybir.AxisListType

P = 128
B, L, D = 8, 512, 128
T = B * L
NT = L // P
PAIRS = B // 2
EPS = 1e-5
H0, DH = 8, 16
ATTN_EPS = 1e-6
E0, K0N, F0, CAP = 64, 8, 96, 64
EP = E0 // 2
EP_EARLY = 12
ROW = D + E0
NKEY = T * K0N
NEG = -3.0e38
STRUCK = 3.0e38
G, HID, QK = 32, 256, 128
BIAS_SCALE = float(QK) ** 0.5
NBUCKET, MAXDIST = 32, 128
E1, H1 = 8, 256
MASKED = -1e30
NROWS = 5 + 4 + 4 + E1 + 4 * E1
AT = dict(zT=0, out=2, gate=2, y4=3, quads=3, gate2=3, v=4, outb=5, sim=6, off=7, av=8, w=9, x3=11, x3T=12, lg=13, y=6, z=11)
GATING = {13: (0, 1), 14: (2, 3, 4), 15: (5, 6, 7, 8)}
GATING_NEXT = {0: ((9, 10), (11,)), 1: ((12, 13), (14,))}
GATE_STEPS = 15
WEIGH = {2: 0, 3: 1, 5: 2, 7: 3, 9: 4, 11: 5, 13: 6, 15: 7}


def bcast_last(ap, n):
    shape = list(ap.shape) + [n]
    return ap.unsqueeze(len(shape) - 1).broadcast_to(shape)


def bcast_mid(ap, n):
    return ap.unsqueeze(1).broadcast_to([ap.shape[0], n, ap.shape[1]])


def bucket_runs():
    exact = NBUCKET // 2
    runs = []
    for n in range(G):
        if n < exact:
            b = n
        else:
            b = exact + int(np.float32(np.log(np.float32(n) / np.float32(exact))) / np.float32(np.log(MAXDIST / exact))
                            * np.float32(NBUCKET - exact))
            b = min(b, NBUCKET - 1)
        if runs and runs[-1][2] == b:
            runs[-1] = (runs[-1][0], runs[-1][1] + 1, b)
        else:
            runs.append((n, 1, b))
    return runs


def first(f):
    return isinstance(f, int) and f == 0


class StageC:

    def __init__(self, nc, sb, sem, region):
        self.nc = nc
        keep = {}
        def k(name, shape, dt=F32):
            keep[name] = sb("c_" + name, shape, dt)
        k("rows", [NROWS, D]); k("cols", [P, NROWS]); k("whqk", [P, 2 * HID + QK])
        k("wh_hi", [P, 2 * HID + QK], F32R); k("wh_lo", [P, 2 * HID + QK], F32R)
        k("vb", [1, HID]); k("vb_hi", [1, HID], F32R); k("vb_lo", [1, HID], F32R); k("bh_row", [1, HID]); k("one11", [1, 1])
        k("ones_f", [1, P]); k("ones", [1, P], F32R); k("bcols", [P, 3]); k("quadw", [P, 2]); k("quadb", [P, 2])
        k("biasT", [P, P]); k("ltmask", [P, P]); k("rel", [1, 64]); k("ext", [1, 64])
        k("wout", [P, 2, D]); k("wo", [P, H1]); k("woT", [P, 2, D])
        k("bout", [1, NT, D]); k("bout_hi", [1, NT * D], F32R); k("bout_lo", [1, NT * D], F32R)
        k("bo16", [16, D]); k("bo_hi", [16, D], F32R); k("bo_lo", [16, D], F32R)
        k("wg_hi", [P, E1], F32R); k("wg_lo", [P, E1], F32R)
        k("sel_f", [16, E1, P]); k("sel", [16, E1, P], F32R); k("iota8", [P, E1])
        k("mhalf", [P, NT]); k("eps", [P, NT])
        self.k = keep
        self.region = region
        self.sem = sem
        self.setup_loaded = sem("c_setup_loaded")
        self.setup_skew = sem("c_setup_skew")
        self.setup_pool = sem("c_setup_pool")
        self.act_setup = sem("c_setup_act")
        self.setup_cols = sem("c_setup_cols")
        self.n_loads = 19

    def buffers(self, sb):
        b = {}
        def k(name, shape, dt=F32):
            b[name] = sb("c_" + name, shape, dt)
        k("c", [P, NT, K0N * D]); k("y", [P, NT * D])
        k("w1_hi", [P, E1, 2 * H1], F32R); k("w1_lo", [P, E1, 2 * H1], F32R)
        for u in range(2):
            k(f"x2{u}", [P, NT * D]); k(f"z{u}", [P, NT * D]); k(f"x3{u}", [P, NT * D])
            k(f"x3h{u}", [P, L], F32R); k(f"x3l{u}", [P, L], F32R); k(f"combT{u}", [16, L], F32R)
            k(f"outb{u}", [P, NT * D]); k(f"sgt{u}", [P, L]); k(f"sg{u}", [P, L]); k(f"g{u}", [P, 2, L])
        k("zh", [P, L], F32R); k("zl", [P, L], F32R); k("v", [P, NT, HID]); k("gateT", [P, 2, L]); k("qkT", [P, L])
        for n in ("qq", "lq", "qk", "lk"):
            k(n, [P, L])
        k("t", [P, NT, P]); k("ml", [P, NT, P]); k("off1", [P, 512]); k("off2", [P, 256]); k("goT", [P, 2, L])
        k("y3", [P, NT * D]); k("acc0", [P, 2, L]); k("acc1", [P, 2, L]); k("y4", [P, NT * D])
        for n in ("r", "a", "f"):
            k(f"st_{n}", [P, 6 * NT]); k(f"mv_{n}", [P, 2 * NT]); k(f"rs_{n}", [P, NT])
        k("rq", [P, NT])
        for n in ("lgs", "top", "dif", "s1", "s2", "zap", "mask", "em", "comb"):
            k(n, [P, NT * E1])
        k("zsum", [P, NT]); k("esum", [P, NT]); k("den", [P, NT])
        k("ch", [P, NT * 16]); k("chr", [P, NT * E1], F32R)
        self.b = b
        self.contrib_loaded, self.out_stored = self.sem("contrib_loaded"), [self.sem(f"out_stored{u}") for u in range(2)]
        self.w1_loaded = [self.sem(f"w1_loaded{q}") for q in range(2)]
        self.s = {n: self.sem("c_" + n) for n in """w1_mm w1_hi w1_lo sum_step y st_r mv_r rz_step r12 z zT_mm zh zl
            v_mm gate_mm x2 sig5 prod5 quads diag_mm t1 t2 atd off_mm off2 av_mm go w_mm y3 st_a mv_a rs_step rf_step rs_a x3
            x3T_mm x3h x3l lg_mm gate_step sig_d combT_mm combT cb_mm b_mm a_mm sig g gc acc out_mm y4 st_f mv_f rs_f outb""".split()}

    def setup_sync(self, sp):
        k, i = self.k, self.inputs
        r = k["rows"]
        loads = [(r[0:1, :], i["ln_w"].unsqueeze(0)), (r[1:2, :], i["ln_b"].unsqueeze(0)),
                 (r[2:4, :], i["bh"][HID:2 * HID].rearrange("(h p) -> h p", p=P)), (r[4:5, :], i["bqk"].unsqueeze(0)),
                 (r[5:9, :], i["qk_w"]), (r[9:13, :], i["qk_b"]), (r[13:21, :], i["Wg"]),
                 (r[21:53, :], i["b1e"].rearrange("e (c p) -> (e c) p", p=P)), 
                 (k["whqk"][:, 0:2 * HID], i["Wh"]), (k["whqk"][:, 2 * HID:], i["Wqk"]),
                 (k["bh_row"][:, :], i["bh"][0:HID].unsqueeze(0)), (k["rel"][:, 0:NBUCKET], i["rel_table"].unsqueeze(0)),
                 (k["wout"][:, :, :], i["Wout"].rearrange("(h p) d -> p h d", p=P)), (k["wo"][:, :], i["Wo"]),
                 (k["bo16"][:, :], i["bo"].partition_broadcast(16))]
        loads += [(k["bout"][:, j, :], i["bout"].unsqueeze(0)) for j in range(NT)]
        assert len(loads) == self.n_loads
        for dst, src in loads:
            sp.dma_start(dst, src).then_inc(self.setup_loaded, 16)

    def setup_sync_skew(self, sp):
        k, G2 = self.k, 2 * G - 1
        sp.wait_ge(self.setup_pool, self.pool_ext)
        for j in range(G):
            sp.dma_start(self.skew[j:j + 1, :], k["ext"][0:1, 0:G2]).then_inc(self.setup_skew, 16)
        sp.wait_ge(self.setup_skew, 16 * G)
        src = bass.AP(tensor=self.skew.tensor, offset=G - 1, ap=[[G2 - 1, G], [1, G]])
        for q in range(P // G):
            sp.dma_start(k["biasT"][q * G:(q + 1) * G, q * G:(q + 1) * G], src).then_inc(self.setup_skew, 16)

    def setup_pool_early(self, pool):
        g, k = self.nc.gpsimd, self.k
        c = [0]

        def chain(ins):
            c[0] += 1
            ins.then_inc(self.setup_pool, 1)
            pool.wait_ge(self.setup_pool, c[0])
        pool.wait_ge(self.setup_loaded, 16 * self.n_loads)
        chain(g.memset(k["ext"][:, :], 0.0))
        for n0, cnt, b in bucket_runs():
            for n in range(n0, n0 + cnt):
                ins = g.tensor_scalar(k["ext"][:, G - 1 + n:G + n], k["rel"][:, b:b + 1], BIAS_SCALE, None, ALU.mult)
        chain(ins)
        self.pool_ext = c[0]
        chain(g.memset(k["biasT"][:, :], MASKED))
        self.pool_masked = c[0]
        chain(g.memset(k["ltmask"][:, :], 0.0))
        for q in range(P // G - 1):
            chain(g.memset(k["ltmask"][q * G:(q + 1) * G, (q + 1) * G:P], 1.0))
        g.memset(k["one11"][:, :], 1.0)
        g.memset(k["mhalf"][:, :], -0.5)
        g.memset(k["eps"][:, :], EPS)
        chain(g.memset(k["ones_f"][:, :], 1.0))
        g.tensor_copy(k["ones"][:, :], k["ones_f"][:, :])
        g.iota(k["iota8"][:, :], pattern=[[1, E1]], base=0, channel_multiplier=0, allow_small_or_imprecise_dtypes=True)
        chain(g.memset(k["sel_f"][:, :, :], 0.0))
        for o in (0, E1):
            chain(g.affine_select(out=k["sel_f"][:, :, :], in_=k["sel_f"][:, :, :], compare_op=ALU.not_equal, fill=1.0, base=-o,
                                  pattern=[[-1, E1], [0, P]], channel_multiplier=1))
        chain(g.tensor_copy(k["sel"][:, :, :], k["sel_f"][:, :, :]))
        g.tensor_copy(k["bout_hi"][:, :], k["bout"][:, :, :].rearrange("o j d -> o (j d)"))
        chain(g.tensor_copy(k["bo_hi"][:, :], k["bo16"][:, :]))
        g.tensor_tensor(k["bout_lo"][:, :], k["bout"][:, :, :].rearrange("o j d -> o (j d)"), k["bout_hi"][:, :].bitcast(F32), ALU.subtract)
        chain(g.tensor_tensor(k["bo_lo"][:, :], k["bo16"][:, :], k["bo_hi"][:, :].bitcast(F32), ALU.subtract))
        self.pool_consts = c[0]
        self.pool_chain = chain
        self.pool_c = c

    def setup_pool_late(self, pool):
        g, k, chain = self.nc.gpsimd, self.k, self.pool_chain
        pool.wait_ge(self.act_setup, 2)
        cols = k["cols"]
        chain(g.tensor_scalar(k["whqk"][:, :], k["whqk"][:, :], cols[:, 0:1], None, ALU.mult))
        chain(g.tensor_copy(k["wh_hi"][:, :], k["whqk"][:, :]))
        chain(g.tensor_tensor(k["wh_lo"][:, :], k["whqk"][:, :], k["wh_hi"][:, :].bitcast(F32), ALU.subtract))
        chain(g.tensor_tensor(k["bcols"][:, :], k["bcols"][:, :], cols[:, 2:5], ALU.add))
        g.tensor_scalar(k["quadw"][:, :], cols[:, 5:7], 1.0 / G, None, ALU.mult)
        g.tensor_scalar(k["quadb"][:, :], cols[:, 9:11], 1.0 / G, None, ALU.mult)
        chain(g.tensor_copy(k["vb_hi"][:, :], k["vb"][:, :]))
        chain(g.tensor_tensor(k["vb_lo"][:, :], k["vb"][:, :], k["vb_hi"][:, :].bitcast(F32), ALU.subtract))
        chain(g.tensor_copy(k["wg_hi"][:, :], cols[:, 13:21]))
        chain(g.tensor_tensor(k["wg_lo"][:, :], cols[:, 13:21], k["wg_hi"][:, :].bitcast(F32), ALU.subtract))
        pool.wait_ge(self.setup_skew, 16 * (G + P // G))
        chain(g.affine_select(out=k["biasT"][:, :], in_=k["biasT"][:, :], compare_op=ALU.is_ge, fill=MASKED, base=0,
                              pattern=[[1, P]], channel_multiplier=-1))
        self.pool_done = self.pool_c[0]

    def setup_pe(self, pe):
        t, k, bank = self.nc.tensor, self.k, self.bank
        pe.wait_ge(self.setup_loaded, 16 * self.n_loads)
        pe.wait_ge(self.setup_pool, self.pool_consts)
        t.transpose(bank[3][:, 0:NROWS], k["rows"][:, :], self.ident[0:NROWS, 0:NROWS])
        for h in range(2):
            ins = t.transpose(bank[3][:, 128 + h * D:128 + (h + 1) * D], k["wo"][:, h * P:(h + 1) * P], self.ident[:, :])
        ins.then_inc(self.setup_cols, 1)
        pe.wait_ge(self.act_setup, 1)
        lnb = k["cols"][:, 1:2]
        t.matmul(bank[7][0:1, 0:HID], lnb, k["whqk"][:, 0:HID], start=True, stop=False)
        t.matmul(bank[7][0:1, 0:HID], k["one11"][:, :], k["bh_row"][:, :], start=False, stop=True)
        for c in range(3):
            ins = t.matmul(bank[3][:, c:c + 1], k["whqk"][:, HID + c * P:HID + (c + 1) * P], lnb, start=True, stop=True)
        ins.then_inc(self.setup_cols, 1)

    def setup_act(self, act):
        a, k, bank = self.nc.scalar, self.k, self.bank
        act.wait_ge(self.setup_cols, 1)
        a.copy(k["cols"][:, :], bank[3][:, 0:NROWS])
        a.copy(k["woT"][:, :, :], bank[3][:, 128:128 + 2 * D].rearrange("p (h d) -> p h d", h=2)).then_inc(self.act_setup, 1)
        act.wait_ge(self.setup_cols, 2)
        a.copy(k["vb"][:, :], bank[7][0:1, 0:HID])
        a.copy(k["bcols"][:, :], bank[3][:, 0:3]).then_inc(self.act_setup, 1)

    @staticmethod
    def bodies(eng, body):
        body(eng, 0, 1, r=0)
        body(eng, 1, 0, r=1, a=0)
        body(eng, 0, 1, r=2, a=1, f=0)
        with eng.Fori(0, (B - 4) // 2) as i:
            k = 2 * i
            body(eng, 1, 0, r=k + 3, a=k + 2, f=k + 1, t=k)
            body(eng, 0, 1, r=k + 4, a=k + 3, f=k + 2, t=k + 1)
        body(eng, 1, 0, r=B - 1, a=B - 2, f=B - 3, t=B - 4)
        body(eng, 0, 1, a=B - 1, f=B - 2, t=B - 3)
        body(eng, 1, 0, f=B - 1, t=B - 2)
        body(eng, 0, 1, t=B - 1)

    def sync(self, sp):
        b, s = self.b, self.s
        sp.wait_ge(self.rows_scattered, 16 * EP)
        self.load_contrib(sp, 0)
        for q in range(4):
            if q >= 2:
                sp.wait_ge(s["w1_mm"], 2 * (q - 1))
            dst = b[f"g{q % 2}"][:, :, :].rearrange("p h l -> p (h l)").rearrange("p (n d) -> p n d", d=D)
            sp.dma_start(dst, self.inputs["W1e"][2 * q:2 * q + 2].rearrange("e (c p) d -> p (e c) d", p=P)).then_inc(self.w1_loaded[q % 2], 16)

        def body(sp, ur, ua, r=None, a=None, f=None, t=None):
            if r is not None and not (isinstance(r, int) and r == B - 1):
                sp.wait_ge(s["sum_step"], 3 * r + 3)
                self.load_contrib(sp, r + 1)
            if t is not None:
                sp.wait_ge(s["outb"], t + 1)
                self.store_out(sp, t, ua)

        self.bodies(sp, body)
        for u in range(2):
            sp.wait_ge(self.out_stored[u], 16 * (B // 2) + 16)

    def load_contrib(self, sp, r):
        src = self.contrib_view[r] if isinstance(r, int) else self.contrib_view[bass.ds(r, 1)].rearrange("o p j d -> (o p) j d")
        sp.dma_start(self.b["c"][:, :, :], src).then_inc(self.contrib_loaded, 16)

    def store_out(self, sp, f, u):
        dst = self.out_view[f] if isinstance(f, int) else self.out_view[bass.ds(f, 1)].rearrange("o p j d -> (o p) j d")
        sp.dma_start(dst, self.b[f"outb{u}"][:, :].rearrange("p (j d) -> p j d", d=D)).then_inc(self.out_stored[u], 16)

    def pool(self, pool):
        g, b, s, k = self.nc.gpsimd, self.b, self.s, self.k

        def rstd(name, n, step, at, done):
            var = b["mv_" + name][:, :].rearrange("p (j t) -> p j t", t=2)[:, :, 1]
            pool.wait_ge(s["mv_" + name], n)
            g.tensor_tensor(b["rs_" + name][:, :], var, k["eps"][:, :], ALU.add).then_inc(s[step], 1)
            pool.wait_ge(s[step], at)
            g.tensor_tensor(b["rs_" + name][:, :], b["rs_" + name][:, :], k["mhalf"][:, :], ALU.pow).then_inc(s[done], 1)

        def add_expert(f, uf, e):
            pool.wait_ge(s["gc"], 8 * f + (e + 1))
            if e >= 2:
                pool.wait_ge(s["acc"], 7 * f + (e - 1))
            acc = b[f"acc{uf}"][:, :, :]
            g.tensor_tensor(acc, acc, b[f"g{e % 2}"][:, :, :], ALU.add).then_inc(s["acc"], 1)

        def body(pool, ur, ua, r=None, a=None, f=None, t=None):
            c = b["c"]
            uf = ur
            if r is not None:
                pool.wait_ge(self.contrib_loaded, 16 * r + 16)
                g.tensor_tensor(c[:, :, 0:512], c[:, :, 0:512], c[:, :, 512:1024], ALU.add).then_inc(s["sum_step"], 1)
            if f is not None:
                add_expert(f, uf, 1)
            if t is not None:
                rstd("f", t + 1, "rf_step", t + 1, "rs_f")
            if r is not None:
                pool.wait_ge(s["sum_step"], 3 * r + 1)
                g.tensor_tensor(c[:, :, 0:256], c[:, :, 0:256], c[:, :, 256:512], ALU.add).then_inc(s["sum_step"], 1)
                pool.wait_ge(s["sum_step"], 3 * r + 2)
                yv = b["y"][:, :].rearrange("p (j d) -> p j d", d=D)
                g.tensor_tensor(yv, c[:, :, 0:128], c[:, :, 128:256], ALU.add).then_inc(s["sum_step"], 1)
            if f is not None:
                add_expert(f, uf, 2)
            if r is not None:
                pool.wait_ge(s["sum_step"], 3 * r + 3)
                bs = self.base_all[:, r, :] if isinstance(r, int) else self.base_all[:, bass.ds(r, 1), :].rearrange("p o d -> p (o d)")
                g.tensor_tensor(b["y"][:, :], b["y"][:, :], bs, ALU.add).then_inc(s["y"], 1)
            if f is not None:
                add_expert(f, uf, 3)
            if r is not None:
                n = r + 1
                rstd("r", n, "rz_step", 7 * r + 1, "rz_step")
                y3d = b["y"][:, :].rearrange("p (j d) -> p j d", d=D)
                mv = b["mv_r"][:, :].rearrange("p (j t) -> p j t", t=2)
                var = mv[:, :, 1]
                g.tensor_tensor(y3d, y3d, bcast_last(mv[:, :, 0], D), ALU.subtract).then_inc(s["rz_step"], 1)
                pool.wait_ge(s["rz_step"], 7 * r + 3)
                x2 = b[f"x2{ur}"][:, :].rearrange("p (j d) -> p j d", d=D)
                g.tensor_tensor(x2, y3d, bcast_last(b["rs_r"][:, :], D), ALU.mult).then_inc(s["x2"], 1)
                if not first(r):
                    pool.wait_ge(s["z"], r)
                g.tensor_tensor(b["rq"][:, :], b["rs_r"][:, :], b["rs_r"][:, :], ALU.mult).then_inc(s["rz_step"], 1)
                pool.wait_ge(s["rz_step"], 7 * r + 4)
                g.tensor_tensor(b["rq"][:, :], b["rq"][:, :], var, ALU.mult).then_inc(s["rz_step"], 1)
                pool.wait_ge(s["rz_step"], 7 * r + 5)
                g.tensor_tensor(b["rq"][:, :], b["rq"][:, :], k["eps"][:, :], ALU.add).then_inc(s["rz_step"], 1)
                pool.wait_ge(s["rz_step"], 7 * r + 6)
                g.tensor_tensor(b["rq"][:, :], b["rq"][:, :], k["mhalf"][:, :], ALU.pow).then_inc(s["rz_step"], 1)
            if a is not None:
                rstd("a", a + 1, "rs_step", a + 1, "rs_a")
            if f is not None:
                add_expert(f, uf, 4)
                add_expert(f, uf, 5)
                add_expert(f, uf, 6)
                add_expert(f, uf, 7)

        self.bodies(pool, body)

    def act(self, act):
        a_, b, s, k, bank = self.nc.scalar, self.b, self.s, self.k, self.bank
        cols, SIG = k["cols"], ACT.Sigmoid
        X, Y, Z = bank[5], bank[6], bank[7]

        for q in range(8):
            act.wait_ge(s["w1_mm"], q + 1)
            a_.copy(b["w1_hi"][:, q, :], bank[q % 4][:, :]).then_inc(s["w1_hi"], 1)

        def gate(a, step, src, bias=None):
            if step >= 2:
                act.wait_ge(s["prod5"], 5 * a + (step - 1))
            kw = {} if bias is None else {"bias": bias}
            a_.activation(b[f"sgt{step % 2}"][:, :], src[:, :], SIG, **kw).then_inc(s["sig5"], 1)

        def sig(f, kk):
            e, h = divmod(kk, 2)
            act.wait_ge(s["b_mm"], 16 * f + (kk + 1))
            if kk >= 2 or not first(f):
                act.wait_ge(s["g"], 16 * f + (kk - 1))
            col = 21 + 4 * e + 2 + h
            a_.activation(b[f"sg{kk % 2}"][:, :], bank[2 * (kk % 2)][:, :], SIG, bias=cols[:, col:col + 1]).then_inc(s["sig"], 1)

        def body(act, ur, ua, r=None, a=None, f=None, t=None):
            uf = ur
            for q in range(2 * E1):
                if f is not None:
                    sig(f, q)
                if f is not None and q == 2:
                    act.wait_ge(s["combT_mm"], f + 1)
                    a_.copy(b[f"combT{uf}"][:, :], Z[0:16, :]).then_inc(s["combT"], 1)
                if a is not None:
                    if q == AT["zT"]:
                        act.wait_ge(s["zT_mm"], a + 1)
                        a_.copy(b["zh"][:, :], X[:, :]).then_inc(s["zh"], 1)
                    if q == AT["gate"]:
                        act.wait_ge(s["gate_mm"], 3 * a + 1)
                        gate(a, 0, X, k["bcols"][:, 0:1])
                        act.wait_ge(s["gate_mm"], 3 * a + 2)
                        gate(a, 1, Z, k["bcols"][:, 2:3])
                    if q == AT["v"]:
                        act.wait_ge(s["v_mm"], 2 * a + 1)
                        gate(a, 3, Z)
                        act.wait_ge(s["v_mm"], 2 * a + 2)
                        gate(a, 4, Y)
                    if q == AT["quads"]:
                        act.wait_ge(s["prod5"], 5 * a + 2)
                        for n, w, o in (("qq", k["quadw"][:, 0:1], k["quadb"][:, 0:1]), ("lq", k["quadw"][:, 1:2], k["quadb"][:, 1:2]),
                                        ("qk", cols[:, 7:8], cols[:, 11:12]), ("lk", cols[:, 8:9], cols[:, 12:13])):
                            ins = a_.activation(b[n][:, :], b["qkT"][:, :], ACT.Identity, scale=w, bias=o)
                        ins.then_inc(s["quads"], 1)
                    if q == AT["gate2"]:
                        act.wait_ge(s["gate_mm"], 3 * a + 3)
                        gate(a, 2, X, k["bcols"][:, 1:2])
                    if q == AT["sim"]:
                        act.wait_ge(s["off_mm"], 2 * a + 1)
                        a_.copy(b["off1"][:, :], Z[:, :])
                    if q == AT["off"]:
                        act.wait_ge(s["off_mm"], 2 * a + 2)
                        a_.copy(b["off2"][:, :], X[:, 0:256]).then_inc(s["off2"], 1)
                    if q == AT["x3T"]:
                        act.wait_ge(s["x3T_mm"], a + 1)
                        a_.copy(b[f"x3h{ua}"][:, :], Y[:, :]).then_inc(s["x3h"], 1)
                    if q == AT["lg"] + 1:
                        act.wait_ge(s["gate_step"], GATE_STEPS * a + 3)
                        a_.activation(b["s1"][:, :], b["dif"][:, :], SIG)
                        a_.activation(b["s2"][:, :], b["dif"][:, :], SIG, scale=-1.0).then_inc(s["sig_d"], 1)
                if r is not None and q == AT["z"]:
                    act.wait_ge(s["rz_step"], 7 * r + 7)
                    act.wait_ge(s["x2"], r + 1)
                    for j in range(NT):
                        c = slice(j * D, (j + 1) * D)
                        ins = a_.activation(b[f"z{ur}"][:, c], b[f"x2{ur}"][:, c], ACT.Identity, scale=b["rq"][:, j:j + 1])
                    ins.then_inc(s["z"], 1)

        self.bodies(act, body)

    def dve(self, dve):
        v, b, s, k, bank = self.nc.vector, self.b, self.s, self.k, self.bank
        cols = k["cols"]
        X, Y, Z = bank[5], bank[6], bank[7]

        for q in range(8):
            dve.wait_ge(s["w1_hi"], q + 1)
            v.tensor_tensor(b["w1_lo"][:, q, :], bank[q % 4][:, :], b["w1_hi"][:, q, :].bitcast(F32), ALU.subtract).then_inc(s["w1_lo"], 1)
        for u in range(2):
            v.memset(self.landing(), 0.0).then_inc(self.out_stored[u], 16)
        dve.wait_ge(self.setup_pool, self.pool_done)

        def stats(name, src, n):
            st = b["st_" + name][:, :].rearrange("p (j t) -> p j t", t=6)
            mv = b["mv_" + name][:, :].rearrange("p (j t) -> p j t", t=2)
            for j in range(NT):
                ins = v.bn_stats(st[:, j, :], src[:, j * D:(j + 1) * D])
            ins.then_inc(s["st_" + name], 1)
            dve.wait_ge(s["st_" + name], n)
            v.memset(self.landing(), 0.0)
            for j in range(NT):
                ins = v.bn_aggr(mv[:, j, :], st[:, j, :])
            ins.then_inc(s["mv_" + name], 1)

        def norm(name, dst, src, rs, done):
            mv = b["mv_" + name][:, :].rearrange("p (j t) -> p j t", t=2)
            for j in range(NT):
                ins = v.tensor_scalar(dst[:, j * D:(j + 1) * D], src[:, j * D:(j + 1) * D], mv[:, j, 0:1], rs[:, j:j + 1], ALU.subtract, ALU.mult)
            if done is not None:
                ins.then_inc(done, 1)

        def prod(a, step, src, dst, bias=None):
            dve.wait_ge(s["sig5"], 5 * a + (step + 1))
            sg = b[f"sgt{step % 2}"][:, :]
            if bias is None:
                v.tensor_tensor(dst, src[:, :], sg, ALU.mult).then_inc(s["prod5"], 1)
            else:
                v.scalar_tensor_tensor(out=dst, in0=src[:, :], scalar=bias, in1=sg, op0=ALU.add, op1=ALU.mult).then_inc(s["prod5"], 1)

        def half(f, kk):
            e, h = divmod(kk, 2)
            dve.wait_ge(s["sig"], 16 * f + (kk + 1))
            dve.wait_ge(s["a_mm"], 16 * f + (kk + 1))
            if h == 0 and e >= 3:
                dve.wait_ge(s["acc"], 7 * f + (e - 2))
            if h == 0 and e < 2 and not first(f):
                dve.wait_ge(s["acc"], 7 * f + (e - 1))
            col = 21 + 4 * e + h
            v.scalar_tensor_tensor(out=b[f"g{e % 2}"][:, h, :], in0=bank[2 * (kk % 2) + 1][:, :], scalar=cols[:, col:col + 1],
                                   in1=b[f"sg{kk % 2}"][:, :], op0=ALU.add, op1=ALU.mult).then_inc(s["g"], 1)

        def weigh(f, uf, e):
            dve.wait_ge(s["g"], 16 * f + (2 * e + 2))
            dve.wait_ge(s["cb_mm"], 8 * f + (e + 1))
            dst = b[f"acc{uf}"] if e == 0 else b[f"g{e % 2}"]
            v.tensor_tensor(dst[:, :, :], b[f"g{e % 2}"][:, :, :], bcast_mid(bank[4][:, :], 2), ALU.mult).then_inc(s["gc"], 1)

        def gating(a, step):
            def t3(n):
                return b[n][:, :].rearrange("p (j e) -> p j e", e=E1)

            if step == 0:
                dve.wait_ge(s["lg_mm"], a + 1)
                v.tensor_copy(b["lgs"][:, :], Z[:, 0:NT * E1]).then_inc(s["gate_step"], 1)
                return
            dve.wait_ge(s["gate_step"], GATE_STEPS * a + step)
            if step == 1:
                v.memset(self.landing(), 0.0)
                for j in range(NT):
                    ins = v.max(t3("top")[:, j, :], t3("lgs")[:, j, :])
            elif step == 2:
                ins = v.tensor_tensor(t3("dif"), t3("lgs"), bcast_last(t3("top")[:, :, 0], E1), ALU.subtract)
            elif step == 3:
                ins = v.memset(t3("top")[:, :, 2:E1], STRUCK)
            elif step == 4:
                v.memset(self.landing(), 0.0)
                for j in range(NT):
                    ins = v.match_replace(t3("zap")[:, j, :], t3("top")[:, j, :], t3("lgs")[:, j, :], NEG)
            elif step == 5:
                ins = v.tensor_tensor(b["mask"][:, :], b["zap"][:, :], b["lgs"][:, :], ALU.not_equal)
            elif step == 6:
                dve.wait_ge(s["sig_d"], a + 1)
                ins = v.reciprocal(b["s2"][:, :], b["s2"][:, :])
            elif step == 7:
                ins = v.tensor_tensor(b["s1"][:, :], b["s1"][:, :], b["s2"][:, :], ALU.mult)
            elif step == 8:
                v.tensor_reduce(b["zsum"][:, :], t3("s1"), AX.X, ALU.add)
                ins = v.tensor_tensor(b["em"][:, :], b["s1"][:, :], b["mask"][:, :], ALU.mult)
            elif step == 9:
                ins = v.tensor_reduce(b["esum"][:, :], t3("em"), AX.X, ALU.add)
            elif step == 10:
                ins = v.scalar_tensor_tensor(out=b["den"][:, :], in0=b["zsum"][:, :], scalar=1e-9, in1=b["esum"][:, :], op0=ALU.mult, op1=ALU.add)
            elif step == 11:
                ins = v.reciprocal(b["den"][:, :], b["den"][:, :])
            elif step == 12:
                ins = v.tensor_tensor(t3("comb"), t3("em"), bcast_last(b["den"][:, :], E1), ALU.mult)
            elif step == 13:
                ins = v.tensor_copy(b["chr"][:, :], b["comb"][:, :])
            elif step == 14:
                ch = b["ch"][:, :].rearrange("p (j e) -> p j e", e=16)
                v.tensor_copy(ch[:, :, 0:E1], t3("chr").bitcast(F32))
                ins = v.tensor_tensor(ch[:, :, E1:16], t3("comb"), t3("chr").bitcast(F32), ALU.subtract)
            ins.then_inc(s["gate_step"], 1)

        def body(dve, ur, ua, r=None, a=None, f=None, t=None):
            uf = ur
            for q in range(2 * E1):
                gates = list(GATING.get(q, ())) if a is not None else []
                if gates:
                    gating(a, gates.pop(0))
                if f is not None:
                    before, after = GATING_NEXT.get(q, ((), ()))
                    for step in before:
                        gating(f, step)
                    half(f, q)
                    for step in after:
                        gating(f, step)
                if a is not None and q == AT["x3"]:
                    dve.wait_ge(s["rs_a"], a + 1)
                    norm("a", b[f"x3{ua}"], b["y3"], b["rs_a"], s["x3"])
                if gates:
                    gating(a, gates.pop(0))
                if f is not None and q in WEIGH:
                    weigh(f, uf, WEIGH[q])
                for step in gates:
                    gating(a, step)
                if t is not None:
                    if q == AT["y4"]:
                        dve.wait_ge(s["out_mm"], t + 1)
                        v.tensor_tensor(b["y4"][:, :], b[f"x3{ua}"][:, :], Y[:, :], ALU.add).then_inc(s["y4"], 1)
                        dve.wait_ge(s["y4"], t + 1)
                        v.memset(self.landing(), 0.0)
                        stats("f", b["y4"], t + 1)
                    if q == AT["outb"]:
                        dve.wait_ge(s["rs_f"], t + 1)
                        dve.wait_ge(self.out_stored[ua], 8 * (t - ua) + 16)
                        norm("f", b[f"outb{ua}"], b["y4"], b["rs_f"], s["outb"])
                if a is not None:
                    if q == AT["zT"]:
                        dve.wait_ge(s["zh"], a + 1)
                        v.tensor_tensor(b["zl"][:, :], X[:, :], b["zh"][:, :].bitcast(F32), ALU.subtract).then_inc(s["zl"], 1)
                    if q == AT["gate"]:
                        prod(a, 0, X, b["gateT"][:, 0, :], k["bcols"][:, 0:1])
                        prod(a, 1, Z, b["qkT"][:, :], k["bcols"][:, 2:3])
                    if q == AT["v"]:
                        prod(a, 3, Z, b["v"][:, 2:4, :].rearrange("p j e -> p (j e)"))
                        prod(a, 4, Y, b["v"][:, 0:2, :].rearrange("p j e -> p (j e)"))
                    if q == AT["gate2"]:
                        prod(a, 2, X, b["gateT"][:, 1, :], k["bcols"][:, 1:2])
                    if q == AT["sim"]:
                        dve.wait_ge(s["diag_mm"], a + 1)
                        t_, ml = b["t"][:, :, :], b["ml"][:, :, :]
                        v.tensor_tensor(t_, X[:, :].rearrange("p (j i) -> p j i", i=P), bcast_mid(k["biasT"][:, :], NT), ALU.add).then_inc(s["t1"], 1)
                        v.tensor_tensor(ml, Y[:, :].rearrange("p (j i) -> p j i", i=P), bcast_mid(k["ltmask"][:, :], NT), ALU.mult)
                        dve.wait_ge(s["t1"], a + 1)
                        v.scalar_tensor_tensor(out=t_, in0=t_, scalar=0.0, in1=t_, op0=ALU.max, op1=ALU.mult).then_inc(s["t2"], 1)
                        dve.wait_ge(s["t2"], a + 1)
                        v.tensor_tensor(t_, t_, ml, ALU.add).then_inc(s["atd"], 1)
                    if q == AT["av"]:
                        for h, src in ((0, Y), (1, Z)):
                            dve.wait_ge(s["av_mm"], 2 * a + (h + 1))
                            v.tensor_tensor(b["goT"][:, h, :], src[:, :], b["gateT"][:, h, :], ALU.mult).then_inc(s["go"], 1)
                    if q == AT["w"]:
                        dve.wait_ge(s["w_mm"], a + 1)
                        v.scalar_tensor_tensor(out=b["y3"][:, :], in0=b[f"x2{ua}"][:, :], scalar=2.0, in1=X[:, :], op0=ALU.mult, op1=ALU.add).then_inc(s["y3"], 1)
                        dve.wait_ge(s["y3"], a + 1)
                        v.memset(self.landing(), 0.0)
                        stats("a", b["y3"], a + 1)
                    if q == AT["x3T"]:
                        dve.wait_ge(s["x3h"], a + 1)
                        v.tensor_tensor(b[f"x3l{ua}"][:, :], Y[:, :], b[f"x3h{ua}"][:, :].bitcast(F32), ALU.subtract).then_inc(s["x3l"], 1)
                if r is not None and q == AT["y"]:
                    dve.wait_ge(s["y"], r + 1)
                    v.memset(self.landing(), 0.0)
                    stats("r", b["y"], r + 1)
        self.bodies(dve, body)

    def pe(self, pe):
        t, b, s, k, bank = self.nc.tensor, self.b, self.s, self.k, self.bank
        X, Y, Z = bank[5], bank[6], bank[7]
        ident = self.ident

        def split3(dst, w_hi, w_lo, x_hi, x_lo, start=True, stop=True):
            t.matmul(dst, w_hi, x_hi, start=start, stop=False)
            t.matmul(dst, w_hi, x_lo, start=False, stop=False)
            return t.matmul(dst, w_lo, x_hi, start=False, stop=stop)

        pe.wait_ge(self.y_sb, EP)
        for q in range(8):
            if q % 2 == 0:
                pe.wait_ge(self.w1_loaded[(q // 2) % 2], 16 * (q // 4 + 1))
            if q >= 4:
                pe.wait_ge(s["w1_lo"], q - 3)
            src = b[f"g{(q // 2) % 2}"][:, :, :].rearrange("p h l -> p (h l)")
            for c in range(4):
                o = ((q % 2) * 4 + c) * D
                ins = t.transpose(bank[q % 4][:, c * P:(c + 1) * P], src[:, o:o + D], ident[:, :])
            ins.then_inc(s["w1_mm"], 1)
        pe.wait_ge(s["w1_lo"], 8)
        pe.wait_ge(self.setup_pool, self.pool_done)

        def up(f, uf, kk):
            e, h = divmod(kk, 2)
            xh, xl = b[f"x3h{uf}"][:, :], b[f"x3l{uf}"][:, :]
            for part, o, done in (("b", H1, "b_mm"), ("a", 0, "a_mm")):
                if kk >= 2 or not first(f):
                    pe.wait_ge(s["sig" if part == "b" else "g"], 16 * f + (kk - 1))
                w = slice(o + h * P, o + (h + 1) * P)
                split3(bank[2 * (kk % 2) + (part == "a")][:, :], b["w1_hi"][:, e, w], b["w1_lo"][:, e, w], xh, xl).then_inc(s[done], 1)

        def spread(f, uf, e):
            if e == 0:
                pe.wait_ge(s["combT"], f + 1)
            if e > 0 or not first(f):
                pe.wait_ge(s["gc"], 8 * f + e)
            t.matmul(bank[4][:, :], k["sel"][:, e, :], b[f"combT{uf}"][:, :], start=True, stop=True).then_inc(s["cb_mm"], 1)

        def body(pe, ur, ua, r=None, a=None, f=None, t=None):
            t_, t = t, self.nc.tensor
            uf = ur
            zh, zl = b["zh"], b["zl"]
            hi, lo = k["wh_hi"], k["wh_lo"]
            for q in range(2 * E1):
                if f is not None:
                    up(f, uf, q)
                if a is not None and q == AT["zT"]:
                    pe.wait_ge(s["z"], a + 1)
                    for j in range(NT):
                        ins = t.transpose(X[:, j * P:(j + 1) * P], b[f"z{ua}"][:, j * D:(j + 1) * D], ident[:, :])
                    ins.then_inc(s["zT_mm"], 1)
                if f is not None and q == 2:
                    pe.wait_ge(s["gate_step"], GATE_STEPS * f + GATE_STEPS)
                    for j in range(NT):
                        ins = t.transpose(Z[0:16, j * P:(j + 1) * P], b["ch"][:, j * 16:(j + 1) * 16], ident[:, :])
                    ins.then_inc(s["combT_mm"], 1)
                if a is not None and q == AT["gate"]:
                    pe.wait_ge(s["zl"], a + 1)
                    split3(X[:, :], hi[:, HID:HID + P], lo[:, HID:HID + P], zh[:, :], zl[:, :]).then_inc(s["gate_mm"], 1)
                if f is not None and q in WEIGH:
                    spread(f, uf, WEIGH[q])
                if a is not None and q == AT["gate"]:
                    split3(Z[:, :], hi[:, 2 * HID:], lo[:, 2 * HID:], zh[:, :], zl[:, :]).then_inc(s["gate_mm"], 1)
                if t_ is not None and q == AT["out"]:
                    pe.wait_ge(s["acc"], 7 * t_ + 7)
                    cb, acc = b[f"combT{ua}"], b[f"acc{ua}"]
                    for j in range(NT):
                        tok = slice(j * P, (j + 1) * P)
                        dst = Y[:, j * D:(j + 1) * D]
                        t.matmul(dst, cb[:, tok], k["bo_hi"][:, :], start=True, stop=False)
                        t.matmul(dst, cb[:, tok], k["bo_lo"][:, :], start=False, stop=False)
                        t.matmul(dst, acc[:, 0, tok], k["woT"][:, 0, :], start=False, stop=False)
                        ins = t.matmul(dst, acc[:, 1, tok], k["woT"][:, 1, :], start=False, stop=True)
                    ins.then_inc(s["out_mm"], 1)
                if a is not None:
                    if q == AT["v"]:
                        pe.wait_ge(s["prod5"], 5 * a + 2)
                        for j in (2, 3, 0, 1):
                            if j == 0 and t_ is not None:
                                pe.wait_ge(s["y4"], t_ + 1)
                            dst = (Y, Z)[j // 2][:, (j % 2) * HID:(j % 2 + 1) * HID]
                            tok = slice(j * P, (j + 1) * P)
                            t.matmul(dst, k["ones"][:, :], k["vb_hi"][:, :], start=True, stop=False)
                            t.matmul(dst, k["ones"][:, :], k["vb_lo"][:, :], start=False, stop=False)
                            ins = split3(dst, zh[:, tok], zl[:, tok], hi[:, 0:HID], lo[:, 0:HID], start=False)
                            if j % 2:
                                ins.then_inc(s["v_mm"], 1)
                    if q == AT["gate2"]:
                        pe.wait_ge(s["prod5"], 5 * a + 1)
                        split3(X[:, :], hi[:, HID + P:2 * HID], lo[:, HID + P:2 * HID], zh[:, :], zl[:, :]).then_inc(s["gate_mm"], 1)
                    if q == AT["sim"]:
                        pe.wait_ge(s["quads"], a + 1)
                        pe.wait_ge(s["prod5"], 5 * a + 5)
                        for j in range(NT):
                            tok = slice(j * P, (j + 1) * P)
                            t.matmul(X[:, tok], b["qk"][:, tok], b["qq"][:, tok], start=True, stop=True)
                            ins = t.matmul(Y[:, tok], b["lk"][:, tok], b["lq"][:, tok], start=True, stop=True)
                        ins.then_inc(s["diag_mm"], 1)
                        t.matmul(Z[:, 0:384], b["lk"][:, 0:P], b["lq"][:, P:L], start=True, stop=True)
                        t.matmul(Z[:, 384:512], b["lk"][:, 2 * P:3 * P], b["lq"][:, 3 * P:L], start=True, stop=True).then_inc(s["off_mm"], 1)
                    if q == AT["off"]:
                        pe.wait_ge(s["t1"], a + 1)
                        t.matmul(X[:, 0:256], b["lk"][:, P:2 * P], b["lq"][:, 2 * P:L], start=True, stop=True).then_inc(s["off_mm"], 1)
                    if q == AT["av"]:
                        pe.wait_ge(s["atd"], a + 1)
                        pe.wait_ge(s["off2"], a + 1)
                        for h, dst in ((0, Y), (1, Z)):
                            c = slice(h * P, (h + 1) * P)
                            t.matmul(dst[:, P:L], b["v"][:, 0, c], b["off1"][:, 0:384], start=True, stop=False, skip_group_check=True)
                            t.matmul(dst[:, 0:P], b["v"][:, 0, c], b["t"][:, 0, :], start=False, stop=False, skip_group_check=True)
                            t.matmul(dst[:, 2 * P:L], b["v"][:, 1, c], b["off2"][:, 0:256], start=False, stop=False, skip_group_check=True)
                            t.matmul(dst[:, 3 * P:L], b["v"][:, 2, c], b["off1"][:, 384:512], start=False, stop=False, skip_group_check=True)
                            for j in range(1, NT):
                                ins = t.matmul(dst[:, j * P:(j + 1) * P], b["v"][:, j, c], b["t"][:, j, :], start=False, stop=(j == NT - 1), skip_group_check=True)
                            ins.then_inc(s["av_mm"], 1)
                    if q == AT["w"]:
                        t.matmul(X[:, :], k["ones"][:, :], k["bout_hi"][:, :], start=True, stop=False, skip_group_check=True)
                        t.matmul(X[:, :], k["ones"][:, :], k["bout_lo"][:, :], start=False, stop=False, skip_group_check=True)
                        pe.wait_ge(s["go"], 2 * a + 2)
                        for j in range(NT):
                            for h in range(2):
                                ins = t.matmul(X[:, j * D:(j + 1) * D], b["goT"][:, h, j * P:(j + 1) * P], k["wout"][:, h, :],
                                               start=False, stop=(h == 1), skip_group_check=True)
                        ins.then_inc(s["w_mm"], 1)
                    if q == AT["x3T"]:
                        pe.wait_ge(s["x3"], a + 1)
                        for j in range(NT):
                            ins = t.transpose(Y[:, j * P:(j + 1) * P], b[f"x3{ua}"][:, j * D:(j + 1) * D], ident[:, :])
                        ins.then_inc(s["x3T_mm"], 1)
                    if q == AT["lg"]:
                        pe.wait_ge(s["x3l"], a + 1)
                        xh, xl = b[f"x3h{ua}"], b[f"x3l{ua}"]
                        for j in range(NT):
                            tok = slice(j * P, (j + 1) * P)
                            ins = split3(Z[:, j * E1:(j + 1) * E1], xh[:, tok], xl[:, tok], k["wg_hi"][:, :], k["wg_lo"][:, :])
                        ins.then_inc(s["lg_mm"], 1)

        self.bodies(pe, body)


def build(nc, x_in, Wq, Wm, W1, W2, g1, b1, g2, b2, router_w, w_gate, w_up, w_down, ws_gate_up, ws_down,
          ln_w, ln_b, Wh, bh, Wqk, bqk, qk_w, qk_b, rel_table, Wout, bout, Wg, W1e, b1e, Wo, bo, out):
    ctx = ExitStack()
    with ctx:
        def scope():
            return ExitStack()

        def sb(name, shape, dt=F32, where=ctx):
            return where.enter_context(nc.sbuf_tensor(name, shape, dt))

        def sem(name):
            return ctx.enter_context(nc.semaphore(name))

        table = nc.dram_tensor("token_rows", (T + 1, ROW), F32, kind="Internal").ap()
        contrib = nc.dram_tensor("routed_rows", (NKEY, D), F32, kind="Internal").ap()

        ident = sb("ident", [P, P])
        base_all = sb("base_all", [P, B, NT * D])
        landing_all = sb("landing", [P, 96])
        cells = iter(range(96))

        def landing():
            c = next(cells)
            return landing_all[:, c:c + 1]

        C = StageC(nc, sb, sem, None)
        AB = scope()
        x1T_all = sb("x1T_all", [P, T], where=AB)
        y_all = x1T_all
        rows_all = sb("rows_all", [P, EP * ROW], where=AB)
        ZCOLS = 4096
        zeros = rows_all[:, 0:ZCOLS]
        keyT = sb("keyT", [P, T // 2], where=AB)
        cand = sb("cand", [P, CAP], where=AB)
        both = sb("both", [E0, 2 * CAP], where=AB)
        slot_key = sb("slot_key", [E0, CAP], where=AB)
        dest_f = sb("dest_f", [P, EP], where=AB)
        dest_row = sb("dest_row", [P, EP], U32, where=AB)
        tok_row = sb("tok_row", [P, EP], U32, where=AB)
        wgu_e = sb("wgu_early", [P, 2 * EP_EARLY, 2, F0], where=AB)
        wd_e = sb("wd_early", [F0, 2 * EP_EARLY, D], where=AB)
        wsgu_sb = sb("wsgu_sb", [P, 2 * F0], where=AB)
        wsd_sb = sb("wsd_sb", [F0, D], where=AB)
        xgT = [sb(f"xgT{b}", [P, P], where=AB) for b in range(2)]
        sil = [sb(f"sil{b}", [F0, P], where=AB) for b in range(2)]
        hexp = [sb(f"hexp{b}", [F0, P], where=AB) for b in range(2)]
        A = scope()
        Wq_sb = sb("Wq_sb", [P, D], where=A)
        Wm_sb = sb("Wm_sb", [P, D], where=A)
        W1_sb = sb("W1_sb", [P, 2 * D], where=A)
        W2_sb = sb("W2_sb", [P, 2, D], where=A)
        rw_sb = sb("rw_sb", [E0, D], where=A)
        rwT = sb("rwT", [P, E0], where=A)
        g1_bc = sb("g1_bc", [P, D], where=A)
        g2_bc = sb("g2_bc", [P, D], where=A)
        b12_bc = sb("b12_bc", [P, 2, D], where=A)
        headmask = sb("headmask", [P, D + H0], where=A)
        reset = sb("reset", [P, NT * E0], where=A)
        mhalf = sb("mhalf", [P, 2 * NT], where=A)
        epsc = sb("epsc", [P, 2 * NT], where=A)
        keyc = [sb(f"keyc{u}", [P, NT * E0], where=A) for u in range(2)]
        keys = sb("keys", [P, NT, 2, E0], where=A)
        S = []
        for u in range(2):
            s = {}
            for name, cols in dict(x=NT * D, xT=L, feat=NT * D, e=NT * D, featT=L, hT=2 * L, r=NT * D,
                                   lg=NT * E0, zap=NT * E0, mask=NT * E0, ex=NT * E0, incl=NT * E0,
                                   stats=12 * NT, mv=4 * NT, rstd=2 * NT, stats3=6 * NT, mv3=2 * NT, rstd3=NT,
                                   z=NT * H0, kvm=D + H0, top=NT * 8, esum=NT, q=NT * (D + 4), xw=NT * ROW).items():
                s[name] = sb(f"{name}_{u}", [P, cols], where=A)
            s["x1T"] = s["hT"][:, 0:L]
            s["msg"], s["msgT"], s["m2T"], s["a1"], s["a2"] = s["e"], s["xT"], s["featT"], s["feat"], s["e"]
            S.append(s)
        A.close()
        late = scope()
        wgu_l = sb("wgu_late", [P, 2 * (EP - EP_EARLY), 2, F0], where=late)
        wd_l = sb("wd_late", [F0, 2 * (EP - EP_EARLY), D], where=late)
        late.close()
        AB.close()
        C.buffers(sb)

        bank = [ctx.enter_context(nc.psum_tensor(f"bank{k}", [P, 512], F32)) for k in range(8)]

        names = """consts_ready weights_ready zero_tile zeros_written xT_mm xT_sb q_mm negq eq feat_sb featT_mm kv_mm featT_sb kvm_sb
        num_mm z_step msg_sb msgT_mm msgT_sb m2T_mm m2T_sb hT_mm hT1_sb mlp_mm st1 mv1 var_eps rstd1
        xr1 xr2 centred r_step st3 mv3 rstd3 x1_sb x1T_mm x1T_sb x1T_kept lg_mm lg_sb pick_step soft_step
        d_sb ex_sb w_sb incl_sb ka_sb key_sb keyT_mm keyT_sb rwT_mm rwT_sb pool_setup late_weights early_weights
        round_done slots_sb slotT_mm slot_index sg_mm su_sb sh_sb ysh_mm ysh_sb base_sb
        xgT_mm xgT_sb gu_mm sil_sb hexp_sb y_mm y_sb rows_scattered""".split()
        s_ = {n: sem(n) for n in names}
        x_loaded = [sem(f"x_loaded{u}") for u in range(2)]
        xw_stored = [sem(f"xw_stored{u}") for u in range(2)]
        gathered = [sem(f"gathered{m}") for m in range(8)]

        x_view = x_in.rearrange("b (j p) d -> b p j d", p=P)
        table_view = table[0:T, :].rearrange("(b j p) r -> b p j r", j=NT, p=P)
        zero_view = contrib.rearrange("(n p f) d -> n p (f d)", p=P, f=ZCOLS // D)
        NZ = NKEY * D // (P * ZCOLS)

        def tiles(ap, w=D):
            return ap.rearrange("p (j d) -> p j d", d=w)

        def carve(k, cols, parts=P):
            return rows_all[0:parts, k * 512:k * 512 + cols]
        x1s = [carve(5 * u, 512) for u in range(2)]
        sgs = [carve(1 + 5 * u, 512, F0) for u in range(2)]
        sus = [carve(2 + 5 * u, 512, F0) for u in range(2)]
        shs = [carve(3 + 5 * u, 512, F0) for u in range(2)]
        yss = [carve(4 + 5 * u, 512) for u in range(2)]

        def late_early(pair):
            if pair < EP_EARLY:
                return wgu_e[:, 2 * pair:2 * pair + 2], wd_e[:, 2 * pair:2 * pair + 2]
            k = 2 * (pair - EP_EARLY)
            return wgu_l[:, k:k + 2], wd_l[:, k:k + 2]

        def expert_silu(act, m):
            act.wait_ge(s_["gu_mm"], m + 1)
            if m >= 2:
                act.wait_ge(s_["hexp_sb"], m - 1)
            nc.scalar.activation(sil[m % 2][:, :], bank[2 + m % 2][0:F0, 0:P], ACT.Silu).then_inc(s_["sil_sb"], 1)

        def expert_weigh(dve, m):
            dve.wait_ge(s_["y_mm"], m + 1)
            for h in range(2):
                part = slice(h * CAP, (h + 1) * CAP)
                w = rows_all[part, m * ROW + D + 2 * m + h:m * ROW + D + 2 * m + h + 1]
                ins = nc.vector.tensor_scalar(y_all[part, m * D:(m + 1) * D], bank[4 + m % 2][part, 0:D], w, None, ALU.mult)
            ins.then_inc(s_["y_sb"], 1)

        def expert_up(pe, m):
            wgu, _ = late_early(m)
            pe.wait_ge(s_["xgT_sb"], m + 1)
            if m >= 2:
                pe.wait_ge(s_["hexp_sb"], m - 1)
            for gu in range(2):
                for h in range(2):
                    ins = nc.tensor.matmul(bank[2 + m % 2][0:F0, gu * P + h * CAP:gu * P + (h + 1) * CAP], wgu[:, h, gu, :],
                                           xgT[m % 2][:, h * CAP:(h + 1) * CAP], start=True, stop=True)
            ins.then_inc(s_["gu_mm"], 1)

        def expert_down(pe, m):
            _, wd = late_early(m)
            pe.wait_ge(s_["hexp_sb"], m + 1)
            if m >= 2:
                pe.wait_ge(s_["y_sb"], m - 1)
            for h in range(2):
                ins = nc.tensor.matmul(bank[4 + m % 2][h * CAP:(h + 1) * CAP, 0:D], hexp[m % 2][:, h * CAP:(h + 1) * CAP], wd[:, h, :],
                                       start=True, stop=True)
            ins.then_inc(s_["y_mm"], 1)

        C.bank, C.ident, C.landing, C.base_all = bank, ident, landing, base_all
        C.rows_scattered, C.y_sb = s_["rows_scattered"], s_["y_sb"]
        C.skew = nc.dram_tensor("bias_rows", (G, 2 * G - 1), F32, kind="Internal").ap()
        C.contrib_view = contrib.rearrange("(b j p k) d -> b p j (k d)", j=NT, p=P, k=K0N)
        C.out_view = out.rearrange("b (j p) d -> b p j d", p=P)
        C.inputs = dict(Wq=Wq, ln_w=ln_w, ln_b=ln_b, Wh=Wh, bh=bh, Wqk=Wqk, bqk=bqk, qk_w=qk_w, qk_b=qk_b, rel_table=rel_table,
                        Wout=Wout, bout=bout, Wg=Wg, W1e=W1e, b1e=b1e, Wo=Wo, bo=bo)

        block = ctx.enter_context(nc.Block())


        @block.gpsimd
        def _(pool):
            g = nc.gpsimd
            count = [0]

            def chain(ins):
                count[0] += 1
                ins.then_inc(s_["pool_setup"], 1)
                pool.wait_ge(s_["pool_setup"], count[0])

            chain(g.memset(ident[:, :], 0.0))
            g.affine_select(out=ident[:, :], in_=ident[:, :], compare_op=ALU.not_equal, fill=1.0, base=0,
                            pattern=[[-1, P]], channel_multiplier=1).then_inc(s_["consts_ready"], 1)
            g.memset(zeros, 0.0).then_inc(s_["zero_tile"], 1)
            chain(g.memset(headmask[:, :], 1.0))
            hm = headmask[:, 0:D].rearrange("p (h v) -> p h v", v=DH)
            hi = headmask[:, D:D + H0]
            chain(g.affine_select(out=hm, in_=hm, compare_op=ALU.is_ge, fill=0.0, base=0, pattern=[[-DH, H0], [0, DH]], channel_multiplier=1))
            chain(g.affine_select(out=hm, in_=hm, compare_op=ALU.is_ge, fill=0.0, base=DH - 1, pattern=[[DH, H0], [0, DH]], channel_multiplier=-1))
            chain(g.affine_select(out=hi, in_=hi, compare_op=ALU.is_ge, fill=0.0, base=0, pattern=[[-DH, H0]], channel_multiplier=1))
            g.affine_select(out=hi, in_=hi, compare_op=ALU.is_ge, fill=0.0, base=DH - 1, pattern=[[DH, H0]], channel_multiplier=-1).then_inc(s_["consts_ready"], 1)
            chain(g.memset(reset[:, :], 1.0))
            chain(g.memset(tiles(reset[:, :], E0)[:, :, 0:1], 0.0))
            for u in range(2):
                g.memset(tiles(S[u]["q"][:, :], D + 4)[:, :, D:D + 4], 1.0).then_inc(s_["consts_ready"], 1)
                g.iota(keyc[u][:, :], pattern=[[-K0N * P, NT], [0, E0]], base=NKEY + 1 - K0N * L * PAIRS * u, channel_multiplier=-K0N,
                       allow_small_or_imprecise_dtypes=True).then_inc(s_["consts_ready"], 1)
            g.memset(epsc[:, :], EPS)
            g.memset(mhalf[:, :], -0.5).then_inc(s_["consts_ready"], 1)
            pool.wait_ge(s_["weights_ready"], 16 * 11)
            g.tensor_tensor(b12_bc[:, 0, :], b12_bc[:, 0, :], b12_bc[:, 1, :], ALU.add).then_inc(s_["consts_ready"], 1)
            pool.wait_ge(s_["consts_ready"], 8)
            C.setup_pool_early(pool)

            with pool.Fori(0, PAIRS) as i:
                for u in range(2):
                    s, n = S[u], 2 * i + (u + 1)
                    pool.wait_ge(x_loaded[u], 16 * i + 16)
                    g.tensor_tensor(s["r"][:, :], s["x"][:, :], s["x"][:, :], ALU.add).then_inc(s_["xr1"], 1)
                    pool.wait_ge(s_["xr1"], n)
                    g.tensor_tensor(tiles(s["r"][:, :]), tiles(s["r"][:, :]), bcast_mid(b12_bc[:, 0, :], NT), ALU.add).then_inc(s_["xr2"], 1)
                for u in range(2):
                    s, n = S[u], 2 * i + (u + 1)
                    pool.wait_ge(s_["mv1"], n)
                    var = tiles(s["mv"][:, :], 2)[:, :, 1]
                    g.tensor_tensor(s["rstd"][:, :], var, epsc[:, :], ALU.add).then_inc(s_["var_eps"], 1)
                    pool.wait_ge(s_["var_eps"], 4 * i + (u + 1))
                    g.tensor_tensor(s["rstd"][:, :], s["rstd"][:, :], mhalf[:, :], ALU.pow).then_inc(s_["rstd1"], 1)
                for u in range(2):
                    s, n = S[u], 2 * i + (u + 1)
                    pool.wait_ge(s_["mv3"], n)
                    var = tiles(s["mv3"][:, :], 2)[:, :, 1]
                    g.tensor_tensor(s["rstd3"][:, :], var, epsc[:, 0:NT], ALU.add).then_inc(s_["var_eps"], 1)
                    pool.wait_ge(s_["var_eps"], 4 * i + (u + 3))
                    g.tensor_tensor(s["rstd3"][:, :], s["rstd3"][:, :], mhalf[:, 0:NT], ALU.pow).then_inc(s_["rstd3"], 1)
                for u in range(2):
                    s, n = S[u], 2 * i + (u + 1)
                    pool.wait_ge(s_["x1T_sb"], n)
                    g.tensor_copy(x1T_all[:, bass.ds(i * L + u * (T // 2), L)], S[u]["x1T"]).then_inc(s_["x1T_kept"], 1)
                    pool.wait_ge(s_["incl_sb"], n)
                    g.tensor_tensor(s["incl"][:, :], keyc[u][:, :], s["incl"][:, :], ALU.subtract).then_inc(s_["ka_sb"], 1)
                    g.tensor_scalar(keyc[u][:, :], keyc[u][:, :], float(-K0N * L), None, ALU.add)
                    pool.wait_ge(s_["ka_sb"], n)
                    pool.wait_ge(s_["keyT_mm"], i + 1)
                    g.tensor_tensor(keys[:, :, u, :], tiles(s["incl"][:, :], E0), tiles(s["mask"][:, :], E0), ALU.mult).then_inc(s_["key_sb"], 1)
                    pool.wait_ge(s_["key_sb"], n)

            with pool.Fori(0, PAIRS) as i:
                for u in range(2):
                    n = 2 * i + (u + 1)
                    pool.wait_ge(s_["su_sb"], n)
                    g.tensor_tensor(shs[u], sgs[u], sus[u], ALU.mult).then_inc(s_["sh_sb"], 1)
                for u in range(2):
                    n = 2 * i + (u + 1)
                    pool.wait_ge(s_["ysh_sb"], n)
                    pool.wait_ge(x_loaded[u], 16 * i + 16 * (PAIRS + 1))
                    g.tensor_tensor(base_all[:, bass.ds(2 * i + u, 1), :].rearrange("p o d -> p (o d)"), x1s[u], yss[u], ALU.add).then_inc(s_["base_sb"], 1)

            C.setup_pool_late(pool)
            pool.wait_ge(s_["slot_index"], 2)
            pool.wait_ge(s_["x1T_kept"], B)
            pool.wait_ge(s_["base_sb"], B + 1)
            for u in range(2):
                pool.wait_ge(xw_stored[u], 16 * PAIRS + 16)
            pool.wait_ge(s_["zeros_written"], 16 * (NZ + 1))
            for m in range(EP):
                if m >= 8:
                    pool.wait_ge(gathered[m % 8], 16 * (m // 8))
                g.indirect_dma_start(rows_all[:, m * ROW:(m + 1) * ROW], None, table,
                                     bass.IndirectOffsetOnAxis(ap=tok_row[:, m:m + 1], axis=0)).then_inc(gathered[m % 8], 16)
            for m in range(EP):
                pool.wait_ge(s_["y_sb"], m + 1)
                g.indirect_dma_start(contrib, bass.IndirectOffsetOnAxis(ap=dest_row[:, m:m + 1], axis=0),
                                     y_all[:, m * D:(m + 1) * D], None, bounds_check=NKEY - 1, oob_is_err=False).then_inc(s_["rows_scattered"], 16)
            C.pool(pool)


        @block.sync
        def _(sp):
            for u in range(2):
                sp.dma_start(tiles(S[u]["x"][:, :]), x_view[PAIRS * u]).then_inc(x_loaded[u], 16)
            smalls = [(rw_sb[:, :], router_w), (Wq_sb[:, :], Wq), (Wm_sb[:, :], Wm), (W1_sb[:, :], W1),
                      (W2_sb[:, :, :], W2.rearrange("(h p) d -> p h d", p=P)),
                      (g1_bc[:, :], g1.partition_broadcast(P)), (g2_bc[:, :], g2.partition_broadcast(P)),
                      (b12_bc[:, 0, :], b1.partition_broadcast(P)), (b12_bc[:, 1, :], b2.partition_broadcast(P)),
                      (wsgu_sb[:, :], ws_gate_up), (wsd_sb[:, :], ws_down)]
            for dst, src in smalls:
                sp.dma_start(dst, src).then_inc(s_["weights_ready"], 16)
            C.setup_sync(sp)
            sp.wait_ge(s_["zero_tile"], 1)
            sp.dma_start(table[T:T + 1, :], zeros[0:1, 0:ROW]).then_inc(s_["zeros_written"], 16)
            with sp.Fori(0, PAIRS - 1) as i:
                for u in range(2):
                    sp.wait_ge(s_["xT_mm"], 2 * i + u + 1)
                    sp.wait_ge(s_["xr1"], 2 * i + u + 1)
                    sp.dma_start(tiles(S[u]["x"][:, :]), x_view[bass.ds(i + (PAIRS * u + 1), 1)].rearrange("o p j d -> (o p) j d")).then_inc(x_loaded[u], 16)
                for k in range(2):
                    sp.dma_start(zero_view[bass.ds(2 * i + k, 1)].rearrange("o p f -> (o p) f"), zeros).then_inc(s_["zeros_written"], 16)
                for u in range(2):
                    sp.wait_ge(s_["x1_sb"], 2 * i + u + 1)
                    sp.wait_ge(s_["w_sb"], 2 * i + u + 1)
                    sp.dma_start(table_view[bass.ds(i + PAIRS * u, 1)].rearrange("o p j d -> (o p) j d"), tiles(S[u]["xw"][:, :], ROW)).then_inc(xw_stored[u], 16)
            for u in range(2):
                sp.wait_ge(s_["x1_sb"], 2 * (PAIRS - 1) + u + 1)
                sp.wait_ge(s_["w_sb"], 2 * (PAIRS - 1) + u + 1)
                sp.dma_start(table_view[PAIRS - 1 + PAIRS * u], tiles(S[u]["xw"][:, :], ROW)).then_inc(xw_stored[u], 16)
            for k in range(2 * (PAIRS - 1), NZ):
                sp.dma_start(zero_view[k], zeros).then_inc(s_["zeros_written"], 16)
            C.setup_sync_skew(sp)
            for u in range(2):
                sp.wait_ge(xw_stored[u], 16 * PAIRS + 16)
            sp.wait_ge(s_["zeros_written"], 16 * (NZ + 1))
            with sp.Fori(0, PAIRS) as i:
                for u in range(2):
                    sp.wait_ge(s_["base_sb"], 2 * i + 1)
                    sp.dma_start(tiles(x1s[u]), table_view[bass.ds(2 * i + u, 1), :, :, 0:D].rearrange("o p j d -> (o p) j d")).then_inc(x_loaded[u], 16)
            C.sync(sp)


        @block.scalar
        def _(act):
            a = nc.scalar
            act.wait_ge(s_["weights_ready"], 16 * 11)
            n = 2 * EP_EARLY
            act.dma_start(wgu_e[:, :, 0, :], w_gate[0:n].rearrange("e p f -> p e f")).then_inc(s_["early_weights"], 16)
            act.dma_start(wgu_e[:, :, 1, :], w_up[0:n].rearrange("e p f -> p e f")).then_inc(s_["early_weights"], 16)
            act.dma_start(wd_e[:, :, :], w_down[0:n].rearrange("e p f -> p e f")).then_inc(s_["early_weights"], 16)
            act.wait_ge(s_["zero_tile"], 1)
            act.wait_ge(s_["rwT_mm"], 1)
            a.copy(rwT[:, :], bank[2][:, 0:E0]).then_inc(s_["rwT_sb"], 1)
            act.wait_ge(s_["consts_ready"], 8)
            with act.Fori(0, PAIRS) as i:
                for u in range(2):
                    n = 2 * i + (u + 1)
                    act.wait_ge(s_["xT_mm"], n)
                    a.copy(S[u]["xT"][:, :], bank[4 * u][:, :]).then_inc(s_["xT_sb"], 1)
                for u in range(2):
                    s, n = S[u], 2 * i + (u + 1)
                    act.wait_ge(s_["q_mm"], n)
                    a.activation(s["e"][:, :], bank[4 * u + 1][:, :], ACT.Relu, scale=-1.0).then_inc(s_["negq"], 1)
                    a.copy(tiles(s["q"][:, :], D + 4)[:, :, 0:D], tiles(bank[4 * u + 1][:, :]))
                    act.wait_ge(s_["negq"], n)
                    a.activation(s["e"][:, :], s["e"][:, :], ACT.Exp, scale=-1.0).then_inc(s_["eq"], 1)
                for u in range(2):
                    s, n = S[u], 2 * i + (u + 1)
                    act.wait_ge(s_["featT_mm"], n)
                    a.copy(s["featT"][:, :], bank[4 * u][:, :]).then_inc(s_["featT_sb"], 1)
                for u in range(2):
                    s, n = S[u], 2 * i + (u + 1)
                    act.wait_ge(s_["msgT_mm"], n)
                    a.copy(s["msgT"][:, :], bank[4 * u][:, :]).then_inc(s_["msgT_sb"], 1)
                for u in range(2):
                    s, n = S[u], 2 * i + (u + 1)
                    act.wait_ge(s_["m2T_mm"], n)
                    a.copy(s["m2T"][:, :], bank[4 * u + 2][:, :]).then_inc(s_["m2T_sb"], 1)
                for u in range(2):
                    s, n = S[u], 2 * i + (u + 1)
                    act.wait_ge(s_["hT_mm"], n)
                    a.activation(s["hT"][:, 0:L], bank[4 * u][:, :], ACT.Relu)
                    a.activation(s["hT"][:, L:2 * L], bank[4 * u + 3][:, :], ACT.Relu).then_inc(s_["hT1_sb"], 1)
                for u in range(2):
                    n = 2 * i + (u + 1)
                    act.wait_ge(s_["x1T_mm"], n)
                    a.copy(S[u]["x1T"], bank[4 * u][:, :]).then_inc(s_["x1T_sb"], 1)
                for u in range(2):
                    s, n = S[u], 2 * i + (u + 1)
                    act.wait_ge(s_["lg_mm"], n)
                    a.copy(s["lg"][:, :], bank[4 * u + 1][:, 0:NT * E0]).then_inc(s_["lg_sb"], 1)
                for u in range(2):
                    s, n = S[u], 2 * i + (u + 1)
                    act.wait_ge(s_["d_sb"], n)
                    a.activation(s["ex"][:, :], s["ex"][:, :], ACT.Exp).then_inc(s_["ex_sb"], 1)
                act.wait_ge(s_["keyT_mm"], i + 2)
                a.copy(keyT[:, bass.ds(i * L, L)], bank[3][:, :]).then_inc(s_["keyT_sb"], 1)

            for u in range(2):
                act.wait_ge(xw_stored[u], 16 * PAIRS + 16)
            act.wait_ge(s_["key_sb"], B)
            KL = EP - EP_EARLY
            for k in range(0, 2 * KL, KL // 2):
                e0 = 2 * EP_EARLY + k
                n = KL // 2
                act.dma_start(wgu_l[:, k:k + n, 0, :], w_gate[e0:e0 + n].rearrange("e p f -> p e f")).then_inc(s_["late_weights"], 16)
                act.dma_start(wgu_l[:, k:k + n, 1, :], w_up[e0:e0 + n].rearrange("e p f -> p e f")).then_inc(s_["late_weights"], 16)
                act.dma_start(wd_l[:, k:k + n, :], w_down[e0:e0 + n].rearrange("e p f -> p e f")).then_inc(s_["late_weights"], 16)

            act.wait_ge(s_["zeros_written"], 16 * (NZ + 1))
            with act.Fori(0, PAIRS) as i:
                for u in range(2):
                    n = 2 * i + (u + 1)
                    act.wait_ge(s_["sg_mm"], n)
                    a.activation(sgs[u], bank[4 * u][0:F0, :], ACT.Silu)
                    a.copy(sus[u], bank[4 * u + 1][0:F0, :]).then_inc(s_["su_sb"], 1)
                for u in range(2):
                    n = 2 * i + (u + 1)
                    act.wait_ge(s_["ysh_mm"], n)
                    a.copy(yss[u], bank[4 * u + 2][:, :]).then_inc(s_["ysh_sb"], 1)

            C.setup_act(act)
            for m in range(EP):
                act.wait_ge(s_["xgT_mm"], m + 1)
                a.copy(xgT[m % 2][:, :], bank[m % 2][:, 0:P]).then_inc(s_["xgT_sb"], 1)
                if m >= 1:
                    expert_silu(act, m - 1)
            expert_silu(act, EP - 1)
            C.act(act)


        @block.vector
        def _(dve):
            v = nc.vector
            v.memset(landing(), 0.0).then_inc(s_["keyT_mm"], 1)
            v.memset(landing(), 0.0).then_inc(s_["keyT_sb"], 1)
            v.memset(landing(), 0.0).then_inc(s_["base_sb"], 1)
            for u in range(2):
                v.memset(landing(), 0.0).then_inc(xw_stored[u], 16)
            dve.wait_ge(s_["consts_ready"], 8)
            with dve.Fori(0, PAIRS) as i:
                for u in range(2):
                    s, n = S[u], 2 * i + (u + 1)
                    dve.wait_ge(s_["eq"], n)
                    v.scalar_tensor_tensor(out=s["feat"][:, :], in0=bank[4 * u + 1][:, :], scalar=0.0, in1=s["e"][:, :],
                                           op0=ALU.max, op1=ALU.add).then_inc(s_["feat_sb"], 1)
                for u in range(2):
                    s, n = S[u], 2 * i + (u + 1)
                    dve.wait_ge(s_["kv_mm"], n)
                    v.tensor_tensor(s["kvm"][:, 0:D], bank[4 * u + 2][:, 0:D], headmask[:, 0:D], ALU.mult)
                    v.tensor_scalar(s["kvm"][:, D:D + H0], headmask[:, D:D + H0], bank[4 * u + 2][:, D:D + 1], None, ALU.mult).then_inc(s_["kvm_sb"], 1)
                for u in range(2):
                    s, n = S[u], 2 * i + (u + 1)
                    dve.wait_ge(s_["num_mm"], n)
                    v.tensor_scalar(s["z"][:, :], bank[4 * u + 2][:, 256:256 + NT * H0], ATTN_EPS, None, ALU.add).then_inc(s_["z_step"], 1)
                    dve.wait_ge(s_["z_step"], 2 * n - 1)
                    v.reciprocal(s["z"][:, :], s["z"][:, :]).then_inc(s_["z_step"], 1)
                    dve.wait_ge(s_["z_step"], 2 * n)
                    v.tensor_tensor(s["msg"][:, :].rearrange("p (a c) -> p a c", c=DH), bank[4 * u + 1][:, :].rearrange("p (a c) -> p a c", c=DH),
                                    bcast_last(s["z"][:, :], DH), ALU.mult).then_inc(s_["msg_sb"], 1)
                for u in range(2):
                    s, n = S[u], 2 * i + (u + 1)
                    dve.wait_ge(s_["mlp_mm"], n)
                    st = tiles(s["stats"][:, :], 6)
                    mv = tiles(s["mv"][:, :], 2)
                    for k in range(2):
                        for j in range(NT):
                            ins = v.bn_stats(st[:, NT * k + j, :], bank[4 * u + 1 + k][:, j * D:(j + 1) * D])
                    ins.then_inc(s_["st1"], 1)
                    dve.wait_ge(s_["st1"], n)
                    v.memset(landing(), 0.0)
                    for k in range(2 * NT):
                        ins = v.bn_aggr(mv[:, k, :], st[:, k, :])
                    ins.then_inc(s_["mv1"], 1)
                for u in range(2):
                    s, n = S[u], 2 * i + (u + 1)
                    mv = tiles(s["mv"][:, :], 2)
                    dve.wait_ge(s_["mv1"], n)
                    for k, dst, gain in ((0, "a1", g1_bc), (1, "a2", g2_bc)):
                        for j in range(NT):
                            ins = v.scalar_tensor_tensor(out=s[dst][:, j * D:(j + 1) * D], in0=bank[4 * u + 1 + k][:, j * D:(j + 1) * D],
                                                         scalar=mv[:, NT * k + j, 0:1], in1=gain[:, :], op0=ALU.subtract, op1=ALU.mult)
                    ins.then_inc(s_["centred"], 1)
                for u in range(2):
                    s, n = S[u], 2 * i + (u + 1)
                    dve.wait_ge(s_["centred"], n)
                    dve.wait_ge(s_["rstd1"], n)
                    dve.wait_ge(s_["xr2"], n)
                    for k, src in enumerate(("a1", "a2")):
                        for j in range(NT):
                            c = slice(j * D, (j + 1) * D)
                            ins = v.scalar_tensor_tensor(out=s["r"][:, c], in0=s[src][:, c], scalar=s["rstd"][:, NT * k + j:NT * k + j + 1],
                                                         in1=s["r"][:, c], op0=ALU.mult, op1=ALU.add)
                        ins.then_inc(s_["r_step"], 1)
                        dve.wait_ge(s_["r_step"], 2 * n - 1 + k)
                    v.memset(landing(), 0.0)
                    st, mv = tiles(s["stats3"][:, :], 6), tiles(s["mv3"][:, :], 2)
                    for j in range(NT):
                        ins = v.bn_stats(st[:, j, :], s["r"][:, j * D:(j + 1) * D])
                    ins.then_inc(s_["st3"], 1)
                    dve.wait_ge(s_["st3"], n)
                    v.memset(landing(), 0.0)
                    for j in range(NT):
                        ins = v.bn_aggr(mv[:, j, :], st[:, j, :])
                    ins.then_inc(s_["mv3"], 1)
                for u in range(2):
                    s, n = S[u], 2 * i + (u + 1)
                    mv, xw = tiles(s["mv3"][:, :], 2), tiles(s["xw"][:, :], ROW)
                    dve.wait_ge(s_["rstd3"], n)
                    dve.wait_ge(xw_stored[u], 16 * i + 16)
                    for j in range(NT):
                        ins = v.tensor_scalar(xw[:, j, 0:D], s["r"][:, j * D:(j + 1) * D], mv[:, j, 0:1], s["rstd3"][:, j:j + 1], ALU.subtract, ALU.mult)
                    ins.then_inc(s_["x1_sb"], 1)
                for u in range(2):
                    s, n = S[u], 2 * i + (u + 1)
                    dve.wait_ge(s_["lg_sb"], n)
                    v.memset(landing(), 0.0)
                    lg, top = tiles(s["lg"][:, :], E0), tiles(s["top"][:, :], 8)
                    for j in range(NT):
                        ins = v.max(top[:, j, :], lg[:, j, :])
                    ins.then_inc(s_["pick_step"], 1)
                    dve.wait_ge(s_["pick_step"], 3 * n - 2)
                    v.tensor_tensor(tiles(s["ex"][:, :], E0), lg, bcast_last(top[:, :, 0], E0), ALU.subtract).then_inc(s_["d_sb"], 1)
                    for j in range(NT):
                        ins = v.match_replace(tiles(s["zap"][:, :], E0)[:, j, :], top[:, j, :], lg[:, j, :], NEG)
                    ins.then_inc(s_["pick_step"], 1)
                    dve.wait_ge(s_["pick_step"], 3 * n - 1)
                    v.tensor_tensor(s["mask"][:, :], s["zap"][:, :], s["lg"][:, :], ALU.not_equal).then_inc(s_["pick_step"], 1)
                    dve.wait_ge(s_["pick_step"], 3 * n)
                    v.tensor_tensor_scan(s["incl"][:, :], reset[:, :], s["mask"][:, :], 0.0, ALU.mult, ALU.add).then_inc(s_["incl_sb"], 1)
                for u in range(2):
                    s, n = S[u], 2 * i + (u + 1)
                    xw = tiles(s["xw"][:, :], ROW)
                    dve.wait_ge(s_["ex_sb"], n)
                    v.tensor_tensor(s["ex"][:, :], s["ex"][:, :], s["mask"][:, :], ALU.mult).then_inc(s_["soft_step"], 1)
                    dve.wait_ge(s_["soft_step"], 3 * n - 2)
                    v.tensor_reduce(s["esum"][:, :], tiles(s["ex"][:, :], E0), AX.X, ALU.add).then_inc(s_["soft_step"], 1)
                    dve.wait_ge(s_["soft_step"], 3 * n - 1)
                    v.reciprocal(s["esum"][:, :], s["esum"][:, :]).then_inc(s_["soft_step"], 1)
                    dve.wait_ge(s_["soft_step"], 3 * n)
                    v.tensor_tensor(xw[:, :, D:ROW], tiles(s["ex"][:, :], E0), bcast_last(s["esum"][:, :], E0), ALU.mult).then_inc(s_["w_sb"], 1)

            rounds = [0]

            def step(ins):
                rounds[0] += 1
                ins.then_inc(s_["round_done"], 1)
                dve.wait_ge(s_["round_done"], rounds[0])

            dve.wait_ge(s_["keyT_sb"], PAIRS + 1)
            for r in range(CAP // 8):
                step(v.max(cand[:, 8 * r:8 * r + 8], keyT[:, :]))
                if r < CAP // 8 - 1:
                    step(v.match_replace(keyT[:, :], cand[:, 8 * r:8 * r + 8], keyT[:, :], 0.0))
            v.tensor_copy(both[:, 0:CAP], cand[0:E0, :])
            step(v.tensor_copy(both[:, CAP:2 * CAP], cand[E0:2 * E0, :]))
            for r in range(CAP // 8):
                step(v.max(slot_key[:, 8 * r:8 * r + 8], both[:, :]))
                if r < CAP // 8 - 1:
                    step(v.match_replace(both[:, :], slot_key[:, 8 * r:8 * r + 8], both[:, :], 0.0))
            v.tensor_scalar(slot_key[:, :], slot_key[:, :], -1.0, float(NKEY), ALU.mult, ALU.add).then_inc(s_["slots_sb"], 1)
            dve.wait_ge(s_["slotT_mm"], 1)
            pairs = bank[6][0:CAP, 0:E0].rearrange("c (m two) -> c m two", two=2)
            v.tensor_copy(dest_row[0:CAP, :], pairs[:, :, 0])
            v.tensor_copy(dest_row[CAP:2 * CAP, :], pairs[:, :, 1]).then_inc(s_["slot_index"], 1)
            dve.wait_ge(s_["slot_index"], 1)
            v.tensor_scalar(tok_row[:, :], dest_row[:, :], 3, None, ALU.logical_shift_right).then_inc(s_["slot_index"], 1)

            for m in range(EP):
                dve.wait_ge(s_["sil_sb"], m + 1)
                if m >= 2:
                    dve.wait_ge(s_["y_mm"], m - 1)
                v.tensor_tensor(hexp[m % 2][:, :], sil[m % 2][:, :], bank[2 + m % 2][0:F0, P:2 * P], ALU.mult).then_inc(s_["hexp_sb"], 1)
                if m >= 1:
                    expert_weigh(dve, m - 1)
            expert_weigh(dve, EP - 1)
            C.dve(dve)


        @block.tensor
        def _(pe):
            t = nc.tensor

            def transposes(dst, src, w=D):
                for j in range(NT):
                    ins = t.transpose(dst[:, j * P:(j + 1) * P], src[:, j * w:j * w + P], ident[:, :])
                return ins

            pe.wait_ge(s_["consts_ready"], 8)
            pe.wait_ge(s_["weights_ready"], 16 * 11)
            t.transpose(bank[2][:, 0:E0], rw_sb[:, :], ident[0:E0, 0:E0]).then_inc(s_["rwT_mm"], 1)
            pe.wait_ge(s_["rwT_sb"], 1)
            with pe.Fori(0, PAIRS) as i:
                for u in range(2):
                    pe.wait_ge(x_loaded[u], 16 * i + 16)
                    transposes(bank[4 * u], S[u]["x"]).then_inc(s_["xT_mm"], 1)
                for u in range(2):
                    s, n = S[u], 2 * i + (u + 1)
                    pe.wait_ge(s_["xT_sb"], n)
                    for j in range(NT):
                        ins = t.matmul(bank[4 * u + 1][:, j * D:(j + 1) * D], s["xT"][:, j * P:(j + 1) * P], Wq_sb[:, :], start=True, stop=True)
                    ins.then_inc(s_["q_mm"], 1)
                for u in range(2):
                    s, n = S[u], 2 * i + (u + 1)
                    pe.wait_ge(s_["feat_sb"], n)
                    transposes(bank[4 * u], s["feat"]).then_inc(s_["featT_mm"], 1)
                    for j in range(NT):
                        ins = t.matmul(bank[4 * u + 2][:, 0:D + 1], s["feat"][:, j * D:(j + 1) * D], s["q"][:, j * (D + 4):j * (D + 4) + D + 1],
                                       start=(j == 0), stop=(j == NT - 1))
                    ins.then_inc(s_["kv_mm"], 1)
                for u in range(2):
                    s, n = S[u], 2 * i + (u + 1)
                    pe.wait_ge(s_["featT_sb"], n)
                    pe.wait_ge(s_["kvm_sb"], n)
                    for j in range(NT):
                        ft = s["featT"][:, j * P:(j + 1) * P]
                        t.matmul(bank[4 * u + 1][:, j * D:(j + 1) * D], ft, s["kvm"][:, 0:D], start=True, stop=True)
                        ins = t.matmul(bank[4 * u + 2][:, 256 + j * H0:256 + (j + 1) * H0], ft, s["kvm"][:, D:D + H0], start=True, stop=True)
                    ins.then_inc(s_["num_mm"], 1)
                for u in range(2):
                    s, n = S[u], 2 * i + (u + 1)
                    pe.wait_ge(s_["msg_sb"], n)
                    transposes(bank[4 * u], s["msg"]).then_inc(s_["msgT_mm"], 1)
                for u in range(2):
                    s, n = S[u], 2 * i + (u + 1)
                    pe.wait_ge(s_["msgT_sb"], n)
                    t.matmul(bank[4 * u + 2][:, :], Wm_sb[:, :], s["msgT"][:, :], start=True, stop=True).then_inc(s_["m2T_mm"], 1)
                    for j in range(NT):
                        t.matmul(bank[4 * u + 1][:, j * D:(j + 1) * D], s["msgT"][:, j * P:(j + 1) * P], Wm_sb[:, :], start=True, stop=True)
                pe.wait_ge(s_["keyT_sb"], i + 1)
                for u in range(2):
                    s, n = S[u], 2 * i + (u + 1)
                    pe.wait_ge(s_["m2T_sb"], n)
                    t.matmul(bank[4 * u][:, :], W1_sb[:, 0:D], s["m2T"][:, :], start=True, stop=True)
                    t.matmul(bank[4 * u + 3][:, :], W1_sb[:, D:2 * D], s["m2T"][:, :], start=True, stop=True).then_inc(s_["hT_mm"], 1)
                for u in range(2):
                    s, n = S[u], 2 * i + (u + 1)
                    pe.wait_ge(s_["hT1_sb"], n)
                    for j in range(NT):
                        for h in range(2):
                            ins = t.matmul(bank[4 * u + 2][:, j * D:(j + 1) * D], s["hT"][:, h * L + j * P:h * L + (j + 1) * P], W2_sb[:, h, :],
                                           start=(h == 0), stop=(h == 1))
                    ins.then_inc(s_["mlp_mm"], 1)
                for u in range(2):
                    s, n = S[u], 2 * i + (u + 1)
                    pe.wait_ge(s_["x1_sb"], n)
                    transposes(bank[4 * u], s["xw"], ROW).then_inc(s_["x1T_mm"], 1)
                for u in range(2):
                    n = 2 * i + (u + 1)
                    pe.wait_ge(s_["x1T_sb"], n)
                    for j in range(NT):
                        ins = t.matmul(bank[4 * u + 1][:, j * E0:(j + 1) * E0], S[u]["x1T"][:, j * P:(j + 1) * P], rwT[:, :], start=True, stop=True)
                    ins.then_inc(s_["lg_mm"], 1)
                pe.wait_ge(s_["key_sb"], 2 * i + 2)
                for j in range(NT):
                    ins = t.transpose(bank[3][:, j * P:(j + 1) * P], keys[:, j, :, :].rearrange("p u e -> p (u e)"), ident[:, :])
                ins.then_inc(s_["keyT_mm"], 1)

            with pe.Fori(0, PAIRS) as i:
                for u in range(2):
                    n = 2 * i + (u + 1)
                    xs = x1T_all[:, bass.ds(i * 2 * L + u * L, L)]
                    t.matmul(bank[4 * u][0:F0, :], wsgu_sb[:, 0:F0], xs, start=True, stop=True)
                    t.matmul(bank[4 * u + 1][0:F0, :], wsgu_sb[:, F0:2 * F0], xs, start=True, stop=True).then_inc(s_["sg_mm"], 1)
                for u in range(2):
                    n = 2 * i + (u + 1)
                    pe.wait_ge(s_["sh_sb"], n)
                    for j in range(NT):
                        ins = t.matmul(bank[4 * u + 2][:, j * D:(j + 1) * D], shs[u][:, j * P:(j + 1) * P], wsd_sb[:, :], start=True, stop=True)
                    ins.then_inc(s_["ysh_mm"], 1)

            C.setup_pe(pe)
            pe.wait_ge(s_["slots_sb"], 1)
            pe.wait_ge(s_["ysh_sb"], B)
            t.transpose(bank[6][0:CAP, 0:E0], slot_key[:, :], ident[0:E0, 0:E0]).then_inc(s_["slotT_mm"], 1)
            pe.wait_ge(s_["early_weights"], 16 * 3)
            for m in range(EP + 2):
                if m == EP_EARLY:
                    pe.wait_ge(s_["late_weights"], 16 * 12)
                if m < EP:
                    pe.wait_ge(gathered[m % 8], 16 * (m // 8 + 1))
                    t.transpose(bank[m % 2][:, 0:P], rows_all[:, m * ROW:m * ROW + D], ident[:, :]).then_inc(s_["xgT_mm"], 1)
                if 1 <= m <= EP:
                    expert_up(pe, m - 1)
                if m >= 2:
                    expert_down(pe, m - 2)
            C.pe(pe)


_INS = ["L0_attn_x", "L0_attn_Wq", "L0_attn_Wm", "L0_attn_W1", "L0_attn_W2", "L0_attn_g1", "L0_attn_b1", "L0_attn_g2",
        "L0_attn_b2", "L0_ffn_router_w", "L0_ffn_w_gate", "L0_ffn_w_up", "L0_ffn_w_down", "L0_ffn_ws_gate_up",
        "L0_ffn_ws_down", "L1_attn_ln_w", "L1_attn_ln_b", "L1_attn_Wh", "L1_attn_bh", "L1_attn_Wqk", "L1_attn_bqk",
        "L1_attn_qk_w", "L1_attn_qk_b", "L1_attn_rel_table", "L1_attn_Wout", "L1_attn_bout", "L1_ffn_Wg", "L1_ffn_W1",
        "L1_ffn_b1", "L1_ffn_Wo", "L1_ffn_bo"]


def kernel(**inputs):
    import concourse.bacc as bacc
    from concourse.bass_utils import run_bass_kernel_spmd as run

    nc = bacc.Bacc("TRN2", target_bir_lowering=False, num_devices=1)
    arrays, args = {}, []
    for name in _INS:
        a = np.ascontiguousarray(inputs[name])
        arrays[f"in_{name}"] = a
        args.append(nc.dram_tensor(f"in_{name}", a.shape, mybir.dt.from_np(a.dtype), kind="ExternalInput").ap())
    out = nc.dram_tensor("out_0", (B, L, D), F32, kind="ExternalOutput").ap()
    build(nc, *args, out)
    r = run(nc, [arrays], core_ids=[0])
    return r.results[0]["out_0"]
```

```python
import numpy as np
import concourse.bass as bass
from concourse import mybir
from contextlib import ExitStack

F32 = mybir.dt.float32
F32R = mybir.dt.float32r
I32 = mybir.dt.int32
U32 = mybir.dt.uint32
ALU = mybir.AluOpType
ACT = mybir.ActivationFunctionType
AX = mybir.AxisListType

P = 128
B, L, D = 8, 512, 128
T = B * L
NT = L // P
PAIRS = B // 2
EPS = 1e-5
H0, DH = 8, 16
ATTN_EPS = 1e-6
E0, K0N, F0, CAP = 64, 8, 96, 64
EP = E0 // 2
EP_EARLY = 12
ROW = D + E0
NKEY = T * K0N
NEG = -3.0e38
STRUCK = 3.0e38
G, HID, QK = 32, 256, 128
BIAS_SCALE = float(QK) ** 0.5
NBUCKET, MAXDIST = 32, 128
E1, H1 = 8, 256
MASKED = -1e30
NROWS = 5 + 4 + 4 + E1 + 4 * E1
AT = dict(zT=0, out=3, gate=2, y4=4, quads=3, gate2=3, v=4, outb=7, sim=6, off=7, av=8, w=9, x3=11, x3T=12, lg=13, y=7, z=11)
GATING = {13: ((), (0,), (1,)), 14: ((), (2,), (3,)), 15: ((4,), (5,), (6,))}
GATING_NEXT = {0: ((7, 8), (9, 10)), 1: ((11, 12), (13, 14))}
GATE_STEPS = 15
WEIGH = {2: 0, 3: 1, 5: 2, 7: 3, 9: 4, 11: 5, 13: 6, 15: 7}


def bcast_last(ap, n):
    shape = list(ap.shape) + [n]
    return ap.unsqueeze(len(shape) - 1).broadcast_to(shape)


def bcast_mid(ap, n):
    return ap.unsqueeze(1).broadcast_to([ap.shape[0], n, ap.shape[1]])


def bucket_runs():
    exact = NBUCKET // 2
    runs = []
    for n in range(G):
        if n < exact:
            b = n
        else:
            b = exact + int(np.float32(np.log(np.float32(n) / np.float32(exact))) / np.float32(np.log(MAXDIST / exact))
                            * np.float32(NBUCKET - exact))
            b = min(b, NBUCKET - 1)
        if runs and runs[-1][2] == b:
            runs[-1] = (runs[-1][0], runs[-1][1] + 1, b)
        else:
            runs.append((n, 1, b))
    return runs


def first(f):
    return isinstance(f, int) and f == 0


def stage_a(eng, half):
    half(eng, p1=(0, 0))
    half(eng, p1=(0, 1), p2=(0, 0))
    half(eng, p1=(1, 0), p2=(0, 1), p3=(0, 0))
    half(eng, p1=(1, 1), p2=(1, 0), p3=(0, 1))
    with eng.Fori(0, PAIRS - 2) as i:
        half(eng, p1=(i + 2, 0), p2=(i + 1, 1), p3=(i + 1, 0), keys=i)
        half(eng, p1=(i + 2, 1), p2=(i + 2, 0), p3=(i + 1, 1))
    half(eng, p2=(PAIRS - 1, 1), p3=(PAIRS - 1, 0), keys=PAIRS - 2)
    half(eng, p3=(PAIRS - 1, 1))
    half(eng, keys=PAIRS - 1)


class StageC:

    def __init__(self, nc, sb, sem):
        self.nc = nc
        keep = {}
        def k(name, shape, dt=F32):
            keep[name] = sb("c_" + name, shape, dt)
        k("rows", [NROWS, D]); k("cols", [P, NROWS]); k("whqk", [P, 2 * HID + QK])
        k("wh_hi", [P, 2 * HID + QK], F32R); k("wh_lo", [P, 2 * HID + QK], F32R)
        k("vb", [2, HID]); k("vb_hi", [2, HID], F32R); k("vb_hl", [2, HID], F32R); k("bh_row", [1, HID]); k("one12", [1, 2]); k("sel2", [2, 1])
        k("tmp2", [2, NT * D]); k("lnb2", [P, 2])
        k("ones_f", [2, P]); k("ones", [2, P], F32R); k("bcols", [P, 3]); k("quadw", [P, 2]); k("quadb", [P, 2])
        k("biasT", [P, P]); k("ltmask", [P, P]); k("rel", [1, 64]); k("ext", [1, 64])
        k("wout", [P, 2, D]); k("wo", [P, H1]); k("woT", [P, 2, D])
        k("bout", [2, NT, D]); k("bout_hi", [2, NT * D], F32R); k("bout_hl", [2, NT * D], F32R)
        k("bo16", [16, D]); k("bo_hi", [16, D], F32R); k("bo_lo", [16, D], F32R)
        k("wg_hi", [P, E1], F32R); k("wg_lo", [P, E1], F32R)
        k("sel_f", [16, E1, P]); k("sel", [16, E1, P], F32R); k("iota8", [P, E1])
        k("mhalf", [P, NT]); k("eps", [P, NT])
        self.k = keep
        self.sem = sem
        self.setup_loaded = sem("c_setup_loaded")
        self.setup_skew = sem("c_setup_skew")
        self.setup_pool = sem("c_setup_pool")
        self.act_setup = sem("c_setup_act")
        self.setup_cols = sem("c_setup_cols")
        self.n_loads = 19

    def buffers(self, sb):
        b = {}
        def k(name, shape, dt=F32):
            b[name] = sb("c_" + name, shape, dt)
        k("c", [P, NT, K0N * D]); k("y", [P, NT * D])
        k("w1_hi", [P, E1, 2 * H1], F32R); k("w1_lo", [P, E1, 2 * H1], F32R)
        for u in range(2):
            k(f"x2{u}", [P, NT * D]); k(f"z{u}", [P, NT * D]); k(f"x3{u}", [P, NT * D])
            k(f"x3h{u}", [P, L], F32R); k(f"x3l{u}", [P, L], F32R); k(f"combT{u}", [16, L], F32R)
            k(f"outb{u}", [P, NT * D]); k(f"sgt{u}", [P, L]); k(f"sg{u}", [P, L]); k(f"g{u}", [P, 2, L])
        k("zh", [P, L], F32R); k("zl", [P, L], F32R); k("v", [P, NT, HID]); k("gateT", [P, 2, L]); k("qkT", [P, L])
        for n in ("qq", "lq", "qk", "lk"):
            k(n, [P, L])
        k("t", [P, NT, P]); k("ml", [P, NT, P]); k("off1", [P, 512]); k("off2", [P, 256]); k("goT", [P, 2, L])
        k("y3", [P, NT * D]); k("acc0", [P, 2, L]); k("acc1", [P, 2, L]); k("y4", [P, NT * D])
        for n in ("r", "a", "f"):
            k(f"st_{n}", [P, 6 * NT]); k(f"mv_{n}", [P, 2 * NT]); k(f"rs_{n}", [P, NT])
        k("rq", [P, NT])
        for n in ("lgs", "top", "dif", "s1", "s2", "zap", "mask", "em", "comb"):
            k(n, [P, NT * E1])
        k("zsum", [P, NT]); k("esum", [P, NT]); k("den", [P, NT])
        k("ch", [P, NT * 16]); k("chr", [P, NT * E1], F32R)
        self.b = b
        self.contrib_loaded, self.out_stored = self.sem("contrib_loaded"), [self.sem(f"out_stored{u}") for u in range(2)]
        self.w1_loaded = [self.sem(f"w1_loaded{q}") for q in range(2)]
        self.s = {n: self.sem("c_" + n) for n in """w1_mm w1_hi w1_lo sum_step y st_r mv_r rz_step z zT_mm zh zl
            v_mm gate_mm x2 sig5 prod5 quads diag_mm t1 t2 atd off_mm off2 av_mm go w_mm y3 st_a mv_a rs_step rf_step rs_a x3
            x3T_mm x3h x3l lg_mm gate_step sig_d combT_mm combT cb_mm b_mm a_mm sig g gc acc out_mm y4 st_f mv_f rs_f outb""".split()}

    def setup_sync(self, sp):
        k, i = self.k, self.inputs
        r = k["rows"]
        loads = [(r[0:1, :], i["ln_w"].unsqueeze(0)), (r[1:2, :], i["ln_b"].unsqueeze(0)),
                 (r[2:4, :], i["bh"][HID:2 * HID].rearrange("(h p) -> h p", p=P)), (r[4:5, :], i["bqk"].unsqueeze(0)),
                 (r[5:9, :], i["qk_w"]), (r[9:13, :], i["qk_b"]), (r[13:21, :], i["Wg"]),
                 (r[21:53, :], i["b1e"].rearrange("e (c p) -> (e c) p", p=P)), 
                 (k["whqk"][:, 0:2 * HID], i["Wh"]), (k["whqk"][:, 2 * HID:], i["Wqk"]),
                 (k["bh_row"][:, :], i["bh"][0:HID].unsqueeze(0)), (k["rel"][:, 0:NBUCKET], i["rel_table"].unsqueeze(0)),
                 (k["wout"][:, :, :], i["Wout"].rearrange("(h p) d -> p h d", p=P)), (k["wo"][:, :], i["Wo"]),
                 (k["bo16"][:, :], i["bo"].partition_broadcast(16))]
        loads += [(k["bout"][:, j, :], i["bout"].partition_broadcast(2)) for j in range(NT)]
        assert len(loads) == self.n_loads
        for dst, src in loads:
            sp.dma_start(dst, src).then_inc(self.setup_loaded, 16)

    def setup_sync_skew(self, sp):
        k, G2 = self.k, 2 * G - 1
        sp.wait_ge(self.setup_pool, self.pool_ext)
        for j in range(G):
            sp.dma_start(self.skew[j:j + 1, :], k["ext"][0:1, 0:G2]).then_inc(self.setup_skew, 16)
        sp.wait_ge(self.setup_skew, 16 * G)
        sp.wait_ge(self.setup_pool, self.pool_masked)
        src = bass.AP(tensor=self.skew.tensor, offset=G - 1, ap=[[G2 - 1, G], [1, G]])
        for q in range(P // G):
            sp.dma_start(k["biasT"][q * G:(q + 1) * G, q * G:(q + 1) * G], src).then_inc(self.setup_skew, 16)

    def setup_pool_early(self, pool):
        g, k = self.nc.gpsimd, self.k
        c = [0]

        def chain(ins):
            c[0] += 1
            ins.then_inc(self.setup_pool, 1)
            pool.wait_ge(self.setup_pool, c[0])
        pool.wait_ge(self.setup_loaded, 16 * self.n_loads)
        chain(g.memset(k["ext"][:, :], 0.0))
        for n0, cnt, b in bucket_runs():
            for n in range(n0, n0 + cnt):
                ins = g.tensor_scalar(k["ext"][:, G - 1 + n:G + n], k["rel"][:, b:b + 1], BIAS_SCALE, None, ALU.mult)
        chain(ins)
        self.pool_ext = c[0]
        chain(g.memset(k["biasT"][:, :], MASKED))
        self.pool_masked = c[0]
        chain(g.memset(k["ltmask"][:, :], 0.0))
        for q in range(P // G - 1):
            chain(g.memset(k["ltmask"][q * G:(q + 1) * G, (q + 1) * G:P], 1.0))
        g.memset(k["one12"][:, :], 1.0)
        g.iota(k["sel2"][:, :], pattern=[[0, 1]], base=0, channel_multiplier=-1, allow_small_or_imprecise_dtypes=True)
        g.memset(k["mhalf"][:, :], -0.5)
        g.memset(k["eps"][:, :], EPS)
        chain(g.memset(k["ones_f"][:, :], 1.0))
        g.tensor_copy(k["ones"][:, :], k["ones_f"][:, :])
        g.iota(k["iota8"][:, :], pattern=[[1, E1]], base=0, channel_multiplier=0, allow_small_or_imprecise_dtypes=True)
        chain(g.memset(k["sel_f"][:, :, :], 0.0))
        for o in (0, E1):
            chain(g.affine_select(out=k["sel_f"][:, :, :], in_=k["sel_f"][:, :, :], compare_op=ALU.not_equal, fill=1.0, base=-o,
                                  pattern=[[-1, E1], [0, P]], channel_multiplier=1))
        chain(g.tensor_copy(k["sel"][:, :, :], k["sel_f"][:, :, :]))
        g.tensor_copy(k["bout_hi"][:, :], k["bout"][:, :, :].rearrange("o j d -> o (j d)"))
        chain(g.tensor_copy(k["bo_hi"][:, :], k["bo16"][:, :]))
        chain(g.tensor_scalar(k["tmp2"][:, :], k["bout_hi"][:, :].bitcast(F32), k["sel2"][:, :], None, ALU.mult))
        g.tensor_tensor(k["bout_hl"][:, :], k["bout"][:, :, :].rearrange("o j d -> o (j d)"), k["tmp2"][:, :], ALU.add)
        chain(g.tensor_tensor(k["bo_lo"][:, :], k["bo16"][:, :], k["bo_hi"][:, :].bitcast(F32), ALU.subtract))
        self.pool_consts = c[0]
        self.pool_chain = chain
        self.pool_c = c

    def setup_pool_scale(self, pool):
        g, k, chain = self.nc.gpsimd, self.k, self.pool_chain
        pool.wait_ge(self.act_setup, 2)
        cols = k["cols"]
        chain(g.tensor_scalar(k["whqk"][:, :], k["whqk"][:, :], cols[:, 0:1], None, ALU.mult))
        chain(g.tensor_copy(k["wh_hi"][:, :], k["whqk"][:, :]))

    def setup_pool_late(self, pool):
        g, k, chain = self.nc.gpsimd, self.k, self.pool_chain
        cols = k["cols"]
        chain(g.tensor_tensor(k["wh_lo"][:, :], k["whqk"][:, :], k["wh_hi"][:, :].bitcast(F32), ALU.subtract))
        chain(g.tensor_tensor(k["bcols"][:, :], k["bcols"][:, :], cols[:, 2:5], ALU.add))
        g.tensor_scalar(k["quadw"][:, :], cols[:, 5:7], 1.0 / G, None, ALU.mult)
        g.tensor_scalar(k["quadb"][:, :], cols[:, 9:11], 1.0 / G, None, ALU.mult)
        chain(g.tensor_copy(k["vb_hi"][:, :], k["vb"][:, :]))
        chain(g.tensor_scalar(k["tmp2"][:, 0:HID], k["vb_hi"][:, :].bitcast(F32), k["sel2"][:, :], None, ALU.mult))
        chain(g.tensor_tensor(k["vb_hl"][:, :], k["vb"][:, :], k["tmp2"][:, 0:HID], ALU.add))
        chain(g.tensor_copy(k["wg_hi"][:, :], cols[:, 13:21]))
        chain(g.tensor_tensor(k["wg_lo"][:, :], cols[:, 13:21], k["wg_hi"][:, :].bitcast(F32), ALU.subtract))
        pool.wait_ge(self.setup_skew, 16 * (G + P // G))
        chain(g.affine_select(out=k["biasT"][:, :], in_=k["biasT"][:, :], compare_op=ALU.is_ge, fill=MASKED, base=0,
                              pattern=[[1, P]], channel_multiplier=-1))
        self.pool_done = self.pool_c[0]

    def setup_pe(self, pe):
        t, k, bank = self.nc.tensor, self.k, self.bank
        pe.wait_ge(self.setup_loaded, 16 * self.n_loads)
        pe.wait_ge(self.setup_pool, self.pool_consts)
        t.transpose(bank[3][:, 0:NROWS], k["rows"][:, :], self.ident[0:NROWS, 0:NROWS])
        for h in range(2):
            ins = t.transpose(bank[3][:, 128 + h * D:128 + (h + 1) * D], k["wo"][:, h * P:(h + 1) * P], self.ident[:, :])
        ins.then_inc(self.setup_cols, 1)
        pe.wait_ge(self.act_setup, 1)
        lnb = k["cols"][:, 1:2]
        t.matmul(bank[7][0:2, 0:HID], k["lnb2"][:, :], k["whqk"][:, 0:HID], start=True, stop=False)
        t.matmul(bank[7][0:2, 0:HID], k["one12"][:, :], k["bh_row"][:, :], start=False, stop=True)
        for c in range(3):
            ins = t.matmul(bank[3][:, c:c + 1], k["whqk"][:, HID + c * P:HID + (c + 1) * P], lnb, start=True, stop=True)
        ins.then_inc(self.setup_cols, 1)

    def setup_act(self, act):
        a, k, bank = self.nc.scalar, self.k, self.bank
        act.wait_ge(self.setup_cols, 1)
        a.copy(k["cols"][:, :], bank[3][:, 0:NROWS])
        for row in range(2):
            a.copy(k["lnb2"][:, row:row + 1], bank[3][:, 1:2])
        a.copy(k["woT"][:, :, :], bank[3][:, 128:128 + 2 * D].rearrange("p (h d) -> p h d", h=2)).then_inc(self.act_setup, 1)
        act.wait_ge(self.setup_cols, 2)
        a.copy(k["vb"][:, :], bank[7][0:2, 0:HID])
        a.copy(k["bcols"][:, :], bank[3][:, 0:3]).then_inc(self.act_setup, 1)

    @staticmethod
    def bodies(eng, body):
        body(eng, 0, 1, r=0)
        body(eng, 1, 0, r=1, a=0)
        body(eng, 0, 1, r=2, a=1, f=0)
        with eng.Fori(0, (B - 4) // 2) as i:
            k = 2 * i
            body(eng, 1, 0, r=k + 3, a=k + 2, f=k + 1, t=k)
            body(eng, 0, 1, r=k + 4, a=k + 3, f=k + 2, t=k + 1)
        body(eng, 1, 0, r=B - 1, a=B - 2, f=B - 3, t=B - 4)
        body(eng, 0, 1, a=B - 1, f=B - 2, t=B - 3)
        body(eng, 1, 0, f=B - 1, t=B - 2)
        body(eng, 0, 1, t=B - 1)

    def sync(self, sp):
        b, s = self.b, self.s
        sp.wait_ge(self.rows_scattered, 16 * EP)
        self.load_contrib(sp, 0)
        for q in range(4):
            if q >= 2:
                sp.wait_ge(s["w1_mm"], 2 * (q - 1))
            dst = b[f"g{q % 2}"][:, :, :].rearrange("p h l -> p (h l)").rearrange("p (n d) -> p n d", d=D)
            sp.dma_start(dst, self.inputs["W1e"][2 * q:2 * q + 2].rearrange("e (c p) d -> p (e c) d", p=P)).then_inc(self.w1_loaded[q % 2], 16)

        def body(sp, ur, ua, r=None, a=None, f=None, t=None):
            if r is not None and not (isinstance(r, int) and r == B - 1):
                sp.wait_ge(s["sum_step"], 3 * r + 3)
                self.load_contrib(sp, r + 1)
            if t is not None:
                sp.wait_ge(s["outb"], t + 1)
                self.store_out(sp, t, ua)

        self.bodies(sp, body)
        for u in range(2):
            sp.wait_ge(self.out_stored[u], 16 * (B // 2) + 16)

    def load_contrib(self, sp, r):
        src = self.contrib_view[r] if isinstance(r, int) else self.contrib_view[bass.ds(r, 1)].rearrange("o p j d -> (o p) j d")
        sp.dma_start(self.b["c"][:, :, :], src).then_inc(self.contrib_loaded, 16)

    def store_out(self, sp, f, u):
        dst = self.out_view[f] if isinstance(f, int) else self.out_view[bass.ds(f, 1)].rearrange("o p j d -> (o p) j d")
        sp.dma_start(dst, self.b[f"outb{u}"][:, :].rearrange("p (j d) -> p j d", d=D)).then_inc(self.out_stored[u], 16)

    def pool(self, pool):
        g, b, s, k = self.nc.gpsimd, self.b, self.s, self.k

        def rstd(name, n, step, at, done):
            var = b["mv_" + name][:, :].rearrange("p (j t) -> p j t", t=2)[:, :, 1]
            pool.wait_ge(s["mv_" + name], n)
            g.tensor_tensor(b["rs_" + name][:, :], var, k["eps"][:, :], ALU.add).then_inc(s[step], 1)
            pool.wait_ge(s[step], at)
            g.tensor_tensor(b["rs_" + name][:, :], b["rs_" + name][:, :], k["mhalf"][:, :], ALU.pow).then_inc(s[done], 1)

        def add_expert(f, uf, e):
            pool.wait_ge(s["gc"], 8 * f + (e + 1))
            if e >= 2:
                pool.wait_ge(s["acc"], 7 * f + (e - 1))
            acc = b[f"acc{uf}"][:, :, :]
            g.tensor_tensor(acc, acc, b[f"g{e % 2}"][:, :, :], ALU.add).then_inc(s["acc"], 1)

        def body(pool, ur, ua, r=None, a=None, f=None, t=None):
            c = b["c"]
            uf = ur
            summed = r is None or first(r)
            if not summed:
                pool.wait_ge(self.contrib_loaded, 16 * r + 16)
                g.tensor_tensor(c[:, :, 0:512], c[:, :, 0:512], c[:, :, 512:1024], ALU.add).then_inc(s["sum_step"], 1)
            if f is not None:
                add_expert(f, uf, 1)
            if t is not None:
                rstd("f", t + 1, "rf_step", t + 1, "rs_f")
            if not summed:
                pool.wait_ge(s["sum_step"], 3 * r + 1)
                g.tensor_tensor(c[:, :, 0:256], c[:, :, 0:256], c[:, :, 256:512], ALU.add).then_inc(s["sum_step"], 1)
                pool.wait_ge(s["sum_step"], 3 * r + 2)
                yv = b["y"][:, :].rearrange("p (j d) -> p j d", d=D)
                g.tensor_tensor(yv, c[:, :, 0:128], c[:, :, 128:256], ALU.add).then_inc(s["sum_step"], 1)
            if f is not None:
                add_expert(f, uf, 2)
            if not summed:
                pool.wait_ge(s["sum_step"], 3 * r + 3)
                bs = self.base_all[:, r, :] if isinstance(r, int) else self.base_all[:, bass.ds(r, 1), :].rearrange("p o d -> p (o d)")
                g.tensor_tensor(b["y"][:, :], b["y"][:, :], bs, ALU.add).then_inc(s["y"], 1)
            if f is not None:
                add_expert(f, uf, 3)
            if r is not None:
                n = r + 1
                rstd("r", n, "rz_step", 7 * r + 1, "rz_step")
                y3d = b["y"][:, :].rearrange("p (j d) -> p j d", d=D)
                mv = b["mv_r"][:, :].rearrange("p (j t) -> p j t", t=2)
                var = mv[:, :, 1]
                g.tensor_tensor(y3d, y3d, bcast_last(mv[:, :, 0], D), ALU.subtract).then_inc(s["rz_step"], 1)
                pool.wait_ge(s["rz_step"], 7 * r + 3)
                x2 = b[f"x2{ur}"][:, :].rearrange("p (j d) -> p j d", d=D)
                g.tensor_tensor(x2, y3d, bcast_last(b["rs_r"][:, :], D), ALU.mult).then_inc(s["x2"], 1)
                if not first(r):
                    pool.wait_ge(s["z"], r)
                g.tensor_tensor(b["rq"][:, :], b["rs_r"][:, :], b["rs_r"][:, :], ALU.mult).then_inc(s["rz_step"], 1)
                pool.wait_ge(s["rz_step"], 7 * r + 4)
                g.tensor_tensor(b["rq"][:, :], b["rq"][:, :], var, ALU.mult).then_inc(s["rz_step"], 1)
                pool.wait_ge(s["rz_step"], 7 * r + 5)
                g.tensor_tensor(b["rq"][:, :], b["rq"][:, :], k["eps"][:, :], ALU.add).then_inc(s["rz_step"], 1)
                pool.wait_ge(s["rz_step"], 7 * r + 6)
                g.tensor_tensor(b["rq"][:, :], b["rq"][:, :], k["mhalf"][:, :], ALU.pow).then_inc(s["rz_step"], 1)
            if a is not None:
                rstd("a", a + 1, "rs_step", a + 1, "rs_a")
            if f is not None:
                add_expert(f, uf, 4)
                add_expert(f, uf, 5)
                add_expert(f, uf, 6)
                add_expert(f, uf, 7)

        self.bodies(pool, body)

    def act(self, act):
        a_, b, s, k, bank = self.nc.scalar, self.b, self.s, self.k, self.bank
        cols, SIG = k["cols"], ACT.Sigmoid
        X, Y, Z = bank[5], bank[6], bank[7]

        for q in range(8):
            act.wait_ge(s["w1_mm"], q + 1)
            a_.copy(b["w1_hi"][:, q, :], bank[q % 4][:, :]).then_inc(s["w1_hi"], 1)

        def gate(a, step, src, bias=None):
            if step >= 2:
                act.wait_ge(s["prod5"], 5 * a + (step - 1))
            kw = {} if bias is None else {"bias": bias}
            a_.activation(b[f"sgt{step % 2}"][:, :], src[:, :], SIG, **kw).then_inc(s["sig5"], 1)

        def sig(f, kk):
            e, h = divmod(kk, 2)
            act.wait_ge(s["b_mm"], 16 * f + (kk + 1))
            if kk >= 2 or not first(f):
                act.wait_ge(s["g"], 16 * f + (kk - 1))
            col = 21 + 4 * e + 2 + h
            a_.activation(b[f"sg{kk % 2}"][:, :], bank[2 * (kk % 2)][:, :], SIG, bias=cols[:, col:col + 1]).then_inc(s["sig"], 1)

        def body(act, ur, ua, r=None, a=None, f=None, t=None):
            uf = ur
            for q in range(2 * E1):
                if f is not None:
                    sig(f, q)
                if a is not None and q == AT["gate"]:
                    act.wait_ge(s["gate_mm"], 3 * a + 1)
                    gate(a, 0, X, k["bcols"][:, 0:1])
                if f is not None and q == 2:
                    act.wait_ge(s["combT_mm"], f + 1)
                    a_.copy(b[f"combT{uf}"][:, :], Y[0:16, :]).then_inc(s["combT"], 1)
                if a is not None:
                    if q == AT["zT"]:
                        act.wait_ge(s["zT_mm"], a + 1)
                        a_.copy(b["zh"][:, :], X[:, :]).then_inc(s["zh"], 1)
                    if q == AT["gate"]:
                        act.wait_ge(s["gate_mm"], 3 * a + 2)
                        gate(a, 1, Z, k["bcols"][:, 2:3])
                    if q == AT["v"]:
                        act.wait_ge(s["v_mm"], 2 * a + 1)
                        gate(a, 3, Z)
                        act.wait_ge(s["v_mm"], 2 * a + 2)
                        gate(a, 4, Y)
                    if q == AT["quads"]:
                        act.wait_ge(s["prod5"], 5 * a + 2)
                        for n, w, o in (("qq", k["quadw"][:, 0:1], k["quadb"][:, 0:1]), ("lq", k["quadw"][:, 1:2], k["quadb"][:, 1:2]),
                                        ("qk", cols[:, 7:8], cols[:, 11:12]), ("lk", cols[:, 8:9], cols[:, 12:13])):
                            ins = a_.activation(b[n][:, :], b["qkT"][:, :], ACT.Identity, scale=w, bias=o)
                        ins.then_inc(s["quads"], 1)
                    if q == AT["gate2"]:
                        act.wait_ge(s["gate_mm"], 3 * a + 3)
                        gate(a, 2, X, k["bcols"][:, 1:2])
                    if q == AT["sim"]:
                        act.wait_ge(s["off_mm"], 2 * a + 1)
                        a_.copy(b["off1"][:, :], Z[:, :])
                    if q == AT["off"]:
                        act.wait_ge(s["off_mm"], 2 * a + 2)
                        a_.copy(b["off2"][:, :], X[:, 0:256]).then_inc(s["off2"], 1)
                    if q == AT["x3T"]:
                        act.wait_ge(s["x3T_mm"], a + 1)
                        a_.copy(b[f"x3h{ua}"][:, :], Y[:, :]).then_inc(s["x3h"], 1)
                    if q == AT["lg"] + 1:
                        act.wait_ge(s["gate_step"], GATE_STEPS * a + 3)
                        a_.activation(b["s1"][:, :], b["dif"][:, :], SIG)
                        a_.activation(b["s2"][:, :], b["dif"][:, :], SIG, scale=-1.0).then_inc(s["sig_d"], 1)
                if r is not None and q == AT["z"]:
                    act.wait_ge(s["rz_step"], 7 * r + 7)
                    act.wait_ge(s["x2"], r + 1)
                    for j in range(NT):
                        c = slice(j * D, (j + 1) * D)
                        ins = a_.activation(b[f"z{ur}"][:, c], b[f"x2{ur}"][:, c], ACT.Identity, scale=b["rq"][:, j:j + 1])
                    ins.then_inc(s["z"], 1)

        self.bodies(act, body)

    def dve(self, dve):
        v, b, s, k, bank = self.nc.vector, self.b, self.s, self.k, self.bank
        cols = k["cols"]
        X, Y, Z = bank[5], bank[6], bank[7]

        def stats(name, src, n):
            st = b["st_" + name][:, :].rearrange("p (j t) -> p j t", t=6)
            mv = b["mv_" + name][:, :].rearrange("p (j t) -> p j t", t=2)
            for j in range(NT):
                ins = v.bn_stats(st[:, j, :], src[:, j * D:(j + 1) * D])
            ins.then_inc(s["st_" + name], 1)
            dve.wait_ge(s["st_" + name], n)
            v.memset(self.landing(), 0.0)
            for j in range(NT):
                ins = v.bn_aggr(mv[:, j, :], st[:, j, :])
            ins.then_inc(s["mv_" + name], 1)

        c = b["c"]
        dve.wait_ge(self.contrib_loaded, 16)
        v.tensor_tensor(c[:, :, 0:512], c[:, :, 0:512], c[:, :, 512:1024], ALU.add).then_inc(s["sum_step"], 1)
        dve.wait_ge(s["sum_step"], 1)
        v.tensor_tensor(c[:, :, 0:256], c[:, :, 0:256], c[:, :, 256:512], ALU.add).then_inc(s["sum_step"], 1)
        dve.wait_ge(s["sum_step"], 2)
        v.tensor_tensor(b["y"][:, :].rearrange("p (j d) -> p j d", d=D), c[:, :, 0:128], c[:, :, 128:256], ALU.add).then_inc(s["sum_step"], 1)
        dve.wait_ge(s["sum_step"], 3)
        dve.wait_ge(self.base_sb, B)
        v.tensor_tensor(b["y"][:, :], b["y"][:, :], self.base_all[:, 0, :], ALU.add).then_inc(s["y"], 1)
        dve.wait_ge(s["y"], 1)
        v.memset(self.landing(), 0.0)
        stats("r", b["y"], 1)

        for q in range(8):
            dve.wait_ge(s["w1_hi"], q + 1)
            v.tensor_tensor(b["w1_lo"][:, q, :], bank[q % 4][:, :], b["w1_hi"][:, q, :].bitcast(F32), ALU.subtract).then_inc(s["w1_lo"], 1)
        for u in range(2):
            v.memset(self.landing(), 0.0).then_inc(self.out_stored[u], 16)
        dve.wait_ge(self.setup_pool, self.pool_done)

        def norm(name, dst, src, rs, done):
            mv = b["mv_" + name][:, :].rearrange("p (j t) -> p j t", t=2)
            for j in range(NT):
                ins = v.tensor_scalar(dst[:, j * D:(j + 1) * D], src[:, j * D:(j + 1) * D], mv[:, j, 0:1], rs[:, j:j + 1], ALU.subtract, ALU.mult)
            if done is not None:
                ins.then_inc(done, 1)

        def prod(a, step, src, dst, bias=None):
            dve.wait_ge(s["sig5"], 5 * a + (step + 1))
            sg = b[f"sgt{step % 2}"][:, :]
            if bias is None:
                v.tensor_tensor(dst, src[:, :], sg, ALU.mult).then_inc(s["prod5"], 1)
            else:
                v.scalar_tensor_tensor(out=dst, in0=src[:, :], scalar=bias, in1=sg, op0=ALU.add, op1=ALU.mult).then_inc(s["prod5"], 1)

        def half(f, kk):
            e, h = divmod(kk, 2)
            dve.wait_ge(s["sig"], 16 * f + (kk + 1))
            dve.wait_ge(s["a_mm"], 16 * f + (kk + 1))
            if h == 0 and e >= 3:
                dve.wait_ge(s["acc"], 7 * f + (e - 2))
            if h == 0 and e < 2 and not first(f):
                dve.wait_ge(s["acc"], 7 * f + (e - 1))
            col = 21 + 4 * e + h
            v.scalar_tensor_tensor(out=b[f"g{e % 2}"][:, h, :], in0=bank[2 * (kk % 2) + 1][:, :], scalar=cols[:, col:col + 1],
                                   in1=b[f"sg{kk % 2}"][:, :], op0=ALU.add, op1=ALU.mult).then_inc(s["g"], 1)

        def weigh(f, uf, e):
            dve.wait_ge(s["g"], 16 * f + (2 * e + 2))
            dve.wait_ge(s["cb_mm"], 8 * f + (e + 1))
            dst = b[f"acc{uf}"] if e == 0 else b[f"g{e % 2}"]
            v.tensor_tensor(dst[:, :, :], b[f"g{e % 2}"][:, :, :], bcast_mid(bank[4][:, :], 2), ALU.mult).then_inc(s["gc"], 1)

        def gating(a, step):
            def t3(n):
                return b[n][:, :].rearrange("p (j e) -> p j e", e=E1)

            if step == 0:
                dve.wait_ge(s["lg_mm"], a + 1)
                v.tensor_copy(b["lgs"][:, :], Z[:, 0:NT * E1]).then_inc(s["gate_step"], 1)
                return
            dve.wait_ge(s["gate_step"], GATE_STEPS * a + step)
            if step == 1:
                v.memset(self.landing(), 0.0)
                for j in range(NT):
                    ins = v.max(t3("top")[:, j, :], t3("lgs")[:, j, :])
            elif step == 2:
                ins = v.tensor_tensor(t3("dif"), t3("lgs"), bcast_last(t3("top")[:, :, 0], E1), ALU.subtract)
            elif step == 3:
                ins = v.memset(t3("top")[:, :, 2:E1], STRUCK)
            elif step == 4:
                v.memset(self.landing(), 0.0)
                for j in range(NT):
                    ins = v.match_replace(t3("zap")[:, j, :], t3("top")[:, j, :], t3("lgs")[:, j, :], NEG)
            elif step == 5:
                ins = v.tensor_tensor(b["mask"][:, :], b["zap"][:, :], b["lgs"][:, :], ALU.not_equal)
            elif step == 6:
                dve.wait_ge(s["sig_d"], a + 1)
                ins = v.reciprocal(b["s2"][:, :], b["s2"][:, :])
            elif step == 7:
                ins = v.tensor_tensor(b["s1"][:, :], b["s1"][:, :], b["s2"][:, :], ALU.mult)
            elif step == 8:
                v.tensor_reduce(b["zsum"][:, :], t3("s1"), AX.X, ALU.add)
                ins = v.tensor_tensor(b["em"][:, :], b["s1"][:, :], b["mask"][:, :], ALU.mult)
            elif step == 9:
                ins = v.tensor_reduce(b["esum"][:, :], t3("em"), AX.X, ALU.add)
            elif step == 10:
                ins = v.scalar_tensor_tensor(out=b["den"][:, :], in0=b["zsum"][:, :], scalar=1e-9, in1=b["esum"][:, :], op0=ALU.mult, op1=ALU.add)
            elif step == 11:
                ins = v.reciprocal(b["den"][:, :], b["den"][:, :])
            elif step == 12:
                ins = v.tensor_tensor(t3("comb"), t3("em"), bcast_last(b["den"][:, :], E1), ALU.mult)
            elif step == 13:
                ins = v.tensor_copy(b["chr"][:, :], b["comb"][:, :])
            elif step == 14:
                ch = b["ch"][:, :].rearrange("p (j e) -> p j e", e=16)
                v.tensor_copy(ch[:, :, 0:E1], t3("chr").bitcast(F32))
                ins = v.tensor_tensor(ch[:, :, E1:16], t3("comb"), t3("chr").bitcast(F32), ALU.subtract)
            ins.then_inc(s["gate_step"], 1)

        def body(dve, ur, ua, r=None, a=None, f=None, t=None):
            uf = ur
            for q in range(2 * E1):
                ahead, middle, behind = GATING.get(q, ((), (), ())) if a is not None else ((), (), ())
                for step in ahead:
                    gating(a, step)
                if f is not None:
                    before, after = GATING_NEXT.get(q, ((), ()))
                    for step in before:
                        gating(f, step)
                    half(f, q)
                    for step in after:
                        gating(f, step)
                if a is not None and q == AT["x3"]:
                    dve.wait_ge(s["rs_a"], a + 1)
                    norm("a", b[f"x3{ua}"], b["y3"], b["rs_a"], s["x3"])
                for step in middle:
                    gating(a, step)
                if f is not None and q in WEIGH:
                    weigh(f, uf, WEIGH[q])
                for step in behind:
                    gating(a, step)
                if t is not None:
                    if q == AT["y4"]:
                        dve.wait_ge(s["out_mm"], t + 1)
                        v.tensor_tensor(b["y4"][:, :], b[f"x3{ua}"][:, :], Y[:, :], ALU.add).then_inc(s["y4"], 1)
                        dve.wait_ge(s["y4"], t + 1)
                        v.memset(self.landing(), 0.0)
                        stats("f", b["y4"], t + 1)
                    if q == AT["outb"]:
                        dve.wait_ge(s["rs_f"], t + 1)
                        dve.wait_ge(self.out_stored[ua], 8 * (t - ua) + 16)
                        norm("f", b[f"outb{ua}"], b["y4"], b["rs_f"], s["outb"])
                if a is not None:
                    if q == AT["zT"]:
                        dve.wait_ge(s["zh"], a + 1)
                        v.tensor_tensor(b["zl"][:, :], X[:, :], b["zh"][:, :].bitcast(F32), ALU.subtract).then_inc(s["zl"], 1)
                    if q == AT["gate"]:
                        prod(a, 0, X, b["gateT"][:, 0, :], k["bcols"][:, 0:1])
                        prod(a, 1, Z, b["qkT"][:, :], k["bcols"][:, 2:3])
                    if q == AT["v"]:
                        prod(a, 3, Z, b["v"][:, 2:4, :].rearrange("p j e -> p (j e)"))
                        prod(a, 4, Y, b["v"][:, 0:2, :].rearrange("p j e -> p (j e)"))
                    if q == AT["gate2"]:
                        prod(a, 2, X, b["gateT"][:, 1, :], k["bcols"][:, 1:2])
                    if q == AT["sim"]:
                        dve.wait_ge(s["diag_mm"], a + 1)
                        t_, ml = b["t"][:, :, :], b["ml"][:, :, :]
                        v.tensor_tensor(t_, X[:, :].rearrange("p (j i) -> p j i", i=P), bcast_mid(k["biasT"][:, :], NT), ALU.add).then_inc(s["t1"], 1)
                        v.tensor_tensor(ml, Y[:, :].rearrange("p (j i) -> p j i", i=P), bcast_mid(k["ltmask"][:, :], NT), ALU.mult)
                        dve.wait_ge(s["t1"], a + 1)
                        v.scalar_tensor_tensor(out=t_, in0=t_, scalar=0.0, in1=t_, op0=ALU.max, op1=ALU.mult).then_inc(s["t2"], 1)
                        dve.wait_ge(s["t2"], a + 1)
                        v.tensor_tensor(t_, t_, ml, ALU.add).then_inc(s["atd"], 1)
                    if q == AT["av"]:
                        for h, src in ((0, Y), (1, Z)):
                            dve.wait_ge(s["av_mm"], 2 * a + (h + 1))
                            v.tensor_tensor(b["goT"][:, h, :], src[:, :], b["gateT"][:, h, :], ALU.mult).then_inc(s["go"], 1)
                    if q == AT["w"]:
                        dve.wait_ge(s["w_mm"], a + 1)
                        v.scalar_tensor_tensor(out=b["y3"][:, :], in0=b[f"x2{ua}"][:, :], scalar=2.0, in1=X[:, :], op0=ALU.mult, op1=ALU.add).then_inc(s["y3"], 1)
                        dve.wait_ge(s["y3"], a + 1)
                        v.memset(self.landing(), 0.0)
                        stats("a", b["y3"], a + 1)
                    if q == AT["x3T"]:
                        dve.wait_ge(s["x3h"], a + 1)
                        v.tensor_tensor(b[f"x3l{ua}"][:, :], Y[:, :], b[f"x3h{ua}"][:, :].bitcast(F32), ALU.subtract).then_inc(s["x3l"], 1)
                if r is not None and q == AT["y"] and not first(r):
                    dve.wait_ge(s["y"], r + 1)
                    v.memset(self.landing(), 0.0)
                    stats("r", b["y"], r + 1)
        self.bodies(dve, body)

    def pe(self, pe):
        t, b, s, k, bank = self.nc.tensor, self.b, self.s, self.k, self.bank
        X, Y, Z = bank[5], bank[6], bank[7]
        ident = self.ident

        def split3(dst, w_hi, w_lo, x_hi, x_lo, start=True, stop=True):
            t.matmul(dst, w_hi, x_hi, start=start, stop=False)
            t.matmul(dst, w_hi, x_lo, start=False, stop=False)
            return t.matmul(dst, w_lo, x_hi, start=False, stop=stop)

        pe.wait_ge(self.y_sb, EP)
        for q in range(8):
            if q % 2 == 0:
                pe.wait_ge(self.w1_loaded[(q // 2) % 2], 16 * (q // 4 + 1))
            if q >= 4:
                pe.wait_ge(s["w1_lo"], q - 3)
            src = b[f"g{(q // 2) % 2}"][:, :, :].rearrange("p h l -> p (h l)")
            for c in range(4):
                o = ((q % 2) * 4 + c) * D
                ins = t.transpose(bank[q % 4][:, c * P:(c + 1) * P], src[:, o:o + D], ident[:, :])
            ins.then_inc(s["w1_mm"], 1)
        pe.wait_ge(s["w1_lo"], 8)
        pe.wait_ge(self.setup_pool, self.pool_done)

        def up(f, uf, kk):
            e, h = divmod(kk, 2)
            xh, xl = b[f"x3h{uf}"][:, :], b[f"x3l{uf}"][:, :]
            for part, o, done in (("b", H1, "b_mm"), ("a", 0, "a_mm")):
                if kk >= 2 or not first(f):
                    pe.wait_ge(s["sig" if part == "b" else "g"], 16 * f + (kk - 1))
                w = slice(o + h * P, o + (h + 1) * P)
                split3(bank[2 * (kk % 2) + (part == "a")][:, :], b["w1_hi"][:, e, w], b["w1_lo"][:, e, w], xh, xl).then_inc(s[done], 1)

        def spread(f, uf, e):
            if e == 0:
                pe.wait_ge(s["combT"], f + 1)
            if e > 0 or not first(f):
                pe.wait_ge(s["gc"], 8 * f + e)
            t.matmul(bank[4][:, :], k["sel"][:, e, :], b[f"combT{uf}"][:, :], start=True, stop=True).then_inc(s["cb_mm"], 1)

        def body(pe, ur, ua, r=None, a=None, f=None, t=None):
            t_, t = t, self.nc.tensor
            uf = ur
            zh, zl = b["zh"], b["zl"]
            hi, lo = k["wh_hi"], k["wh_lo"]
            for q in range(2 * E1):
                if f is not None:
                    up(f, uf, q)
                if a is not None and q == AT["zT"]:
                    pe.wait_ge(s["z"], a + 1)
                    for j in range(NT):
                        ins = t.transpose(X[:, j * P:(j + 1) * P], b[f"z{ua}"][:, j * D:(j + 1) * D], ident[:, :])
                    ins.then_inc(s["zT_mm"], 1)
                if a is not None and q == AT["gate"]:
                    pe.wait_ge(s["zl"], a + 1)
                    split3(X[:, :], hi[:, HID:HID + P], lo[:, HID:HID + P], zh[:, :], zl[:, :]).then_inc(s["gate_mm"], 1)
                if f is not None and q == 2:
                    pe.wait_ge(s["gate_step"], GATE_STEPS * f + GATE_STEPS)
                    for j in range(NT):
                        ins = t.transpose(Y[0:16, j * P:(j + 1) * P], b["ch"][:, j * 16:(j + 1) * 16], ident[:, :])
                    ins.then_inc(s["combT_mm"], 1)
                if a is not None and q == AT["gate"]:
                    split3(Z[:, :], hi[:, 2 * HID:], lo[:, 2 * HID:], zh[:, :], zl[:, :]).then_inc(s["gate_mm"], 1)
                if f is not None and q in WEIGH:
                    spread(f, uf, WEIGH[q])
                if t_ is not None and q == AT["out"]:
                    pe.wait_ge(s["acc"], 7 * t_ + 7)
                    cb, acc = b[f"combT{ua}"], b[f"acc{ua}"]
                    for j in range(NT):
                        tok = slice(j * P, (j + 1) * P)
                        dst = Y[:, j * D:(j + 1) * D]
                        t.matmul(dst, cb[:, tok], k["bo_hi"][:, :], start=True, stop=False)
                        t.matmul(dst, cb[:, tok], k["bo_lo"][:, :], start=False, stop=False)
                        t.matmul(dst, acc[:, 0, tok], k["woT"][:, 0, :], start=False, stop=False)
                        ins = t.matmul(dst, acc[:, 1, tok], k["woT"][:, 1, :], start=False, stop=True)
                    ins.then_inc(s["out_mm"], 1)
                if a is not None:
                    if q == AT["v"]:
                        pe.wait_ge(s["prod5"], 5 * a + 2)
                        for j in (2, 3, 0, 1):
                            if j == 0 and t_ is not None:
                                pe.wait_ge(s["y4"], t_ + 1)
                            dst = (Y, Z)[j // 2][:, (j % 2) * HID:(j % 2 + 1) * HID]
                            tok = slice(j * P, (j + 1) * P)
                            t.matmul(dst, k["ones"][:, :], k["vb_hl"][:, :], start=True, stop=False)
                            ins = split3(dst, zh[:, tok], zl[:, tok], hi[:, 0:HID], lo[:, 0:HID], start=False)
                            if j % 2:
                                ins.then_inc(s["v_mm"], 1)
                    if q == AT["gate2"]:
                        pe.wait_ge(s["prod5"], 5 * a + 1)
                        split3(X[:, :], hi[:, HID + P:2 * HID], lo[:, HID + P:2 * HID], zh[:, :], zl[:, :]).then_inc(s["gate_mm"], 1)
                    if q == AT["sim"]:
                        pe.wait_ge(s["quads"], a + 1)
                        pe.wait_ge(s["prod5"], 5 * a + 5)
                        for j in range(NT):
                            tok = slice(j * P, (j + 1) * P)
                            t.matmul(X[:, tok], b["qk"][:, tok], b["qq"][:, tok], start=True, stop=True)
                            ins = t.matmul(Y[:, tok], b["lk"][:, tok], b["lq"][:, tok], start=True, stop=True)
                        ins.then_inc(s["diag_mm"], 1)
                        t.matmul(Z[:, 0:384], b["lk"][:, 0:P], b["lq"][:, P:L], start=True, stop=True)
                        t.matmul(Z[:, 384:512], b["lk"][:, 2 * P:3 * P], b["lq"][:, 3 * P:L], start=True, stop=True).then_inc(s["off_mm"], 1)
                    if q == AT["off"]:
                        pe.wait_ge(s["t1"], a + 1)
                        t.matmul(X[:, 0:256], b["lk"][:, P:2 * P], b["lq"][:, 2 * P:L], start=True, stop=True).then_inc(s["off_mm"], 1)
                    if q == AT["av"]:
                        pe.wait_ge(s["atd"], a + 1)
                        pe.wait_ge(s["off2"], a + 1)
                        for h, dst in ((0, Y), (1, Z)):
                            c = slice(h * P, (h + 1) * P)
                            t.matmul(dst[:, P:L], b["v"][:, 0, c], b["off1"][:, 0:384], start=True, stop=False, skip_group_check=True)
                            t.matmul(dst[:, 0:P], b["v"][:, 0, c], b["t"][:, 0, :], start=False, stop=False, skip_group_check=True)
                            t.matmul(dst[:, 2 * P:L], b["v"][:, 1, c], b["off2"][:, 0:256], start=False, stop=False, skip_group_check=True)
                            t.matmul(dst[:, 3 * P:L], b["v"][:, 2, c], b["off1"][:, 384:512], start=False, stop=False, skip_group_check=True)
                            for j in range(1, NT):
                                ins = t.matmul(dst[:, j * P:(j + 1) * P], b["v"][:, j, c], b["t"][:, j, :], start=False, stop=(j == NT - 1), skip_group_check=True)
                            ins.then_inc(s["av_mm"], 1)
                    if q == AT["w"]:
                        t.matmul(X[:, :], k["ones"][:, :], k["bout_hl"][:, :], start=True, stop=False, skip_group_check=True)
                        pe.wait_ge(s["go"], 2 * a + 2)
                        for j in range(NT):
                            for h in range(2):
                                ins = t.matmul(X[:, j * D:(j + 1) * D], b["goT"][:, h, j * P:(j + 1) * P], k["wout"][:, h, :],
                                               start=False, stop=(h == 1), skip_group_check=True)
                        ins.then_inc(s["w_mm"], 1)
                    if q == AT["x3T"]:
                        pe.wait_ge(s["x3"], a + 1)
                        for j in range(NT):
                            ins = t.transpose(Y[:, j * P:(j + 1) * P], b[f"x3{ua}"][:, j * D:(j + 1) * D], ident[:, :])
                        ins.then_inc(s["x3T_mm"], 1)
                    if q == AT["lg"]:
                        pe.wait_ge(s["x3l"], a + 1)
                        xh, xl = b[f"x3h{ua}"], b[f"x3l{ua}"]
                        for j in range(NT):
                            tok = slice(j * P, (j + 1) * P)
                            ins = split3(Z[:, j * E1:(j + 1) * E1], xh[:, tok], xl[:, tok], k["wg_hi"][:, :], k["wg_lo"][:, :])
                        ins.then_inc(s["lg_mm"], 1)

        self.bodies(pe, body)


def build(nc, x_in, Wq, Wm, W1, W2, g1, b1, g2, b2, router_w, w_gate, w_up, w_down, ws_gate_up, ws_down,
          ln_w, ln_b, Wh, bh, Wqk, bqk, qk_w, qk_b, rel_table, Wout, bout, Wg, W1e, b1e, Wo, bo, out):
    ctx = ExitStack()
    with ctx:
        def scope():
            return ExitStack()

        def sb(name, shape, dt=F32, where=ctx):
            return where.enter_context(nc.sbuf_tensor(name, shape, dt))

        def sem(name):
            return ctx.enter_context(nc.semaphore(name))

        table = nc.dram_tensor("token_rows", (T + 1, ROW), F32, kind="Internal").ap()
        contrib = nc.dram_tensor("routed_rows", (NKEY, D), F32, kind="Internal").ap()

        ident = sb("ident", [P, P])
        base_all = sb("base_all", [P, B, NT * D])
        landing_all = sb("landing", [P, 96])
        cells = iter(range(96))

        def landing():
            c = next(cells)
            return landing_all[:, c:c + 1]

        C = StageC(nc, sb, sem)
        AB = scope()
        x1T_all = sb("x1T_all", [P, T], where=AB)
        y_all = x1T_all
        rows_all = sb("rows_all", [P, EP * ROW], where=AB)
        ZCOLS = 4096
        zeros = rows_all[:, 0:ZCOLS]
        keyT = sb("keyT", [P, T // 2], where=AB)
        cand = sb("cand", [P, CAP], where=AB)
        both = sb("both", [E0, 2 * CAP], where=AB)
        slot_key = sb("slot_key", [E0, CAP], where=AB)
        dest_row = sb("dest_row", [P, EP], U32, where=AB)
        tok_row = sb("tok_row", [P, EP], U32, where=AB)
        wgu_e = sb("wgu_early", [P, 2 * EP_EARLY, 2, F0], where=AB)
        wd_e = sb("wd_early", [F0, 2 * EP_EARLY, D], where=AB)
        wsgu_sb = sb("wsgu_sb", [P, 2 * F0], where=AB)
        wsd_sb = sb("wsd_sb", [F0, D], where=AB)
        xgT = [sb(f"xgT{b}", [P, P], where=AB) for b in range(2)]
        sil = [sb(f"sil{b}", [F0, P], where=AB) for b in range(2)]
        hexp = [sb(f"hexp{b}", [F0, P], where=AB) for b in range(2)]
        A = scope()
        Wq_sb = sb("Wq_sb", [P, D], where=A)
        Wm_sb = sb("Wm_sb", [P, D], where=A)
        W1_sb = sb("W1_sb", [P, 2 * D], where=A)
        W2_sb = sb("W2_sb", [P, 2, D], where=A)
        rw_sb = sb("rw_sb", [E0, D], where=A)
        rwT = sb("rwT", [P, E0], where=A)
        g1_bc = sb("g1_bc", [P, D], where=A)
        g2_bc = sb("g2_bc", [P, D], where=A)
        b12_bc = sb("b12_bc", [P, 2, D], where=A)
        headmask = sb("headmask", [P, D + H0], where=A)
        reset = sb("reset", [P, NT * E0], where=A)
        mhalf = sb("mhalf", [P, 2 * NT], where=A)
        epsc = sb("epsc", [P, 2 * NT], where=A)
        keyc = [sb(f"keyc{u}", [P, NT * E0], where=A) for u in range(2)]
        keys_sb = sb("keys", [P, NT, 2, E0], where=A)
        S = []
        for u in range(2):
            s = {}
            for name, cols in dict(x=NT * D, xT=L, feat=NT * D, e=NT * D, featT=L, hT=2 * L, r=NT * D,
                                   lg=NT * E0, zap=NT * E0, mask=NT * E0, ex=NT * E0, incl=NT * E0,
                                   stats=12 * NT, mv=4 * NT, rstd=2 * NT, stats3=6 * NT, mv3=2 * NT, rstd3=NT,
                                   z=NT * H0, kvm=D + H0, top=NT * 8, esum=NT, q=NT * (D + 4), xw=NT * ROW).items():
                s[name] = sb(f"{name}_{u}", [P, cols], where=A)
            s["x1T"] = s["hT"][:, 0:L]
            s["msg"], s["msgT"], s["m2T"], s["a1"], s["a2"] = s["e"], s["xT"], s["featT"], s["feat"], s["e"]
            S.append(s)
        A.close()
        late = scope()
        wgu_l = sb("wgu_late", [P, 2 * (EP - EP_EARLY), 2, F0], where=late)
        wd_l = sb("wd_late", [F0, 2 * (EP - EP_EARLY), D], where=late)
        late.close()
        AB.close()
        C.buffers(sb)

        bank = [ctx.enter_context(nc.psum_tensor(f"bank{k}", [P, 512], F32)) for k in range(8)]

        names = """consts_ready weights_ready zero_tile zeros_written xT_mm xT_sb q_mm negq eq feat_sb featT_mm kv_mm featT_sb kvm_sb
        num_mm z_step msg_sb msgT_mm msgT_sb m2T_mm m2T_sb hT_mm hT1_sb mlp_mm st1 mv1 var_eps rstd1
        xr1 xr2 centred r_step st3 mv3 rstd3 x1_sb x1T_mm x1T_sb x1T_kept lg_mm lg_sb pick_step soft_step
        d_sb ex_sb w_sb incl_sb ka_sb key_sb keyc_sb keyT_mm keyT_sb rwT_mm rwT_sb pool_setup late_weights early_weights
        round_done slots_sb slotT_mm slot_index sg_mm su_sb sh_sb ysh_mm ysh_sb base_sb
        xgT_mm xgT_sb gu_mm sil_sb hexp_sb y_mm y_sb rows_scattered""".split()
        s_ = {n: sem(n) for n in names}
        x_loaded = [sem(f"x_loaded{u}") for u in range(2)]
        xw_stored = [sem(f"xw_stored{u}") for u in range(2)]
        gathered = [sem(f"gathered{m}") for m in range(8)]

        x_view = x_in.rearrange("b (j p) d -> b p j d", p=P)
        table_view = table[0:T, :].rearrange("(b j p) r -> b p j r", j=NT, p=P)
        zero_view = contrib.rearrange("(n p f) d -> n p (f d)", p=P, f=ZCOLS // D)
        NZ = NKEY * D // (P * ZCOLS)

        def tiles(ap, w=D):
            return ap.rearrange("p (j d) -> p j d", d=w)

        base_rows = base_all[:, :, :].rearrange("p b (j d) -> p b j d", d=D)

        def carve(k, cols, parts=P):
            return rows_all[0:parts, k * 512:k * 512 + cols]
        sgs = [carve(0 + 4 * u, 512, F0) for u in range(2)]
        sus = [carve(1 + 4 * u, 512, F0) for u in range(2)]
        shs = [carve(2 + 4 * u, 512, F0) for u in range(2)]
        yss = [carve(3 + 4 * u, 512) for u in range(2)]

        def late_early(pair):
            if pair < EP_EARLY:
                return wgu_e[:, 2 * pair:2 * pair + 2], wd_e[:, 2 * pair:2 * pair + 2]
            k = 2 * (pair - EP_EARLY)
            return wgu_l[:, k:k + 2], wd_l[:, k:k + 2]

        def expert_silu(act, m):
            act.wait_ge(s_["gu_mm"], m + 1)
            if m >= 2:
                act.wait_ge(s_["hexp_sb"], m - 1)
            nc.scalar.activation(sil[m % 2][:, :], bank[2 + m % 2][0:F0, 0:P], ACT.Silu).then_inc(s_["sil_sb"], 1)

        def expert_weigh(dve, m):
            dve.wait_ge(s_["y_mm"], m + 1)
            for h in range(2):
                part = slice(h * CAP, (h + 1) * CAP)
                w = rows_all[part, m * ROW + D + 2 * m + h:m * ROW + D + 2 * m + h + 1]
                ins = nc.vector.tensor_scalar(y_all[part, m * D:(m + 1) * D], bank[4 + m % 2][part, 0:D], w, None, ALU.mult)
            ins.then_inc(s_["y_sb"], 1)

        def expert_up(pe, m):
            wgu, _ = late_early(m)
            pe.wait_ge(s_["xgT_sb"], m + 1)
            if m >= 2:
                pe.wait_ge(s_["hexp_sb"], m - 1)
            for gu in range(2):
                for h in range(2):
                    ins = nc.tensor.matmul(bank[2 + m % 2][0:F0, gu * P + h * CAP:gu * P + (h + 1) * CAP], wgu[:, h, gu, :],
                                           xgT[m % 2][:, h * CAP:(h + 1) * CAP], start=True, stop=True)
            ins.then_inc(s_["gu_mm"], 1)

        def expert_down(pe, m):
            _, wd = late_early(m)
            pe.wait_ge(s_["hexp_sb"], m + 1)
            if m >= 2:
                pe.wait_ge(s_["y_sb"], m - 1)
            for h in range(2):
                ins = nc.tensor.matmul(bank[4 + m % 2][h * CAP:(h + 1) * CAP, 0:D], hexp[m % 2][:, h * CAP:(h + 1) * CAP], wd[:, h, :],
                                       start=True, stop=True)
            ins.then_inc(s_["y_mm"], 1)

        C.bank, C.ident, C.landing, C.base_all = bank, ident, landing, base_all
        C.rows_scattered, C.y_sb, C.base_sb = s_["rows_scattered"], s_["y_sb"], s_["base_sb"]
        C.skew = nc.dram_tensor("bias_rows", (G, 2 * G - 1), F32, kind="Internal").ap()
        C.contrib_view = contrib.rearrange("(b j p k) d -> b p j (k d)", j=NT, p=P, k=K0N)
        C.out_view = out.rearrange("b (j p) d -> b p j d", p=P)
        C.inputs = dict(Wq=Wq, ln_w=ln_w, ln_b=ln_b, Wh=Wh, bh=bh, Wqk=Wqk, bqk=bqk, qk_w=qk_w, qk_b=qk_b, rel_table=rel_table,
                        Wout=Wout, bout=bout, Wg=Wg, W1e=W1e, b1e=b1e, Wo=Wo, bo=bo)

        block = ctx.enter_context(nc.Block())

        @block.gpsimd
        def _(pool):
            g = nc.gpsimd
            count = [0]

            def chain(ins):
                count[0] += 1
                ins.then_inc(s_["pool_setup"], 1)
                pool.wait_ge(s_["pool_setup"], count[0])

            chain(g.memset(ident[:, :], 0.0))
            g.affine_select(out=ident[:, :], in_=ident[:, :], compare_op=ALU.not_equal, fill=1.0, base=0,
                            pattern=[[-1, P]], channel_multiplier=1).then_inc(s_["consts_ready"], 1)
            g.memset(zeros, 0.0).then_inc(s_["zero_tile"], 1)
            chain(g.memset(headmask[:, :], 1.0))
            hm = headmask[:, 0:D].rearrange("p (h v) -> p h v", v=DH)
            hi = headmask[:, D:D + H0]
            chain(g.affine_select(out=hm, in_=hm, compare_op=ALU.is_ge, fill=0.0, base=0, pattern=[[-DH, H0], [0, DH]], channel_multiplier=1))
            chain(g.affine_select(out=hm, in_=hm, compare_op=ALU.is_ge, fill=0.0, base=DH - 1, pattern=[[DH, H0], [0, DH]], channel_multiplier=-1))
            chain(g.affine_select(out=hi, in_=hi, compare_op=ALU.is_ge, fill=0.0, base=0, pattern=[[-DH, H0]], channel_multiplier=1))
            g.affine_select(out=hi, in_=hi, compare_op=ALU.is_ge, fill=0.0, base=DH - 1, pattern=[[DH, H0]], channel_multiplier=-1).then_inc(s_["consts_ready"], 1)
            chain(g.memset(reset[:, :], 1.0))
            chain(g.memset(tiles(reset[:, :], E0)[:, :, 0:1], 0.0))
            for u in range(2):
                g.memset(tiles(S[u]["q"][:, :], D + 4)[:, :, D:D + 4], 1.0).then_inc(s_["consts_ready"], 1)
                g.iota(keyc[u][:, :], pattern=[[-K0N * P, NT], [0, E0]], base=NKEY + 1 - K0N * L * PAIRS * u, channel_multiplier=-K0N,
                       allow_small_or_imprecise_dtypes=True).then_inc(s_["consts_ready"], 1)
            g.memset(epsc[:, :], EPS)
            g.memset(mhalf[:, :], -0.5).then_inc(s_["consts_ready"], 1)
            pool.wait_ge(s_["weights_ready"], 16 * 11)
            g.tensor_tensor(b12_bc[:, 0, :], b12_bc[:, 0, :], b12_bc[:, 1, :], ALU.add).then_inc(s_["consts_ready"], 1)
            pool.wait_ge(s_["consts_ready"], 8)
            C.setup_pool_early(pool)

            def half(pool, p1=None, p2=None, p3=None, keys=None):
                if p2:
                    i, u = p2
                    s, n = S[u], 2 * i + (u + 1)
                    pool.wait_ge(s_["mv1"], n)
                    var = tiles(s["mv"][:, :], 2)[:, :, 1]
                    g.tensor_tensor(s["rstd"][:, :], var, epsc[:, :], ALU.add).then_inc(s_["var_eps"], 1)
                    pool.wait_ge(s_["var_eps"], 2 * n - 1)
                    g.tensor_tensor(s["rstd"][:, :], s["rstd"][:, :], mhalf[:, :], ALU.pow).then_inc(s_["rstd1"], 1)
                    pool.wait_ge(s_["mv3"], n)
                    var = tiles(s["mv3"][:, :], 2)[:, :, 1]
                    g.tensor_tensor(s["rstd3"][:, :], var, epsc[:, 0:NT], ALU.add).then_inc(s_["var_eps"], 1)
                    pool.wait_ge(s_["var_eps"], 2 * n)
                    g.tensor_tensor(s["rstd3"][:, :], s["rstd3"][:, :], mhalf[:, 0:NT], ALU.pow).then_inc(s_["rstd3"], 1)
                if p1:
                    i, u = p1
                    s, n = S[u], 2 * i + (u + 1)
                    pool.wait_ge(x_loaded[u], 16 * i + 16)
                    g.tensor_tensor(s["r"][:, :], s["x"][:, :], s["x"][:, :], ALU.add).then_inc(s_["xr1"], 1)
                    pool.wait_ge(s_["xr1"], n)
                    g.tensor_tensor(tiles(s["r"][:, :]), tiles(s["r"][:, :]), bcast_mid(b12_bc[:, 0, :], NT), ALU.add).then_inc(s_["xr2"], 1)
                if p2:
                    i, u = p2
                    s, n = S[u], 2 * i + (u + 1)
                    pool.wait_ge(s_["x1T_sb"], n)
                    seq = i + PAIRS * u
                    kept = x1T_all[:, seq * L:(seq + 1) * L] if isinstance(i, int) else x1T_all[:, bass.ds(i * L + u * (T // 2), L)]
                    g.tensor_copy(kept, s["x1T"]).then_inc(s_["x1T_kept"], 1)
                if p3:
                    i, u = p3
                    s, n = S[u], 2 * i + (u + 1)
                    pool.wait_ge(s_["incl_sb"], n)
                    g.tensor_tensor(s["incl"][:, :], keyc[u][:, :], s["incl"][:, :], ALU.subtract).then_inc(s_["ka_sb"], 1)
                    pool.wait_ge(s_["ka_sb"], n)
                    pool.wait_ge(s_["keyT_mm"], i + 1)
                    g.tensor_tensor(keys_sb[:, :, u, :], tiles(s["incl"][:, :], E0), tiles(s["mask"][:, :], E0), ALU.mult).then_inc(s_["key_sb"], 1)
                    g.tensor_scalar(keyc[u][:, :], keyc[u][:, :], float(-K0N * L), None, ALU.add).then_inc(s_["keyc_sb"], 1)
                    pool.wait_ge(s_["keyc_sb"], n)

            stage_a(pool, half)
            def shared_product(n, u):
                pool.wait_ge(s_["su_sb"], n)
                g.tensor_tensor(shs[u], sgs[u], sus[u], ALU.mult).then_inc(s_["sh_sb"], 1)

            def base_sum(b, n, u):
                pool.wait_ge(s_["ysh_sb"], n)
                dst = base_all[:, b, :] if isinstance(b, int) else base_all[:, bass.ds(b, 1), :].rearrange("p o d -> p (o d)")
                g.tensor_tensor(dst, dst, yss[u], ALU.add).then_inc(s_["base_sb"], 1)

            C.setup_pool_scale(pool)
            for u in range(2):
                pool.wait_ge(xw_stored[u], 32 * PAIRS + 16)
            shared_product(1, 0)
            with pool.Fori(0, PAIRS - 1) as i:
                shared_product(2 * i + 2, 1)
                base_sum(2 * i, 2 * i + 1, 0)
                shared_product(2 * i + 3, 0)
                base_sum(2 * i + 1, 2 * i + 2, 1)
            shared_product(B, 1)
            base_sum(B - 2, B - 1, 0)
            base_sum(B - 1, B, 1)

            C.setup_pool_late(pool)
            pool.wait_ge(s_["slot_index"], 2)
            pool.wait_ge(s_["x1T_kept"], B)
            pool.wait_ge(s_["base_sb"], B)
            pool.wait_ge(s_["zeros_written"], 16 * (NZ + 1))
            for m in range(EP):
                if m >= 8:
                    pool.wait_ge(gathered[m % 8], 16 * (m // 8))
                g.indirect_dma_start(rows_all[:, m * ROW:(m + 1) * ROW], None, table,
                                     bass.IndirectOffsetOnAxis(ap=tok_row[:, m:m + 1], axis=0)).then_inc(gathered[m % 8], 16)
            for m in range(EP):
                pool.wait_ge(s_["y_sb"], m + 1)
                g.indirect_dma_start(contrib, bass.IndirectOffsetOnAxis(ap=dest_row[:, m:m + 1], axis=0),
                                     y_all[:, m * D:(m + 1) * D], None, bounds_check=NKEY - 1, oob_is_err=False).then_inc(s_["rows_scattered"], 16)
            C.pool(pool)

        @block.sync
        def _(sp):
            for u in range(2):
                sp.dma_start(tiles(S[u]["x"][:, :]), x_view[PAIRS * u]).then_inc(x_loaded[u], 16)
            smalls = [(rw_sb[:, :], router_w), (Wq_sb[:, :], Wq), (Wm_sb[:, :], Wm), (W1_sb[:, :], W1),
                      (W2_sb[:, :, :], W2.rearrange("(h p) d -> p h d", p=P)),
                      (g1_bc[:, :], g1.partition_broadcast(P)), (g2_bc[:, :], g2.partition_broadcast(P)),
                      (b12_bc[:, 0, :], b1.partition_broadcast(P)), (b12_bc[:, 1, :], b2.partition_broadcast(P)),
                      (wsgu_sb[:, :], ws_gate_up), (wsd_sb[:, :], ws_down)]
            for dst, src in smalls:
                sp.dma_start(dst, src).then_inc(s_["weights_ready"], 16)
            C.setup_sync(sp)
            sp.wait_ge(s_["zero_tile"], 1)
            sp.dma_start(table[T:T + 1, :], zeros[0:1, 0:ROW]).then_inc(s_["zeros_written"], 16)
            def load_next(i, u):
                sp.wait_ge(s_["xT_mm"], 2 * i + u + 1)
                sp.wait_ge(s_["xr1"], 2 * i + u + 1)
                b = i + (PAIRS * u + 1)
                at = slice(b, b + 1) if isinstance(i, int) else bass.ds(b, 1)
                sp.dma_start(tiles(S[u]["x"][:, :]), x_view[at].rearrange("o p j d -> (o p) j d")).then_inc(x_loaded[u], 16)

            def store(i, u, at):
                xw = tiles(S[u]["xw"][:, :], ROW)
                sp.wait_ge(s_["x1_sb"], 2 * i + u + 1)
                sp.wait_ge(s_["w_sb"], 2 * i + u + 1)
                sp.dma_start(table_view[at].rearrange("o p j d -> (o p) j d"), xw).then_inc(xw_stored[u], 16)
                sp.dma_start(base_rows[:, at].rearrange("p o j d -> p (o j) d"), xw[:, :, 0:D]).then_inc(xw_stored[u], 16)

            def zero(k):
                sp.dma_start(zero_view[k].rearrange("o p f -> (o p) f"), zeros).then_inc(s_["zeros_written"], 16)

            n = 2 * EP_EARLY
            sp.dma_start(wgu_e[:, :, 0, :], w_gate[0:n].rearrange("e p f -> p e f")).then_inc(s_["early_weights"], 16)
            sp.dma_start(wgu_e[:, :, 1, :], w_up[0:n].rearrange("e p f -> p e f")).then_inc(s_["early_weights"], 16)
            sp.dma_start(wd_e[:, :, :], w_down[0:n].rearrange("e p f -> p e f")).then_inc(s_["early_weights"], 16)
            zero(slice(0, 1))
            load_next(0, 0)
            zero(slice(1, 2))
            load_next(0, 1)
            C.setup_sync_skew(sp)
            for k in range(2, NZ - 2 * (PAIRS - 2)):
                zero(slice(k, k + 1))
            with sp.Fori(0, PAIRS - 2) as i:
                load_next(i + 1, 0)
                zero(bass.ds(2 * i + (NZ - 2 * (PAIRS - 2)), 1))
                store(i, 0, bass.ds(i, 1))
                load_next(i + 1, 1)
                zero(bass.ds(2 * i + (NZ - 2 * (PAIRS - 2) + 1), 1))
                store(i, 1, bass.ds(i + PAIRS, 1))
            for i in (PAIRS - 2, PAIRS - 1):
                store(i, 0, slice(i, i + 1))
                store(i, 1, slice(i + PAIRS, i + PAIRS + 1))
            for u in range(2):
                sp.wait_ge(xw_stored[u], 32 * PAIRS + 16)
            sp.wait_ge(s_["keyc_sb"], B)
            sp.wait_ge(s_["keyT_mm"], PAIRS + 1)
            KL = EP - EP_EARLY
            for k in range(0, 2 * KL, KL // 2):
                e0 = 2 * EP_EARLY + k
                n = KL // 2
                sp.dma_start(wgu_l[:, k:k + n, 0, :], w_gate[e0:e0 + n].rearrange("e p f -> p e f")).then_inc(s_["late_weights"], 16)
                sp.dma_start(wgu_l[:, k:k + n, 1, :], w_up[e0:e0 + n].rearrange("e p f -> p e f")).then_inc(s_["late_weights"], 16)
                sp.dma_start(wd_l[:, k:k + n, :], w_down[e0:e0 + n].rearrange("e p f -> p e f")).then_inc(s_["late_weights"], 16)

            C.sync(sp)

        @block.scalar
        def _(act):
            a = nc.scalar
            act.wait_ge(s_["rwT_mm"], 1)
            a.copy(rwT[:, :], bank[2][:, 0:E0]).then_inc(s_["rwT_sb"], 1)
            act.wait_ge(s_["consts_ready"], 8)

            def half(act, p1=None, p2=None, p3=None, keys=None):
                if p1:
                    i, u = p1
                    s, n = S[u], 2 * i + (u + 1)
                    act.wait_ge(s_["xT_mm"], n)
                    a.copy(s["xT"][:, :], bank[4 * u][:, :]).then_inc(s_["xT_sb"], 1)
                    act.wait_ge(s_["q_mm"], n)
                    a.activation(s["e"][:, :], bank[4 * u + 1][:, :], ACT.Relu, scale=-1.0).then_inc(s_["negq"], 1)
                    a.copy(tiles(s["q"][:, :], D + 4)[:, :, 0:D], tiles(bank[4 * u + 1][:, :]))
                    act.wait_ge(s_["negq"], n)
                    a.activation(s["e"][:, :], s["e"][:, :], ACT.Exp, scale=-1.0).then_inc(s_["eq"], 1)
                if keys is not None:
                    act.wait_ge(s_["keyT_mm"], keys + 2)
                    dst = keyT[:, keys * L:(keys + 1) * L] if isinstance(keys, int) else keyT[:, bass.ds(keys * L, L)]
                    a.copy(dst, bank[3][:, :]).then_inc(s_["keyT_sb"], 1)
                if p1:
                    act.wait_ge(s_["featT_mm"], n)
                    a.copy(s["featT"][:, :], bank[4 * u][:, :]).then_inc(s_["featT_sb"], 1)
                    act.wait_ge(s_["msgT_mm"], n)
                    a.copy(s["msgT"][:, :], bank[4 * u][:, :]).then_inc(s_["msgT_sb"], 1)
                if p2:
                    v, m = p2[1], 2 * p2[0] + (p2[1] + 1)
                    act.wait_ge(s_["x1T_mm"], m)
                    a.copy(S[v]["x1T"], bank[4 * v][:, :]).then_inc(s_["x1T_sb"], 1)
                if p1:
                    act.wait_ge(s_["m2T_mm"], n)
                    a.copy(s["m2T"][:, :], bank[4 * u + 2][:, :]).then_inc(s_["m2T_sb"], 1)
                if p1:
                    act.wait_ge(s_["hT_mm"], n)
                    if not first(i):
                        act.wait_ge(s_["x1T_kept"], n - 2)
                    a.activation(s["hT"][:, 0:L], bank[4 * u][:, :], ACT.Relu)
                    a.activation(s["hT"][:, L:2 * L], bank[4 * u + 3][:, :], ACT.Relu).then_inc(s_["hT1_sb"], 1)
                if p3:
                    w, k = p3[1], 2 * p3[0] + (p3[1] + 1)
                    act.wait_ge(s_["d_sb"], k)
                    a.activation(S[w]["ex"][:, :], S[w]["ex"][:, :], ACT.Exp).then_inc(s_["ex_sb"], 1)
                if p2:
                    act.wait_ge(s_["lg_mm"], m)
                    a.copy(S[v]["lg"][:, :], bank[4 * v + 1][:, 0:NT * E0]).then_inc(s_["lg_sb"], 1)

            stage_a(act, half)
            C.setup_act(act)

            act.wait_ge(s_["zeros_written"], 16 * (NZ + 1))
            def shared_up(n, u):
                act.wait_ge(s_["sg_mm"], n)
                a.activation(sgs[u], bank[4 * u][0:F0, :], ACT.Silu)
                a.copy(sus[u], bank[4 * u + 1][0:F0, :]).then_inc(s_["su_sb"], 1)

            def shared_down(n, u):
                act.wait_ge(s_["ysh_mm"], n)
                a.copy(yss[u], bank[4 * u + 2][:, :]).then_inc(s_["ysh_sb"], 1)

            shared_up(1, 0)
            with act.Fori(0, PAIRS - 1) as i:
                shared_up(2 * i + 2, 1)
                shared_down(2 * i + 1, 0)
                shared_up(2 * i + 3, 0)
                shared_down(2 * i + 2, 1)
            shared_up(B, 1)
            shared_down(B - 1, 0)
            shared_down(B, 1)

            for m in range(EP):
                act.wait_ge(s_["xgT_mm"], m + 1)
                a.copy(xgT[m % 2][:, :], bank[m % 2][:, 0:P]).then_inc(s_["xgT_sb"], 1)
                if m >= 1:
                    expert_silu(act, m - 1)
            expert_silu(act, EP - 1)
            C.act(act)

        @block.vector
        def _(dve):
            v = nc.vector
            v.memset(landing(), 0.0).then_inc(s_["keyT_mm"], 1)
            v.memset(landing(), 0.0).then_inc(s_["keyT_sb"], 1)
            for u in range(2):
                v.memset(landing(), 0.0).then_inc(xw_stored[u], 16)
            dve.wait_ge(s_["consts_ready"], 8)

            def half(dve, p1=None, p2=None, p3=None, keys=None):
                if p2:
                    i, u = p2
                    s, n = S[u], 2 * i + (u + 1)
                    dve.wait_ge(s_["mlp_mm"], n)
                    st = tiles(s["stats"][:, :], 6)
                    mv = tiles(s["mv"][:, :], 2)
                    for k in range(2):
                        for j in range(NT):
                            ins = v.bn_stats(st[:, NT * k + j, :], bank[4 * u + 1 + k][:, j * D:(j + 1) * D])
                    ins.then_inc(s_["st1"], 1)
                    dve.wait_ge(s_["st1"], n)
                    v.memset(landing(), 0.0)
                    for k in range(2 * NT):
                        ins = v.bn_aggr(mv[:, k, :], st[:, k, :])
                    ins.then_inc(s_["mv1"], 1)
                    mv = tiles(s["mv"][:, :], 2)
                    dve.wait_ge(s_["mv1"], n)
                    for j in range(NT):
                        ins = v.scalar_tensor_tensor(out=s["a1"][:, j * D:(j + 1) * D], in0=bank[4 * u + 1][:, j * D:(j + 1) * D],
                                                     scalar=mv[:, j, 0:1], in1=g1_bc[:, :], op0=ALU.subtract, op1=ALU.mult)
                if p1:
                    i, u = p1
                    s, n = S[u], 2 * i + (u + 1)
                    dve.wait_ge(s_["eq"], n)
                    v.scalar_tensor_tensor(out=s["feat"][:, :], in0=bank[4 * u + 1][:, :], scalar=0.0, in1=s["e"][:, :],
                                           op0=ALU.max, op1=ALU.add).then_inc(s_["feat_sb"], 1)
                if p2:
                    i, u = p2
                    s, n = S[u], 2 * i + (u + 1)
                    mv = tiles(s["mv"][:, :], 2)
                    for j in range(NT):
                        ins = v.scalar_tensor_tensor(out=s["a2"][:, j * D:(j + 1) * D], in0=bank[4 * u + 2][:, j * D:(j + 1) * D],
                                                     scalar=mv[:, NT + j, 0:1], in1=g2_bc[:, :], op0=ALU.subtract, op1=ALU.mult)
                    ins.then_inc(s_["centred"], 1)
                    dve.wait_ge(s_["centred"], n)
                    dve.wait_ge(s_["rstd1"], n)
                    dve.wait_ge(s_["xr2"], n)
                    for j in range(NT):
                        c = slice(j * D, (j + 1) * D)
                        ins = v.scalar_tensor_tensor(out=s["r"][:, c], in0=s["a1"][:, c], scalar=s["rstd"][:, j:j + 1],
                                                     in1=s["r"][:, c], op0=ALU.mult, op1=ALU.add)
                    ins.then_inc(s_["r_step"], 1)
                if p1:
                    i, u = p1
                    s, n = S[u], 2 * i + (u + 1)
                    dve.wait_ge(s_["kv_mm"], n)
                    v.tensor_tensor(s["kvm"][:, 0:D], bank[4 * u + 2][:, 0:D], headmask[:, 0:D], ALU.mult)
                    v.tensor_scalar(s["kvm"][:, D:D + H0], headmask[:, D:D + H0], bank[4 * u + 2][:, D:D + 1], None, ALU.mult).then_inc(s_["kvm_sb"], 1)
                if p2:
                    i, u = p2
                    s, n = S[u], 2 * i + (u + 1)
                    dve.wait_ge(s_["r_step"], 2 * n - 1)
                    for j in range(NT):
                        c = slice(j * D, (j + 1) * D)
                        ins = v.scalar_tensor_tensor(out=s["r"][:, c], in0=s["a2"][:, c], scalar=s["rstd"][:, NT + j:NT + j + 1],
                                                     in1=s["r"][:, c], op0=ALU.mult, op1=ALU.add)
                    ins.then_inc(s_["r_step"], 1)
                    dve.wait_ge(s_["r_step"], 2 * n)
                    v.memset(landing(), 0.0)
                    st, mv = tiles(s["stats3"][:, :], 6), tiles(s["mv3"][:, :], 2)
                    for j in range(NT):
                        ins = v.bn_stats(st[:, j, :], s["r"][:, j * D:(j + 1) * D])
                    ins.then_inc(s_["st3"], 1)
                    dve.wait_ge(s_["st3"], n)
                    v.memset(landing(), 0.0)
                    for j in range(NT):
                        ins = v.bn_aggr(mv[:, j, :], st[:, j, :])
                    ins.then_inc(s_["mv3"], 1)
                if p1:
                    i, u = p1
                    s, n = S[u], 2 * i + (u + 1)
                    dve.wait_ge(s_["num_mm"], n)
                    v.tensor_scalar(s["z"][:, :], bank[4 * u + 2][:, 256:256 + NT * H0], ATTN_EPS, None, ALU.add).then_inc(s_["z_step"], 1)
                    dve.wait_ge(s_["z_step"], 2 * n - 1)
                    v.reciprocal(s["z"][:, :], s["z"][:, :]).then_inc(s_["z_step"], 1)
                    dve.wait_ge(s_["z_step"], 2 * n)
                    v.tensor_tensor(s["msg"][:, :].rearrange("p (a c) -> p a c", c=DH), bank[4 * u + 1][:, :].rearrange("p (a c) -> p a c", c=DH),
                                    bcast_last(s["z"][:, :], DH), ALU.mult).then_inc(s_["msg_sb"], 1)
                if p2:
                    i, u = p2
                    s, n = S[u], 2 * i + (u + 1)
                    mv, xw = tiles(s["mv3"][:, :], 2), tiles(s["xw"][:, :], ROW)
                    dve.wait_ge(s_["rstd3"], n)
                    dve.wait_ge(xw_stored[u], 32 * i + 16)
                    for j in range(NT):
                        ins = v.tensor_scalar(xw[:, j, 0:D], s["r"][:, j * D:(j + 1) * D], mv[:, j, 0:1], s["rstd3"][:, j:j + 1], ALU.subtract, ALU.mult)
                    ins.then_inc(s_["x1_sb"], 1)
                if p3:
                    i, u = p3
                    s, n = S[u], 2 * i + (u + 1)
                    dve.wait_ge(s_["lg_sb"], n)
                    v.memset(landing(), 0.0)
                    lg, top = tiles(s["lg"][:, :], E0), tiles(s["top"][:, :], 8)
                    for j in range(NT):
                        ins = v.max(top[:, j, :], lg[:, j, :])
                    ins.then_inc(s_["pick_step"], 1)
                    dve.wait_ge(s_["pick_step"], 3 * n - 2)
                    v.tensor_tensor(tiles(s["ex"][:, :], E0), lg, bcast_last(top[:, :, 0], E0), ALU.subtract).then_inc(s_["d_sb"], 1)
                    for j in range(NT):
                        ins = v.match_replace(tiles(s["zap"][:, :], E0)[:, j, :], top[:, j, :], lg[:, j, :], NEG)
                    ins.then_inc(s_["pick_step"], 1)
                    dve.wait_ge(s_["pick_step"], 3 * n - 1)
                    v.tensor_tensor(s["mask"][:, :], s["zap"][:, :], s["lg"][:, :], ALU.not_equal).then_inc(s_["pick_step"], 1)
                    dve.wait_ge(s_["pick_step"], 3 * n)
                    v.tensor_tensor_scan(s["incl"][:, :], reset[:, :], s["mask"][:, :], 0.0, ALU.mult, ALU.add).then_inc(s_["incl_sb"], 1)
                    xw = tiles(s["xw"][:, :], ROW)
                    dve.wait_ge(s_["ex_sb"], n)
                    v.tensor_tensor(s["ex"][:, :], s["ex"][:, :], s["mask"][:, :], ALU.mult).then_inc(s_["soft_step"], 1)
                    dve.wait_ge(s_["soft_step"], 3 * n - 2)
                    v.tensor_reduce(s["esum"][:, :], tiles(s["ex"][:, :], E0), AX.X, ALU.add).then_inc(s_["soft_step"], 1)
                    dve.wait_ge(s_["soft_step"], 3 * n - 1)
                    v.reciprocal(s["esum"][:, :], s["esum"][:, :]).then_inc(s_["soft_step"], 1)
                    dve.wait_ge(s_["soft_step"], 3 * n)
                    v.tensor_tensor(xw[:, :, D:ROW], tiles(s["ex"][:, :], E0), bcast_last(s["esum"][:, :], E0), ALU.mult).then_inc(s_["w_sb"], 1)

            stage_a(dve, half)

            rounds = [0]

            def step(ins):
                rounds[0] += 1
                ins.then_inc(s_["round_done"], 1)
                dve.wait_ge(s_["round_done"], rounds[0])

            dve.wait_ge(s_["keyT_sb"], PAIRS + 1)
            for r in range(CAP // 8):
                step(v.max(cand[:, 8 * r:8 * r + 8], keyT[:, :]))
                if r < CAP // 8 - 1:
                    step(v.match_replace(keyT[:, :], cand[:, 8 * r:8 * r + 8], keyT[:, :], 0.0))
            v.tensor_copy(both[:, 0:CAP], cand[0:E0, :])
            step(v.tensor_copy(both[:, CAP:2 * CAP], cand[E0:2 * E0, :]))
            for r in range(CAP // 8):
                step(v.max(slot_key[:, 8 * r:8 * r + 8], both[:, :]))
                if r < CAP // 8 - 1:
                    step(v.match_replace(both[:, :], slot_key[:, 8 * r:8 * r + 8], both[:, :], 0.0))
            v.tensor_scalar(slot_key[:, :], slot_key[:, :], -1.0, float(NKEY), ALU.mult, ALU.add).then_inc(s_["slots_sb"], 1)
            dve.wait_ge(s_["slotT_mm"], 1)
            pairs = bank[6][0:CAP, 0:E0].rearrange("c (m two) -> c m two", two=2)
            v.tensor_copy(dest_row[0:CAP, :], pairs[:, :, 0])
            v.tensor_copy(dest_row[CAP:2 * CAP, :], pairs[:, :, 1]).then_inc(s_["slot_index"], 1)
            dve.wait_ge(s_["slot_index"], 1)
            v.tensor_scalar(tok_row[:, :], dest_row[:, :], 3, None, ALU.logical_shift_right).then_inc(s_["slot_index"], 1)

            for m in range(EP):
                dve.wait_ge(s_["sil_sb"], m + 1)
                if m >= 2:
                    dve.wait_ge(s_["y_mm"], m - 1)
                v.tensor_tensor(hexp[m % 2][:, :], sil[m % 2][:, :], bank[2 + m % 2][0:F0, P:2 * P], ALU.mult).then_inc(s_["hexp_sb"], 1)
                if m >= 1:
                    expert_weigh(dve, m - 1)
            expert_weigh(dve, EP - 1)
            C.dve(dve)

        @block.tensor
        def _(pe):
            t = nc.tensor

            def transposes(dst, src, w=D):
                for j in range(NT):
                    ins = t.transpose(dst[:, j * P:(j + 1) * P], src[:, j * w:j * w + P], ident[:, :])
                return ins

            pe.wait_ge(s_["consts_ready"], 8)
            pe.wait_ge(s_["weights_ready"], 16 * 11)
            t.transpose(bank[2][:, 0:E0], rw_sb[:, :], ident[0:E0, 0:E0]).then_inc(s_["rwT_mm"], 1)
            pe.wait_ge(s_["rwT_sb"], 1)

            def half(pe, p1=None, p2=None, p3=None, keys=None):
                if p1:
                    i, u = p1
                    s, n = S[u], 2 * i + (u + 1)
                    pe.wait_ge(x_loaded[u], 16 * i + 16)
                    transposes(bank[4 * u], s["x"]).then_inc(s_["xT_mm"], 1)
                    pe.wait_ge(s_["xT_sb"], n)
                    for j in range(NT):
                        ins = t.matmul(bank[4 * u + 1][:, j * D:(j + 1) * D], s["xT"][:, j * P:(j + 1) * P], Wq_sb[:, :], start=True, stop=True)
                    ins.then_inc(s_["q_mm"], 1)
                if keys is not None:
                    pe.wait_ge(s_["key_sb"], 2 * keys + 2)
                    for j in range(NT):
                        ins = t.transpose(bank[3][:, j * P:(j + 1) * P], keys_sb[:, j, :, :].rearrange("p u e -> p (u e)"), ident[:, :])
                    ins.then_inc(s_["keyT_mm"], 1)
                if p1:
                    pe.wait_ge(s_["feat_sb"], n)
                    transposes(bank[4 * u], s["feat"]).then_inc(s_["featT_mm"], 1)
                    for j in range(NT):
                        ins = t.matmul(bank[4 * u + 2][:, 0:D + 1], s["feat"][:, j * D:(j + 1) * D], s["q"][:, j * (D + 4):j * (D + 4) + D + 1],
                                       start=(j == 0), stop=(j == NT - 1))
                    ins.then_inc(s_["kv_mm"], 1)
                    pe.wait_ge(s_["featT_sb"], n)
                    pe.wait_ge(s_["kvm_sb"], n)
                    for j in range(NT):
                        ft = s["featT"][:, j * P:(j + 1) * P]
                        t.matmul(bank[4 * u + 1][:, j * D:(j + 1) * D], ft, s["kvm"][:, 0:D], start=True, stop=True)
                        ins = t.matmul(bank[4 * u + 2][:, 256 + j * H0:256 + (j + 1) * H0], ft, s["kvm"][:, D:D + H0], start=True, stop=True)
                    ins.then_inc(s_["num_mm"], 1)
                    pe.wait_ge(s_["msg_sb"], n)
                    transposes(bank[4 * u], s["msg"]).then_inc(s_["msgT_mm"], 1)
                if p2:
                    v, m = p2[1], 2 * p2[0] + (p2[1] + 1)
                    pe.wait_ge(s_["x1_sb"], m)
                    transposes(bank[4 * v], S[v]["xw"], ROW).then_inc(s_["x1T_mm"], 1)
                if p1:
                    pe.wait_ge(s_["msgT_sb"], n)
                    t.matmul(bank[4 * u + 2][:, :], Wm_sb[:, :], s["msgT"][:, :], start=True, stop=True).then_inc(s_["m2T_mm"], 1)
                    for j in range(NT):
                        t.matmul(bank[4 * u + 1][:, j * D:(j + 1) * D], s["msgT"][:, j * P:(j + 1) * P], Wm_sb[:, :], start=True, stop=True)
                    pe.wait_ge(s_["m2T_sb"], n)
                    if u == 0 and not first(i):
                        pe.wait_ge(s_["keyT_sb"], i)
                    t.matmul(bank[4 * u][:, :], W1_sb[:, 0:D], s["m2T"][:, :], start=True, stop=True)
                    t.matmul(bank[4 * u + 3][:, :], W1_sb[:, D:2 * D], s["m2T"][:, :], start=True, stop=True).then_inc(s_["hT_mm"], 1)
                if p2:
                    pe.wait_ge(s_["x1T_sb"], m)
                    for j in range(NT):
                        ins = t.matmul(bank[4 * v + 1][:, j * E0:(j + 1) * E0], S[v]["x1T"][:, j * P:(j + 1) * P], rwT[:, :], start=True, stop=True)
                    ins.then_inc(s_["lg_mm"], 1)
                if p1:
                    pe.wait_ge(s_["hT1_sb"], n)
                    for j in range(NT):
                        for h in range(2):
                            ins = t.matmul(bank[4 * u + 2][:, j * D:(j + 1) * D], s["hT"][:, h * L + j * P:h * L + (j + 1) * P], W2_sb[:, h, :],
                                           start=(h == 0), stop=(h == 1))
                    ins.then_inc(s_["mlp_mm"], 1)

            stage_a(pe, half)
            pe.wait_ge(s_["keyT_sb"], PAIRS + 1)
            C.setup_pe(pe)
            def shared_up(b, u):
                xs = x1T_all[:, b * L:(b + 1) * L] if isinstance(b, int) else x1T_all[:, bass.ds(b * L, L)]
                t.matmul(bank[4 * u][0:F0, :], wsgu_sb[:, 0:F0], xs, start=True, stop=True)
                t.matmul(bank[4 * u + 1][0:F0, :], wsgu_sb[:, F0:2 * F0], xs, start=True, stop=True).then_inc(s_["sg_mm"], 1)

            def shared_down(n, u):
                pe.wait_ge(s_["sh_sb"], n)
                for j in range(NT):
                    ins = t.matmul(bank[4 * u + 2][:, j * D:(j + 1) * D], shs[u][:, j * P:(j + 1) * P], wsd_sb[:, :], start=True, stop=True)
                ins.then_inc(s_["ysh_mm"], 1)

            pe.wait_ge(s_["x1T_kept"], B)
            shared_up(0, 0)
            with pe.Fori(0, PAIRS - 1) as i:
                shared_up(2 * i + 1, 1)
                shared_down(2 * i + 1, 0)
                shared_up(2 * i + 2, 0)
                shared_down(2 * i + 2, 1)
            shared_up(B - 1, 1)
            shared_down(B - 1, 0)
            shared_down(B, 1)
            pe.wait_ge(s_["slots_sb"], 1)
            pe.wait_ge(s_["ysh_sb"], B)
            t.transpose(bank[6][0:CAP, 0:E0], slot_key[:, :], ident[0:E0, 0:E0]).then_inc(s_["slotT_mm"], 1)
            pe.wait_ge(s_["early_weights"], 16 * 3)
            for m in range(EP + 2):
                if m == EP_EARLY:
                    pe.wait_ge(s_["late_weights"], 16 * 12)
                if m < EP:
                    pe.wait_ge(gathered[m % 8], 16 * (m // 8 + 1))
                    t.transpose(bank[m % 2][:, 0:P], rows_all[:, m * ROW:m * ROW + D], ident[:, :]).then_inc(s_["xgT_mm"], 1)
                if 1 <= m <= EP:
                    expert_up(pe, m - 1)
                if m >= 2:
                    expert_down(pe, m - 2)
            C.pe(pe)


_INS = ["L0_attn_x", "L0_attn_Wq", "L0_attn_Wm", "L0_attn_W1", "L0_attn_W2", "L0_attn_g1", "L0_attn_b1", "L0_attn_g2",
        "L0_attn_b2", "L0_ffn_router_w", "L0_ffn_w_gate", "L0_ffn_w_up", "L0_ffn_w_down", "L0_ffn_ws_gate_up",
        "L0_ffn_ws_down", "L1_attn_ln_w", "L1_attn_ln_b", "L1_attn_Wh", "L1_attn_bh", "L1_attn_Wqk", "L1_attn_bqk",
        "L1_attn_qk_w", "L1_attn_qk_b", "L1_attn_rel_table", "L1_attn_Wout", "L1_attn_bout", "L1_ffn_Wg", "L1_ffn_W1",
        "L1_ffn_b1", "L1_ffn_Wo", "L1_ffn_bo"]


def kernel(**inputs):
    import concourse.bacc as bacc
    from concourse.bass_utils import run_bass_kernel_spmd as run

    nc = bacc.Bacc("TRN2", target_bir_lowering=False, num_devices=1)
    arrays, args = {}, []
    for name in _INS:
        a = np.ascontiguousarray(inputs[name])
        arrays[f"in_{name}"] = a
        args.append(nc.dram_tensor(f"in_{name}", a.shape, mybir.dt.from_np(a.dtype), kind="ExternalInput").ap())
    out = nc.dram_tensor("out_0", (B, L, D), F32, kind="ExternalOutput").ap()
    build(nc, *args, out)
    r = run(nc, [arrays], core_ids=[0])
    return r.results[0]["out_0"]
```
